# Optimizing a Trainium2 kernel written in Bass

```python
import numpy as np
import jax
import jax.numpy as jnp

def _softmax(x, axis=-1):
    return jax.nn.softmax(x, axis=axis)

def _gelu(x):
    return jax.nn.gelu(x, approximate=True)

def _silu(x):
    return jax.nn.silu(x)

def _sigmoid(x):
    return jax.nn.sigmoid(x)

def _layernorm(x, axis=-1, eps=1e-05):
    m = jnp.mean(x, axis=axis, keepdims=True)
    v = jnp.var(x, axis=axis, keepdims=True)
    return (x - m) / jnp.sqrt(v + eps)

def _scatter_add(tgt, idx, src, axis=0):
    return tgt.at[idx].add(src)

def _segment_sum(src, seg, n):
    return jax.ops.segment_sum(src, seg, n)
kernel_name = 'mk_flamingo_gated_d1_seqx_r4_672419'

def setup_inputs(seed: int=0):
    np.random.seed(seed)
    _w = jnp.asarray

    def _rec_inputs():
        import jax
        import jax.numpy as jnp
        _rk = jax.random.key(seed)
        x = -0.0002928 + 1 * jax.random.normal(jax.random.fold_in(_rk, 1), (32, 100, 256), jnp.float32)
        _lenS = 100 - jax.random.randint(jax.random.fold_in(_rk, 7), (32,), 0, max(1, 100 // 4) + 1, jnp.int32)
        _lenS2 = 361 - jax.random.randint(jax.random.fold_in(_rk, 8), (32,), 0, max(1, 361 // 4) + 1, jnp.int32)
        _ctx_1024P = jax.random.normal(jax.random.fold_in(_rk, 11), (32, 16, 256), jnp.float32)
        _ctx_1024c = jax.random.dirichlet(jax.random.fold_in(_rk, 511), 0.3 * jnp.ones((16,), jnp.float32), (32, 361))
        _ctx_1024t = jnp.einsum('bsk,bkd->bsd', _ctx_1024c, _ctx_1024P)
        _ctx_1024t = _ctx_1024t * jax.lax.rsqrt(jnp.mean(jnp.square(_ctx_1024t)) + 1e-12) * 0.953939
        ctx_1024 = -1.39393e-06 + 0.999914 * (_ctx_1024t + 0.3 * jax.random.normal(jax.random.fold_in(_rk, 611), (32, 361, 256), jnp.float32))
        _g = jax.random.normal(jax.random.fold_in(_rk, 9001), (2, 1), jnp.float32)
        _g = jnp.sign(_g) * jnp.maximum(jnp.abs(_g), 1.0) + (_g == 0) * 1.0
        g_xattn = _g[0]
        g_ffn = _g[1]
        return (x, ctx_1024, g_xattn, g_ffn)
    x, ctx_1024, g_xattn, g_ffn = _rec_inputs()

    def _L0_xattn_setup():
        import jax, jax.numpy as jnp
        import numpy as np
        import math
        DIM_Q = 256
        DIM_V = 256
        DIM_O = 256
        H = 16
        DH_Q = DIM_Q // H
        DH_V = DIM_O // H
        TEMP = math.sqrt(DIM_O)
        EPS = 1e-05

        def layernorm(x, g, b):
            mu = jnp.mean(x, axis=-1, keepdims=True)
            var = jnp.mean(jnp.square(x - mu), axis=-1, keepdims=True)
            return (x - mu) * jax.lax.rsqrt(var + EPS) * g + b
        key = jax.random.key(seed)
        ks = jax.random.split(key, 8)
        B, LQ, LK = (2, 512, 512)
        s = 0.02
        return {'Q': jax.random.normal(ks[0], (B, LQ, DIM_Q), jnp.float32), 'K': jax.random.normal(ks[1], (B, LK, DIM_Q), jnp.float32), 'V': jax.random.normal(ks[2], (B, LK, DIM_V), jnp.float32), 'Wq': jax.random.normal(ks[3], (DIM_Q, DIM_Q), jnp.float32) * s, 'Wk': jax.random.normal(ks[4], (DIM_Q, DIM_Q), jnp.float32) * s, 'Wv': jax.random.normal(ks[5], (DIM_O, DIM_V), jnp.float32) * s, 'Wo': jax.random.normal(ks[6], (DIM_O, DIM_O), jnp.float32) * s, 'g_pre': jnp.ones((DIM_Q,), jnp.float32), 'b_pre': jnp.zeros((DIM_Q,), jnp.float32), 'g_ln': jnp.ones((DIM_O,), jnp.float32), 'b_ln': jnp.zeros((DIM_O,), jnp.float32)}
    _L0_xattn_all = _L0_xattn_setup()
    _L0_xattn_in = {k: v for k, v in _L0_xattn_all.items() if k in ('Wq', 'Wk', 'Wv', 'Wo', 'g_pre', 'b_pre', 'g_ln', 'b_ln')}
    del _L0_xattn_all

    def _L0_ffn_setup():
        import jax, jax.numpy as jnp
        import numpy as np
        B, S, D = (1, 512, 256)
        F = 352
        E = 16
        K = 2
        CAP_FACTOR = 1.25

        def _mlp(h, wg, wu, wd):
            return jax.nn.silu(h @ wg) * (h @ wu) @ wd
        key = jax.random.key(seed)
        ks = jax.random.split(key, 10)
        sd = 0.02
        return {'x': jax.random.normal(ks[0], (B, S, D), jnp.float32), 'router_w': jax.random.normal(ks[1], (D, E), jnp.float32) * sd, 'router_b': jnp.zeros((E,), jnp.float32), 'w_gate': jax.random.normal(ks[2], (E, D, F), jnp.float32) * sd, 'w_up': jax.random.normal(ks[3], (E, D, F), jnp.float32) * sd, 'w_down': jax.random.normal(ks[4], (E, F, D), jnp.float32) * sd, 'sw_gate': jax.random.normal(ks[5], (D, F), jnp.float32) * sd, 'sw_up': jax.random.normal(ks[6], (D, F), jnp.float32) * sd, 'sw_down': jax.random.normal(ks[7], (F, D), jnp.float32) * sd}
    _L0_ffn_all = _L0_ffn_setup()
    _L0_ffn_in = {k: v for k, v in _L0_ffn_all.items() if k in ('router_w', 'router_b', 'w_gate', 'w_up', 'w_down', 'sw_gate', 'sw_up', 'sw_down')}
    del _L0_ffn_all
    return {'x': x, 'ctx_1024': ctx_1024, 'g_xattn': g_xattn, 'g_ffn': g_ffn, 'L0_xattn_Wq': _L0_xattn_in['Wq'], 'L0_xattn_Wk': _L0_xattn_in['Wk'], 'L0_xattn_Wv': _L0_xattn_in['Wv'], 'L0_xattn_Wo': _L0_xattn_in['Wo'], 'L0_xattn_g_pre': _L0_xattn_in['g_pre'], 'L0_xattn_b_pre': _L0_xattn_in['b_pre'], 'L0_xattn_g_ln': _L0_xattn_in['g_ln'], 'L0_xattn_b_ln': _L0_xattn_in['b_ln'], 'L0_ffn_router_w': _L0_ffn_in['router_w'], 'L0_ffn_router_b': _L0_ffn_in['router_b'], 'L0_ffn_w_gate': _L0_ffn_in['w_gate'], 'L0_ffn_w_up': _L0_ffn_in['w_up'], 'L0_ffn_w_down': _L0_ffn_in['w_down'], 'L0_ffn_sw_gate': _L0_ffn_in['sw_gate'], 'L0_ffn_sw_up': _L0_ffn_in['sw_up'], 'L0_ffn_sw_down': _L0_ffn_in['sw_down']}

def reference(x, ctx_1024, g_xattn, g_ffn, L0_xattn_Wq, L0_xattn_Wk, L0_xattn_Wv, L0_xattn_Wo, L0_xattn_g_pre, L0_xattn_b_pre, L0_xattn_g_ln, L0_xattn_b_ln, L0_ffn_router_w, L0_ffn_router_b, L0_ffn_w_gate, L0_ffn_w_up, L0_ffn_w_down, L0_ffn_sw_gate, L0_ffn_sw_up, L0_ffn_sw_down):
    import jax
    import jax.numpy as jnp

    def _L0_xattn_ref(Q, K, V, Wq, Wk, Wv, Wo, g_pre, b_pre, g_ln, b_ln):
        import jax, jax.numpy as jnp
        import numpy as np
        import math
        DIM_Q = 256
        DIM_V = 256
        DIM_O = 256
        H = 16
        DH_Q = DIM_Q // H
        DH_V = DIM_O // H
        TEMP = math.sqrt(DIM_O)
        EPS = 1e-05

        def layernorm(x, g, b):
            mu = jnp.mean(x, axis=-1, keepdims=True)
            var = jnp.mean(jnp.square(x - mu), axis=-1, keepdims=True)
            return (x - mu) * jax.lax.rsqrt(var + EPS) * g + b
        B, LQ, _ = Q.shape
        LK = K.shape[1]
        Qn = layernorm(Q, g_pre, b_pre)
        Kn = layernorm(K, g_pre, b_pre)
        q = (Qn @ Wq.T).reshape(B, LQ, H, DH_Q)
        k = (Kn @ Wk.T).reshape(B, LK, H, DH_Q)
        v = (V @ Wv.T).reshape(B, LK, H, DH_V)
        L = jnp.einsum('bqhd,bkhd->bhqk', q, k) / TEMP
        L = jnp.clip(L, -10000.0, 10000.0)
        A = jax.nn.softmax(L, axis=-1)
        O = jnp.einsum('bhqk,bkhd->bqhd', A, v).reshape(B, LQ, DIM_O)
        O = layernorm(O, g_ln, b_ln)
        O = O + jax.nn.gelu(O @ Wo.T, approximate=False)
        return O

    def _L0_ffn_ref(x, router_w, router_b, w_gate, w_up, w_down, sw_gate, sw_up, sw_down):
        import jax, jax.numpy as jnp
        import numpy as np
        B, S, D = (1, 512, 256)
        F = 352
        E = 16
        K = 2
        CAP_FACTOR = 1.25

        def _mlp(h, wg, wu, wd):
            return jax.nn.silu(h @ wg) * (h @ wu) @ wd
        b, s, d = x.shape
        N = b * s
        NK = N * K
        C = int(np.ceil(CAP_FACTOR * NK / E))
        x_tokens = x.reshape(N, d)
        logits = x_tokens @ router_w + router_b
        probs = jax.nn.softmax(logits, axis=-1)
        vals, idx = jax.lax.top_k(probs, K)
        vals = vals / (jnp.sum(vals, axis=-1, keepdims=True) + 1e-09)
        idx_flat = idx.reshape(NK)
        vals_flat = vals.reshape(NK)
        oh_e = jax.nn.one_hot(idx_flat, E, dtype=x.dtype)
        pos = (jnp.cumsum(oh_e, axis=0) * oh_e).sum(axis=1) - 1
        within = (pos < C).astype(x.dtype)
        pos_c = jnp.clip(pos, 0, C - 1).astype(jnp.int32)
        token_ids = jnp.arange(NK) // K
        x_pair = x_tokens[token_ids] * within[:, None]
        expert_inputs = jnp.zeros((E, C, d), x.dtype).at[idx_flat, pos_c].add(x_pair)
        expert_outputs = jax.vmap(_mlp)(expert_inputs, w_gate, w_up, w_down)
        gathered = expert_outputs[idx_flat, pos_c] * (vals_flat * within)[:, None]
        output_tokens = gathered.reshape(N, K, d).sum(axis=1)
        return x + _mlp(x, sw_gate, sw_up, sw_down) + output_tokens.reshape(b, s, d)
    x = x + jnp.tanh(g_xattn[0]) * _L0_xattn_ref(_layernorm(x, axis=-1), ctx_1024, ctx_1024, L0_xattn_Wq, L0_xattn_Wk, L0_xattn_Wv, L0_xattn_Wo, L0_xattn_g_pre, L0_xattn_b_pre, L0_xattn_g_ln, L0_xattn_b_ln)
    x = x + jnp.tanh(g_ffn[0]) * _L0_ffn_ref(_layernorm(x, axis=-1), L0_ffn_router_w, L0_ffn_router_b, L0_ffn_w_gate, L0_ffn_w_up, L0_ffn_w_down, L0_ffn_sw_gate, L0_ffn_sw_up, L0_ffn_sw_down)
    return x

_drawn_inputs = setup_inputs


def setup_inputs(seed=0):
    import zlib

    import numpy as np

    out = dict(_drawn_inputs(seed))
    spreads = {'L0_xattn_g_pre': (1.0, 0.6),
     'L0_xattn_b_pre': (0.0, 0.8),
     'L0_xattn_g_ln': (1.0, 0.2),
     'L0_xattn_b_ln': (0.0, 0.1),
     'L0_ffn_router_b': (0.0, 0.336)}
    factors = {'L0_xattn_Wq': 7.875, 'L0_xattn_Wk': 7.977}
    for name, (base, spread) in spreads.items():
        noise = np.random.default_rng([zlib.crc32(name.encode()), seed]).standard_normal(out[name].shape)
        drawn = base * np.exp(spread * noise) if base else spread * noise
        out[name] = jnp.asarray(drawn.astype(out[name].dtype))
    for name, factor in factors.items():
        out[name] = (out[name] * factor).astype(out[name].dtype)
    return out
```

```python
import concourse.bass as bass
from concourse import mybir
from contextlib import ExitStack

F32 = mybir.dt.float32
BF16 = mybir.dt.bfloat16
U32 = mybir.dt.uint32
ALU = mybir.AluOpType
ACT = mybir.ActivationFunctionType
X = mybir.AxisListType.X

B, LQ, LK, D = 32, 100, 361, 256
H, DH = 16, 16
KH = D // 128
HH = H // KH
KT = 3
KN = [121, 120, 120]
KOFF = [0, 121, 241]
EPS = 1e-5
TEMP = 16.0
CLIP = 10000.0 * TEMP
BOUND = 0.99 * CLIP
SHARE = 8
E, F, CAP = 16, 352, 500
FN = [128, 128, 96]
RT, RN = 4, 125
CB = 4
CN = CB * LQ
NC = B // CB


class Memory:
    pass


def setup(nc, ins, m):
    loads = [
        (m.x[:, :, :], ins["x"].rearrange("b t d -> t b d")),
        (m.wq[:, :, :], ins["wqT"].rearrange("(k p) n -> p k n", p=128)),
        (m.wk[:, :, :], ins["wkT"].rearrange("(k p) n -> p k n", p=128)),
        (m.wv[:, :, :], ins["wvT"].rearrange("(k p) n -> p k n", p=128)),
        (m.wo[:, :, :], ins["woT"].rearrange("(k p) n -> p k n", p=128)),
        (m.gb_pre[:, 0, :], ins["g_pre"]),
        (m.gb_pre[:, 1, :], ins["b_pre"]),
        (m.g_ln[:, :], ins["g_ln"].partition_broadcast(LQ)),
        (m.b_ln[:, :], ins["b_ln"].partition_broadcast(LQ)),
        (m.wr[:, :, :], ins["router_w"].rearrange("(k p) n -> p k n", p=128)),
        (m.br[:, :], ins["router_b"].rearrange("(p o) -> p o", o=1)),
        (m.gates[:, 0:1], ins["g_xattn"].partition_broadcast(128)),
        (m.gates[:, 1:2], ins["g_ffn"].partition_broadcast(128)),
    ]
    with ExitStack() as ctx:
        def sb(name, shape, dt=F32):
            return ctx.enter_context(nc.sbuf_tensor(name, shape, dt))

        def sem(name):
            return ctx.enter_context(nc.semaphore(name))

        loaded, made, masks, zeroed = sem("loaded"), sem("made"), sem("masks"), sem("zeroed")
        squared, summed, bound_step = sem("squared"), sem("summed"), sem("bound_step")
        wgain = [sb(f"weight_gain_{n}", [128, KH, D]) for n in "qk"]
        wsq = [sb(f"weight_square_{n}", [128, KH, D]) for n in "qk"]
        norm2 = sb("row_norm2", [1, 2 * D])
        off = sb("row_offset", [1, 2 * D])
        off2 = sb("row_offset2", [1, 2 * D])
        size2 = sb("row_bound2", [1, 2 * D])
        heads = sb("head_sums", [1, 2, H])
        prod = sb("head_bounds", [1, H])
        largest = sb("largest_bound", [1, 1])
        inside = sb("inside_bound", [1, 1])
        np_ = ctx.enter_context(nc.psum_tensor("row_norm_psum", [128, 512], F32))
        op_ = ctx.enter_context(nc.psum_tensor("row_offset_psum", [128, 512], F32))
        block = ctx.enter_context(nc.Block())

        @block.sync
        def _(sp):
            for dst, src in loads:
                sp.dma_start(dst, src).then_inc(loaded, 16)
            sp.wait_ge(loaded, 16 * len(loads))

        @block.gpsimd
        def _(pool):
            nc.gpsimd.memset(m.ident[:, :], 0.0).then_inc(made, 1)
            nc.gpsimd.memset(m.headmask[:, :], 1.0).then_inc(made, 1)
            nc.gpsimd.memset(m.earlier[:, :], 1.0).then_inc(made, 1)
            nc.gpsimd.iota(m.expert_u[:, :], pattern=[[1, E]], base=0, channel_multiplier=0).then_inc(made, 1)
            pool.wait_ge(made, 4)
            nc.gpsimd.affine_select(out=m.ident[:, :], in_=m.ident[:, :], compare_op=ALU.not_equal, fill=1.0,
                                    base=0, pattern=[[-1, 128]], channel_multiplier=1).then_inc(masks, 1)
            nc.gpsimd.affine_select(out=m.headmask[:, :], in_=m.headmask[:, :], compare_op=ALU.is_ge, fill=0.0,
                                    base=0, pattern=[[-DH, HH]], channel_multiplier=1).then_inc(masks, 1)
            nc.gpsimd.affine_select(out=m.earlier[:, :], in_=m.earlier[:, :], compare_op=ALU.is_ge, fill=0.0,
                                    base=-1, pattern=[[1, LQ]], channel_multiplier=-1).then_inc(masks, 1)
            pool.wait_ge(masks, 3)
            nc.gpsimd.affine_select(out=m.headmask[:, :], in_=m.headmask[:, :], compare_op=ALU.is_ge, fill=0.0,
                                    base=DH - 1, pattern=[[DH, HH]], channel_multiplier=-1).then_inc(masks, 1)

        @block.vector
        def _(dve):
            nc.vector.memset(m.ones[:, :], 1.0)
            nc.vector.memset(m.ones_b[:, :], 1.0)
            nc.vector.memset(m.minus_half[:, :], -0.5)
            nc.vector.memset(m.eps[:, :], EPS)
            for s in range(2):
                nc.vector.memset(m.mv[s][:, :, :], 1.0)
            nc.vector.memset(m.zeros[:, :], 0.0).then_inc(zeroed, 1)
            dve.wait_ge(masks, 4)
            nc.vector.reduce_sum(m.side[:, 0:1], m.headmask[:, 0:HH:2], axis=X)
            nc.vector.reduce_sum(m.side[:, 1:2], m.headmask[:, 1:HH:2], axis=X)
            nc.vector.tensor_copy(m.ident_b[:, :], m.ident[:, :])
            nc.vector.tensor_copy(m.headmask_b[:, :], m.headmask[:, :])
            nc.vector.tensor_copy(m.expert_f[:, :], m.expert_u[:, :])
            dve.wait_ge(loaded, 16 * len(loads))
            for i, w in enumerate((m.wq, m.wk)):
                for k in range(KH):
                    last = nc.vector.tensor_scalar(wgain[i][:, k, :], w[:, k, :], m.gb_pre[:, 0, k:k + 1], None,
                                                   ALU.mult)
            last.then_inc(squared, 1)
            dve.wait_ge(squared, 1)
            for i in range(2):
                last = nc.vector.tensor_tensor(wsq[i][:, :, :], wgain[i][:, :, :], wgain[i][:, :, :], ALU.mult)
            last.then_inc(squared, 1)
            dve.wait_ge(summed, 1)
            nc.vector.tensor_scalar(off[:, :], op_[0:1, :], 1.0, None, ALU.mult)
            nc.vector.tensor_scalar(norm2[:, :], np_[0:1, :], (1 + 1 / SHARE) * D, None, ALU.mult
                                    ).then_inc(bound_step, 1)
            dve.wait_ge(bound_step, 1)
            nc.vector.tensor_tensor(off2[:, :], off[:, :], off[:, :], ALU.mult).then_inc(bound_step, 1)
            dve.wait_ge(bound_step, 2)
            nc.vector.scalar_tensor_tensor(size2[:, :], off2[:, :], 1.0 + SHARE, norm2[:, :], ALU.mult, ALU.add
                                           ).then_inc(bound_step, 1)
            dve.wait_ge(bound_step, 3)
            nc.vector.reduce_sum(heads[:, :, :], size2[:, :].rearrange("p (w h d) -> p w h d", w=2, d=DH), axis=X
                                 ).then_inc(bound_step, 1)
            dve.wait_ge(bound_step, 4)
            nc.vector.tensor_tensor(prod[:, :], heads[:, 0, :], heads[:, 1, :], ALU.mult).then_inc(bound_step, 1)
            dve.wait_ge(bound_step, 5)
            nc.vector.reduce_max(largest[:, :], prod[:, :], axis=X).then_inc(bound_step, 1)
            dve.wait_ge(bound_step, 6)
            nc.vector.tensor_scalar(inside[:, :], largest[:, :], BOUND * BOUND, None, ALU.is_lt).then_inc(bound_step, 1)
            dve.wait_ge(bound_step, 7)
            nc.vector.tensor_copy(m.inside[:, :], inside[:, :])

        @block.tensor
        def _(pe):
            pe.wait_ge(squared, 2)
            for i, w in enumerate((m.wq, m.wk)):
                cols = slice(i * D, (i + 1) * D)
                for k in range(KH):
                    nc.tensor.matmul(np_[0:1, cols], m.ones[:, 0:1], wsq[i][:, k, :], start=k == 0, stop=k == KH - 1)
                for k in range(KH):
                    last = nc.tensor.matmul(op_[0:1, cols], m.gb_pre[:, 1, k:k + 1], w[:, k, :],
                                            start=k == 0, stop=k == KH - 1)
            last.then_inc(summed, 1)

        @block.scalar
        def _(act):
            act.wait_ge(loaded, 16 * len(loads))
            nc.scalar.activation(m.tanh[:, :], m.gates[:, :], ACT.Tanh)


def attention(nc, ins, m):
    RING = 10 + H
    with ExitStack() as ctx:
        def sb(name, shape, dt=F32):
            return ctx.enter_context(nc.sbuf_tensor(name, shape, dt))

        def pair(name, shape, dt=F32):
            return [sb(f"{name}{s}", shape, dt) for s in range(2)]

        def sem(name):
            return ctx.enter_context(nc.semaphore(name))

        raw = pair("ctx_raw", [128, KT, D])
        norm = pair("ctx_norm", [128, KT, D])
        zq = pair("x_norm", [LQ, D])
        st = pair("stats", [128, KT + 1, 6])
        st2 = pair("stats2", [LQ, 6])
        mv2 = pair("mean_var2", [LQ, 2])
        var = pair("var_eps", [128, KT + 1])
        rs = pair("rstd", [128, KT + 1])
        var2 = pair("var_eps2", [LQ, 1])
        rs2 = pair("rstd2", [LQ, 1])
        qnT = sb("qnT", [128, KH, LQ])
        knT = sb("knT", [128, KH, LK])
        cT = sb("cT", [128, KH, LK])
        qh = sb("q_hi", [128, KH, LQ], BF16)
        ql = sb("q_lo", [128, KH, LQ], BF16)
        kh = pair("k_hi", [128, KH, LK], BF16)
        kl = pair("k_lo", [128, KH, LK], BF16)
        v = pair("v", [128, KT, D])
        qbh = pair("q_block_hi", [128, KH, HH, LQ], BF16)
        qbl = pair("q_block_lo", [128, KH, HH, LQ], BF16)
        mx = pair("score_max", [LQ, H])
        mxn = pair("minus_max", [LQ, H])
        mneg = pair("minus_max_bf", [LQ, H], BF16)
        mdiag = pair("minus_max_diag", [LQ, H, LQ], BF16)
        probs = pair("probs", [128, HH, LQ])
        dsel0 = sb("den_first", [128, KH, LQ])
        dsel = sb("den", [128, KH, LQ])
        osel0 = sb("o_first", [128, KH, LQ])
        osel = sb("o_sum", [128, KH, LQ])
        rden = sb("den_inv", [128, KH, LQ])
        onT = sb("oT", [128, KH, LQ])
        carrier_p, carrier_v = sb("carrier_pool", [1, 1]), sb("carrier_vector", [1, 1])

        scores = ctx.enter_context(nc.psum_tensor("scores", [128, 4, 512], F32))
        ring = [ctx.enter_context(nc.psum_tensor(f"ring{s}", [128, 512], F32)) for s in range(2)]
        ob = ctx.enter_context(nc.psum_tensor("o_bank", [128, 512], F32))
        db = ctx.enter_context(nc.psum_tensor("den_bank", [128, 512], F32))

        raw_loaded = [sem(f"raw_loaded{s}") for s in range(2)]
        xg_zeroed = sem("xg_zeroed")
        bn_done = sem("bn_done")
        stats_done = sem("stats_done")
        rstd_step = sem("rstd_step")
        z1_done = sem("z1_done")
        norm_done = sem("norm_done")
        bn2_done = sem("bn2_done")
        stats2_done = sem("stats2_done")
        rstd2_step = sem("rstd2_step")
        z2_done = sem("z2_done")
        filled = [sem(f"ring_filled{s}") for s in range(2)]
        emptied = [sem(f"ring_emptied{s}") for s in range(2)]
        qh_done = sem("qh_done")
        qb_done = sem("q_block_done")
        kh_done = sem("kh_done")
        max_clipped = sem("max_clipped")
        mneg_done = sem("mneg_done")
        mdiag_done = sem("mdiag_done")
        raw_done = sem("raw_scores_done")
        clipped = sem("scores_clipped")
        scores_done = sem("scores_done")
        exp_done = sem("exp_done")
        pv_done = sem("pv_done")
        fin_step = sem("fin_step")
        on_done = sem("on_done")
        ot_done = sem("ot_done")
        ot_emptied = sem("ot_emptied")

        def nth(b, pos):
            return (RING // 2) * b + pos // 2 + 1

        def over_batches(eng, step):
            step(-1, 1, False, True, False)
            for b in range(2):
                step(b, b, True, True, True)
            with eng.Fori(1, B // 2 - 1) as it:
                for s in range(2):
                    step(it * 2 + s, s, True, True, True)
            step(B - 2, 0, True, True, False)
            step(B - 1, 1, True, False, False)

        def either(eng, program):
            inside = eng.value_load(m.inside[0:1, 0:1], min_val=0, max_val=1)
            with eng.If(inside > 0):
                program(False)
            with eng.Else():
                program(True)

        with nc.Block() as block:

            @block.sync
            def _(sp):
                def load(b, s, use):
                    sp.dma_start(raw[s][0:120, :, :],
                                 ins["ctx"][bass.ds(b, 1), 0:360, :].rearrange("o (p t) d -> p (o t) d", t=KT)
                                 ).then_inc(raw_loaded[s], 16)
                    sp.dma_start(raw[s][120:121, 0, :],
                                 ins["ctx"][bass.ds(b, 1), 360:361, :].rearrange("o p d -> p (o d)")
                                 ).then_inc(raw_loaded[s], 16)

                load(0, 0, 0)
                load(1, 1, 0)
                for e in range(E):
                    sp.dma_start(ins["xg"][e * CAP:(e + 1) * CAP, :].rearrange("(p t) d -> p (t d)", t=RT),
                                 m.zeros[0:RN, :]).then_inc(xg_zeroed, 16)
                with sp.Fori(1, B // 2) as it:
                    for s in range(2):
                        sp.wait_ge(filled[1], nth(it * 2 + s - 2, 5))
                        load(it * 2 + s, s, it)
                sp.wait_ge(xg_zeroed, 16 * E)

            @block.gpsimd
            def _(pool):
                def after(semaphore, count):
                    pool.wait_ge(semaphore, count)
                    nc.gpsimd.tensor_tensor(carrier_p[:, :], m.eps[0:1, 0:1], m.eps[0:1, 0:1], ALU.add)

                def normalise(b, s, first=False):
                    pool.wait_ge(stats_done, b + 1)
                    if not first:
                        pool.wait_ge(filled[0], nth(b - 2, 2))
                        pool.wait_ge(filled[1], nth(b - 2, 1))
                    nc.gpsimd.tensor_tensor(var[s][:, :], m.mv[s][:, :, 1], m.eps[:, 0:KT + 1], ALU.add
                                            ).then_inc(rstd_step, 1)
                    pool.wait_ge(rstd_step, 2 * b + 1)
                    nc.gpsimd.tensor_tensor(rs[s][:, :], var[s][:, :], m.minus_half[:, 0:KT + 1],
                                            ALU.pow).then_inc(rstd_step, 1)
                    after(rstd_step, 2 * b + 2)
                    for t in range(KT):
                        last = nc.gpsimd.tensor_scalar(norm[s][0:KN[t], t, :], raw[s][0:KN[t], t, :],
                                                       m.mv[s][0:KN[t], t, 0:1], rs[s][0:KN[t], t:t + 1],
                                                       ALU.subtract, ALU.mult)
                    last.then_inc(norm_done, 1)

                def normalise_again(b, s):
                    pool.wait_ge(stats2_done, b + 1)
                    nc.gpsimd.tensor_tensor(var2[s][:, :], mv2[s][:, 1:2], m.eps[0:LQ, 0:1], ALU.add
                                            ).then_inc(rstd2_step, 1)
                    pool.wait_ge(rstd2_step, 2 * b + 1)
                    nc.gpsimd.tensor_tensor(rs2[s][:, :], var2[s][:, :], m.minus_half[0:LQ, 0:1],
                                            ALU.pow).then_inc(rstd2_step, 1)
                    after(rstd2_step, 2 * b + 2)
                    nc.gpsimd.tensor_scalar(zq[s][:, :], zq[s][:, :], mv2[s][:, 0:1], rs2[s][:, :],
                                            ALU.subtract, ALU.mult).then_inc(z2_done, 1)

                def q_blocks(b, s):
                    pool.wait_ge(qh_done, b + 1)
                    pool.wait_ge(emptied[1], nth(b, 3))
                    for src, dst in ((qh, qbh[s]), (ql, qbl[s])):
                        for k in range(KH):
                            last = nc.gpsimd.tensor_tensor(
                                dst[:, k, :, :], src[:, k, :].unsqueeze(1).to_broadcast([128, HH, LQ]),
                                m.headmask_b[:, :].unsqueeze(2).to_broadcast([128, HH, LQ]), ALU.mult)
                        last.then_inc(qb_done, 1)

                def max_diagonal(b, s, k):
                    pool.wait_ge(mneg_done, 2 * b + k + 1)
                    nc.gpsimd.tensor_tensor(
                        mdiag[s][:, HH * k:HH * (k + 1), :],
                        mneg[s][:, HH * k:HH * (k + 1)].unsqueeze(2).to_broadcast([LQ, HH, LQ]),
                        m.ident_b[0:LQ, 0:LQ].unsqueeze(1).to_broadcast([LQ, HH, LQ]),
                        ALU.mult).then_inc(mdiag_done, 1)

                def step(b, s, this, following, after):
                    if after:
                        normalise(b + 2, s)
                    if following:
                        q_blocks(b + 1, 1 - s)
                    if after:
                        normalise_again(b + 2, s)
                    if following:
                        for k in range(KH):
                            max_diagonal(b + 1, 1 - s, k)

                for b in range(2):
                    normalise(b, b, first=True)
                    normalise_again(b, b)
                over_batches(pool, step)

            @block.vector
            def _(dve):
                def after(semaphore, count):
                    dve.wait_ge(semaphore, count)
                    nc.vector.memset(carrier_v[:, :], 0.0)

                def statistics(b, s, use):
                    dve.wait_ge(raw_loaded[s], 32 * (use + 1))
                    for t in range(KT):
                        nc.vector.bn_stats(st[s][0:KN[t], t, :], raw[s][0:KN[t], t, :])
                    nc.vector.bn_stats(st[s][0:LQ, KT, :], m.x[:, bass.ds(b, 1), :].rearrange("p o d -> p (o d)")
                                       ).then_inc(bn_done, 1)
                    after(bn_done, b + 1)
                    for t in range(KT):
                        nc.vector.bn_aggr(m.mv[s][0:KN[t], t, :], st[s][0:KN[t], t, :])
                    nc.vector.bn_aggr(m.mv[s][0:LQ, KT, :], st[s][0:LQ, KT, :]).then_inc(stats_done, 1)

                def statistics_again(b, s):
                    dve.wait_ge(rstd_step, 2 * b + 2)
                    nc.vector.tensor_scalar(zq[s][:, :], m.x[:, bass.ds(b, 1), :].rearrange("p o d -> p (o d)"),
                                            m.mv[s][0:LQ, KT, 0:1], rs[s][0:LQ, KT:KT + 1],
                                            ALU.subtract, ALU.mult).then_inc(z1_done, 1)
                    dve.wait_ge(z1_done, b + 1)
                    nc.vector.bn_stats(st2[s][:, :], zq[s][:, :]).then_inc(bn2_done, 1)
                    after(bn2_done, b + 1)
                    nc.vector.bn_aggr(mv2[s][:, :], st2[s][:, :]).then_inc(stats2_done, 1)

                def affine(b, pos, dst, n, halves):
                    dve.wait_ge(filled[pos % 2], nth(b, pos))
                    for i, k in enumerate(halves):
                        last = nc.vector.tensor_scalar(dst[:, k, :], ring[pos % 2][:, i * n:(i + 1) * n],
                                                       m.gb_pre[:, 0, k:k + 1], m.gb_pre[:, 1, k:k + 1],
                                                       ALU.mult, ALU.add)
                    last.then_inc(emptied[pos % 2], 1)

                def low_part(b, pos, dst, hi, n, hi_done, count):
                    dve.wait_ge(filled[pos % 2], nth(b, pos))
                    dve.wait_ge(hi_done, count)
                    nc.vector.tensor_tensor(dst, ring[pos % 2][:, 0:n], hi, ALU.subtract).then_inc(emptied[pos % 2], 1)

                def clip(b, u):
                    k, t = u // KT, u % KT
                    dve.wait_ge(raw_done, 6 * b + u + 1)
                    bank = scores[0:KN[t], 2 * (u % 2):2 * (u % 2) + 2, 0:4 * LQ]
                    nc.vector.tensor_scalar(bank, bank, CLIP, -CLIP, ALU.min, ALU.max).then_inc(clipped, 1)

                def maxima(b, s, k, clips):
                    for h in range(HH * k, HH * (k + 1)):
                        if clips is not None and h in (4, 10):
                            clip(clips, 4 if h == 4 else 5)
                        pos = 10 + h
                        dve.wait_ge(filled[pos % 2], nth(b, pos))
                        nc.vector.reduce_max(mx[s][:, h:h + 1], ring[pos % 2][0:LQ, 0:LK], axis=X
                                             ).then_inc(emptied[pos % 2], 1)
                    half = slice(HH * k, HH * (k + 1))
                    dve.wait_ge(emptied[0], nth(b, 10 + HH * (k + 1) - 2))
                    dve.wait_ge(emptied[1], nth(b, 10 + HH * (k + 1) - 1))
                    nc.vector.tensor_scalar(mxn[s][:, half], mx[s][:, half], -1.0, CLIP, ALU.mult, ALU.min
                                            ).then_inc(max_clipped, 1)
                    dve.wait_ge(max_clipped, 2 * b + k + 1)
                    nc.vector.tensor_scalar(mneg[s][:, half], mxn[s][:, half], -CLIP, None, ALU.max
                                            ).then_inc(mneg_done, 1)

                def finish(b):
                    dve.wait_ge(pv_done, 6 * b + 6)
                    den = db[:, 0:4 * LQ].rearrange("p (m e q) -> p m e q", m=KH, e=2)
                    out = ob[:, 0:4 * LQ].rearrange("p (m e q) -> p m e q", m=KH, e=2)
                    nc.vector.tensor_scalar(dsel0[:, :, :], den[:, :, 0, :], m.side[:, 0:1], None, ALU.mult)
                    nc.vector.tensor_scalar(osel0[:, :, :], out[:, :, 0, :], m.side[:, 0:1], None, ALU.mult
                                            ).then_inc(fin_step, 1)
                    dve.wait_ge(fin_step, 3 * b + 1)
                    nc.vector.scalar_tensor_tensor(dsel[:, :, :], den[:, :, 1, :], m.side[:, 1:2], dsel0[:, :, :],
                                                   ALU.mult, ALU.add)
                    nc.vector.scalar_tensor_tensor(osel[:, :, :], out[:, :, 1, :], m.side[:, 1:2], osel0[:, :, :],
                                                   ALU.mult, ALU.add).then_inc(fin_step, 1)
                    dve.wait_ge(fin_step, 3 * b + 2)
                    nc.vector.reciprocal(rden[:, :, :], dsel[:, :, :]).then_inc(fin_step, 1)
                    dve.wait_ge(fin_step, 3 * b + 3)
                    nc.vector.tensor_tensor(onT[:, :, :], osel[:, :, :], rden[:, :, :], ALU.mult).then_inc(on_done, 1)

                def step(b, s, this, following, after, clips):
                    n = 1 - s
                    clips = clips and this
                    if clips:
                        clip(b, 0)
                    if this and not (isinstance(b, int) and b == 0):
                        finish(b - 1)
                    if following:
                        affine(b + 1, 0, qnT, LQ, range(KH))
                        affine(b + 1, 1, knT, LK, [0])
                        affine(b + 1, 2, knT, LK, [1])
                    if clips:
                        clip(b, 1)
                    if after:
                        statistics(b + 2, s, (b + 2 - s) // 2)
                    if following:
                        low_part(b + 1, 3, ql[:, :, :].rearrange("p k q -> p (k q)"),
                                 qh[:, :, :].rearrange("p k q -> p (k q)"), KH * LQ, qh_done, b + 2)
                        low_part(b + 1, 6, kl[n][:, 0, :], kh[n][:, 0, :], LK, kh_done, 2 * (b + 1) + 1)
                    if clips:
                        clip(b, 2)
                    if following:
                        low_part(b + 1, 7, kl[n][:, 1, :], kh[n][:, 1, :], LK, kh_done, 2 * (b + 1) + 2)
                    if clips:
                        clip(b, 3)
                    if after:
                        statistics_again(b + 2, s)
                    if following:
                        for k in range(KH):
                            maxima(b + 1, n, k, b if clips else None)
                    elif clips:
                        clip(b, 4)
                        clip(b, 5)

                for b in range(2):
                    statistics(b, b, 0)
                    statistics_again(b, b)
                either(dve, lambda clips: over_batches(dve, lambda *a: step(*a, clips)))
                finish(B - 1)

            @block.scalar
            def _(act):
                def evacuate(b, pos, dst, src, then=None):
                    act.wait_ge(filled[pos % 2], nth(b, pos))
                    nc.scalar.activation(dst, src, ACT.Copy).then_inc(then or emptied[pos % 2], 1)

                def exps(b, u):
                    k, t = u // KT, u % KT
                    act.wait_ge(scores_done, 6 * b + u + 1)
                    if not (isinstance(b, int) and b == 0 and u < 2):
                        act.wait_ge(pv_done, 6 * b + u - 1)
                    nc.scalar.activation(probs[u % 2][0:KN[t], :, :].rearrange("p (c h) q -> p c (h q)", c=2),
                                         scores[0:KN[t], 2 * (u % 2):2 * (u % 2) + 2, 0:4 * LQ],
                                         ACT.Exp, scale=1.0 / TEMP).then_inc(exp_done, 1)

                def take_o(b):
                    act.wait_ge(ot_done, b + 1)
                    nc.scalar.activation(m.h2[:, bass.ds(b, 1), :].rearrange("p o d -> p (o d)"), ob[0:LQ, 0:D],
                                         ACT.Copy).then_inc(ot_emptied, 1)

                def step(b, s, this, following, after):
                    n = 1 - s
                    if this:
                        exps(b, 0)
                        if not (isinstance(b, int) and b == 0):
                            take_o(b - 1)
                        exps(b, 1)
                    if following:
                        if not (isinstance(b, int) and b == -1):
                            act.wait_ge(qb_done, 2 * b + 2)
                        evacuate(b + 1, 3, qh[:, :, :].rearrange("p k q -> p (k q)"), ring[1][:, 0:KH * LQ], qh_done)
                        evacuate(b + 1, 4, cT[:, 0, :], ring[0][:, 0:LK])
                        evacuate(b + 1, 5, cT[:, 1, :], ring[1][:, 0:LK])
                        evacuate(b + 1, 6, kh[n][:, 0, :], ring[0][:, 0:LK], kh_done)
                    if this:
                        exps(b, 2)
                    if following:
                        evacuate(b + 1, 7, kh[n][:, 1, :], ring[1][:, 0:LK], kh_done)
                        evacuate(b + 1, 8, v[n][0:KN[0], 0, :], ring[0][0:KN[0], 0:D])
                        evacuate(b + 1, 9, v[n][0:KN[1], 1:3, :].rearrange("p t d -> p (t d)"),
                                 ring[1][0:KN[1], 0:2 * D])
                    if this:
                        for u in range(3, 6):
                            exps(b, u)

                over_batches(act, step)
                take_o(B - 1)

            @block.tensor
            def _(pe):
                def free_ring(b, pos):
                    if not (isinstance(b, int) and b == 0 and pos < 2):
                        pe.wait_ge(emptied[pos % 2], nth(b, pos) - 1)

                def transpose_x(b, s):
                    pe.wait_ge(z2_done, b + 1)
                    free_ring(b, 0)
                    for k in range(KH):
                        last = nc.tensor.transpose(ring[0][:, k * LQ:(k + 1) * LQ], zq[s][:, k * 128:(k + 1) * 128],
                                                   m.ident[0:LQ, 0:LQ])
                    last.then_inc(filled[0], 1)

                def transpose_ctx(b, pos, src, k, ready):
                    if ready is not None:
                        pe.wait_ge(ready, b + 1)
                    free_ring(b, pos)
                    for t in range(KT):
                        last = nc.tensor.transpose(ring[pos % 2][:, KOFF[t]:KOFF[t] + KN[t]],
                                                   src[0:KN[t], t, k * 128:(k + 1) * 128],
                                                   m.ident[0:KN[t], 0:KN[t]])
                    last.then_inc(filled[pos % 2], 1)

                def project(b, pos, w, src, mts, n, inputs):
                    for p in inputs:
                        pe.wait_ge(emptied[p % 2], nth(b, p))
                    free_ring(b, pos)
                    for i, mt in enumerate(mts):
                        for k in range(KH):
                            last = nc.tensor.matmul(ring[pos % 2][:, i * n:(i + 1) * n],
                                                    w[:, k, mt * 128:(mt + 1) * 128], src[:, k, :],
                                                    start=k == 0, stop=k == KH - 1)
                    last.then_inc(filled[pos % 2], 1)

                def project_v(b, pos, tiles):
                    if pos == 8:
                        pe.wait_ge(emptied[1], nth(b, 5))
                    free_ring(b, pos)
                    for i, t in enumerate(tiles):
                        for k in range(KH):
                            last = nc.tensor.matmul(ring[pos % 2][0:KN[t], i * D:(i + 1) * D],
                                                    cT[:, k, KOFF[t]:KOFF[t] + KN[t]], m.wv[:, k, :],
                                                    start=k == 0, stop=k == KH - 1)
                    last.then_inc(filled[pos % 2], 1)

                def scores_for_max(b, s, h, clips):
                    pos = 10 + h
                    k, j = h // HH, h % HH
                    pe.wait_ge(qb_done, 2 * b + 1)
                    pe.wait_ge(kh_done, 2 * b + 1 + k)
                    free_ring(b, pos)
                    bank = ring[pos % 2][0:LQ, 0:LK]
                    if clips:
                        if h == 0:
                            pe.wait_ge(qb_done, 2 * b + 2)
                        nc.tensor.matmul(bank, qbl[s][:, k, j, :], kh[s][:, k, :], start=True, stop=False)
                        nc.tensor.matmul(bank, qbh[s][:, k, j, :], kl[s][:, k, :], start=False, stop=False)
                    nc.tensor.matmul(bank, qbh[s][:, k, j, :], kh[s][:, k, :], start=not clips, stop=True
                                     ).then_inc(filled[pos % 2], 1)

                def score_unit(b, s, u, clips):
                    k, t = u // KT, u % KT
                    if u % KT == 0:
                        pe.wait_ge(qb_done, 2 * b + 2)
                        pe.wait_ge(emptied[k], nth(b, 6 + k))
                        pe.wait_ge(mdiag_done, 2 * b + k + 1)
                    if not (isinstance(b, int) and b == 0 and u < 2):
                        pe.wait_ge(exp_done, 6 * b + u - 1)
                    keys = slice(KOFF[t], KOFF[t] + KN[t])
                    banks = [scores[0:KN[t], 2 * (u % 2) + c, 0:4 * LQ] for c in range(2)]
                    for c in range(2):
                        heads = slice(4 * c, 4 * c + 4)
                        nc.tensor.matmul(banks[c], kh[s][:, k, keys], qbh[s][:, k, heads, :], start=True, stop=False)
                        nc.tensor.matmul(banks[c], kh[s][:, k, keys], qbl[s][:, k, heads, :], start=False, stop=False)
                        last = nc.tensor.matmul(banks[c], kl[s][:, k, keys], qbh[s][:, k, heads, :],
                                                start=False, stop=clips)
                    if clips:
                        last.then_inc(raw_done, 1)
                        pe.wait_ge(clipped, 6 * b + u + 1)
                    for c in range(2):
                        last = nc.tensor.matmul(banks[c], m.ones_b[0:LQ, 0:KN[t]],
                                                mdiag[s][:, HH * k + 4 * c:HH * k + 4 * c + 4, :],
                                                start=False, stop=True, skip_group_check=clips)
                    last.then_inc(scores_done, 1)

                def weighted_sum(b, s, u):
                    k, t = u // KT, u % KT
                    pe.wait_ge(exp_done, 6 * b + u + 1)
                    if u == 0:
                        pe.wait_ge(emptied[0], nth(b, 8))
                        pe.wait_ge(emptied[1], nth(b, 9))
                        if not (isinstance(b, int) and b == 0):
                            pe.wait_ge(ot_emptied, b)
                    for lhs, bank in ((v[s], ob), (None, db)):
                        for g in range(4):
                            w = m.ones[0:KN[t], 0:32] if lhs is None else \
                                lhs[0:KN[t], t, 128 * k + 32 * g:128 * k + 32 * g + 32]
                            last = nc.tensor.matmul(bank[32 * g:32 * g + 32, 2 * LQ * k:2 * LQ * (k + 1)], w,
                                                    probs[u % 2][0:KN[t], 2 * g:2 * g + 2, :],
                                                    start=t == 0, stop=t == KT - 1)
                    last.then_inc(pv_done, 1)

                def transpose_o(b):
                    pe.wait_ge(on_done, b + 1)
                    for k in range(KH):
                        last = nc.tensor.transpose(ob[0:LQ, 128 * k:128 * (k + 1)], onT[:, k, :], m.ident[:, :])
                    last.then_inc(ot_done, 1)

                def step(b, s, this, following, after, clips):
                    n = 1 - s
                    if this:
                        score_unit(b, s, 0, clips)
                    if following:
                        transpose_x(b + 1, n)
                        transpose_ctx(b + 1, 1, norm[n], 0, norm_done)
                        transpose_ctx(b + 1, 2, norm[n], 1, None)
                    if this:
                        if not (isinstance(b, int) and b == 0):
                            transpose_o(b - 1)
                        score_unit(b, s, 1, clips)
                    if following:
                        project(b + 1, 3, m.wq, qnT, range(KH), LQ, [0])
                        transpose_ctx(b + 1, 4, raw[n], 0, None)
                    if this:
                        weighted_sum(b, s, 0)
                    if following:
                        transpose_ctx(b + 1, 5, raw[n], 1, None)
                        project(b + 1, 6, m.wk, knT, [0], LK, [1])
                    if this:
                        score_unit(b, s, 2, clips)
                        weighted_sum(b, s, 1)
                    if following:
                        project(b + 1, 7, m.wk, knT, [1], LK, [])
                        project_v(b + 1, 8, [0])
                        project_v(b + 1, 9, [1, 2])
                    if this:
                        score_unit(b, s, 3, clips)
                        weighted_sum(b, s, 2)
                    for u, heads in ((4, range(0, 4)), (5, range(4, 10)), (None, range(10, 16))):
                        if following:
                            for h in heads:
                                scores_for_max(b + 1, n, h, clips)
                        if this:
                            if u is not None:
                                score_unit(b, s, u, clips)
                                weighted_sum(b, s, u - 1)
                            else:
                                weighted_sum(b, s, 5)

                either(pe, lambda clips: over_batches(pe, lambda *a: step(*a, clips)))
                transpose_o(B - 1)


def over_chunks(eng, lead, trail):
    for c in range(4):
        lead(c, c % 2, c < 2)
        if trail and c:
            trail(c - 1, (c - 1) % 2, c < 3)
    with eng.Fori(2, NC // 2) as it:
        for s in range(2):
            lead(it * 2 + s, s, False)
            if trail:
                trail(it * 2 + s - 1, 1 - s, False)
    if trail:
        trail(NC - 1, 1, False)


def output_projection(nc, ins, m):
    with ExitStack() as ctx:
        def sb(name, shape, dt=F32):
            return ctx.enter_context(nc.sbuf_tensor(name, shape, dt))

        def pair(name, shape, dt=F32):
            return [sb(f"{name}{s}", shape, dt) for s in range(2)]

        def sem(name):
            return ctx.enter_context(nc.semaphore(name))

        st = sb("o_stats", [LQ, CB, 6])
        carrier = sb("o_carrier", [1, 1])
        mv = pair("o_mean_var", [LQ, CB, 2])
        var = pair("o_var_eps", [LQ, CB])
        rs = pair("o_rstd", [LQ, CB])
        z = pair("o_norm", [LQ, CB, D])
        zg = pair("o_gained", [LQ, CB, D])
        ol = pair("o_ln", [LQ, CB, D])
        olT = pair("o_lnT", [128, KH, CN])
        ge = pair("o_gelu", [LQ, CB, D])
        y = pair("o_sum", [LQ, CB, D])
        tp = [ctx.enter_context(nc.psum_tensor(f"oT_psum{k}", [128, 512], F32)) for k in range(KH)]
        pr = [ctx.enter_context(nc.psum_tensor(f"proj_psum{s}", [128, 2, 512], F32)) for s in range(2)]

        bn_done, stats_done, rstd_step = sem("o_bn_done"), sem("o_stats_done"), sem("o_rstd_step")
        z_done, zg_done, ln_done = sem("o_z_done"), sem("o_gain_done"), sem("o_ln_done")
        t_done, t_emptied, proj_done = sem("o_t_done"), sem("o_t_emptied"), sem("o_proj_done")
        gelu_done, y_done, x1_done = sem("o_gelu_done"), sem("o_y_done"), sem("o_x1_done")

        def batches(t, c):
            return t[:, bass.ds(c * CB, CB), :]

        with nc.Block() as block:

            @block.vector
            def _(dve):
                def normalise(c, s, first):
                    for j in range(CB):
                        last = nc.vector.bn_stats(st[:, j, :], m.h2[:, bass.ds(c * CB + j, 1), :]
                                                  .rearrange("p o d -> p (o d)"))
                    last.then_inc(bn_done, 1)
                    dve.wait_ge(bn_done, c + 1)
                    nc.vector.memset(carrier[:, :], 0.0)
                    for j in range(CB):
                        last = nc.vector.bn_aggr(mv[s][:, j, :], st[:, j, :])
                    last.then_inc(stats_done, 1)
                    dve.wait_ge(rstd_step, 2 * c + 2)
                    for j in range(CB):
                        last = nc.vector.tensor_scalar(z[s][:, j, :], m.h2[:, bass.ds(c * CB + j, 1), :]
                                                       .rearrange("p o d -> p (o d)"),
                                                       mv[s][:, j, 0:1], rs[s][:, j:j + 1], ALU.subtract, ALU.mult)
                    last.then_inc(z_done, 1)

                def residual(c, s, first):
                    dve.wait_ge(gelu_done, 2 * c + 2)
                    nc.vector.tensor_tensor(y[s][:, :, :], ge[s][:, :, :], ol[s][:, :, :], ALU.add).then_inc(y_done, 1)
                    dve.wait_ge(y_done, c + 1)
                    nc.vector.scalar_tensor_tensor(batches(m.x, c), y[s][:, :, :], m.tanh[0:LQ, 0:1],
                                                   batches(m.x, c), ALU.mult, ALU.add).then_inc(x1_done, 1)

                over_chunks(dve, normalise, residual)

            @block.gpsimd
            def _(pool):
                def step(c, s, first):
                    pool.wait_ge(stats_done, c + 1)
                    nc.gpsimd.tensor_tensor(var[s][:, :], mv[s][:, :, 1], m.eps[0:LQ, 0:CB], ALU.add
                                            ).then_inc(rstd_step, 1)
                    pool.wait_ge(rstd_step, 2 * c + 1)
                    nc.gpsimd.tensor_tensor(rs[s][:, :], var[s][:, :], m.minus_half[0:LQ, 0:CB],
                                            ALU.pow).then_inc(rstd_step, 1)
                    pool.wait_ge(z_done, c + 1)
                    nc.gpsimd.tensor_tensor(zg[s][:, :, :], z[s][:, :, :],
                                            m.g_ln[:, :].unsqueeze(1).to_broadcast([LQ, CB, D]), ALU.mult
                                            ).then_inc(zg_done, 1)
                    pool.wait_ge(zg_done, c + 1)
                    if not first:
                        pool.wait_ge(y_done, c - 1)
                        pool.wait_ge(t_done, c - 1)
                    nc.gpsimd.tensor_tensor(ol[s][:, :, :], zg[s][:, :, :],
                                            m.b_ln[:, :].unsqueeze(1).to_broadcast([LQ, CB, D]), ALU.add
                                            ).then_inc(ln_done, 1)
                over_chunks(pool, step, None)

            @block.tensor
            def _(pe):
                def transposes(c, s, first):
                    pe.wait_ge(ln_done, c + 1)
                    if not (isinstance(c, int) and c == 0):
                        pe.wait_ge(t_emptied, 2 * c)
                    for k in range(KH):
                        for j in range(CB):
                            last = nc.tensor.transpose(tp[k][:, j * LQ:(j + 1) * LQ],
                                                       ol[s][:, j, k * 128:(k + 1) * 128], m.ident[0:LQ, 0:LQ])
                    last.then_inc(t_done, 1)

                def projection(c, s, first):
                    pe.wait_ge(t_emptied, 2 * c + 2)
                    if not first:
                        pe.wait_ge(gelu_done, 2 * c - 2)
                    for j in range(CB):
                        for k in range(KH):
                            last = nc.tensor.matmul(pr[s][0:LQ, j // 2, (j % 2) * D:(j % 2 + 1) * D],
                                                    olT[s][:, k, j * LQ:(j + 1) * LQ], m.wo[:, k, :],
                                                    start=k == 0, stop=k == KH - 1)
                    last.then_inc(proj_done, 1)

                over_chunks(pe, transposes, projection)

            @block.scalar
            def _(act):
                def take(c, s, first):
                    act.wait_ge(t_done, c + 1)
                    if not first:
                        act.wait_ge(proj_done, c - 1)
                    for k in range(KH):
                        nc.scalar.activation(olT[s][:, k, :], tp[k][:, 0:CN], ACT.Copy).then_inc(t_emptied, 1)

                def gelu(c, s, first):
                    act.wait_ge(proj_done, c + 1)
                    if not first:
                        act.wait_ge(y_done, c - 1)
                    for i in range(2):
                        nc.scalar.activation(ge[s][:, 2 * i:2 * i + 2, :].rearrange("p j d -> p (j d)"),
                                             pr[s][0:LQ, i, :], ACT.Gelu).then_inc(gelu_done, 1)

                over_chunks(act, take, gelu)


def tokens_and_logits(nc, ins, m):
    with ExitStack() as ctx:
        def sb(name, shape, dt=F32):
            return ctx.enter_context(nc.sbuf_tensor(name, shape, dt))

        def pair(name, shape, dt=F32):
            return [sb(f"{name}{s}", shape, dt) for s in range(2)]

        def sem(name):
            return ctx.enter_context(nc.semaphore(name))

        st = sb("h_stats", [LQ, CB, 6])
        carrier = sb("h_carrier", [1, 1])
        mv = pair("h_mean_var", [LQ, CB, 2])
        var = pair("h_var_eps", [LQ, CB])
        rs = pair("h_rstd", [LQ, CB])
        h = pair("h_chunk", [LQ, CB, D])
        lT = pair("logits_T", [E, CN])
        tp = [ctx.enter_context(nc.psum_tensor(f"hT_psum{k}", [128, 512], F32)) for k in range(KH)]
        lp = ctx.enter_context(nc.psum_tensor("logits_T_psum", [128, 512], F32))
        lb = ctx.enter_context(nc.psum_tensor("logits_psum", [128, 512], F32))

        bn_done, stats_done, rstd_step = sem("h_bn_done"), sem("h_stats_done"), sem("h_rstd_step")
        h_done, base_done, h_kept = sem("h_done"), sem("base_done"), sem("h_kept")
        t_done, t_emptied, logits_done = sem("h_t_done"), sem("h_t_emptied"), sem("logits_done")
        lT_done, back_done, back_taken = sem("lT_done"), sem("logits_back"), sem("logits_taken")

        def batches(t, c):
            return t[:, bass.ds(c * CB, CB), :]

        def batch(t, c, j):
            return t[:, bass.ds(c * CB + j, 1), :].rearrange("p o d -> p (o d)")

        with nc.Block() as block:

            @block.vector
            def _(dve):
                def normalise(c, s, first):
                    for j in range(CB):
                        last = nc.vector.bn_stats(st[:, j, :], batch(m.x, c, j))
                    last.then_inc(bn_done, 1)
                    dve.wait_ge(bn_done, c + 1)
                    nc.vector.memset(carrier[:, :], 0.0)
                    for j in range(CB):
                        last = nc.vector.bn_aggr(mv[s][:, j, :], st[:, j, :])
                    last.then_inc(stats_done, 1)
                    dve.wait_ge(rstd_step, 2 * c + 2)
                    if not first:
                        dve.wait_ge(t_done, c - 1)
                        dve.wait_ge(h_kept, c - 1)
                    for j in range(CB):
                        last = nc.vector.tensor_scalar(h[s][:, j, :], batch(m.x, c, j), mv[s][:, j, 0:1],
                                                       rs[s][:, j:j + 1], ALU.subtract, ALU.mult)
                    last.then_inc(h_done, 1)
                    dve.wait_ge(h_done, c + 1)
                    nc.vector.scalar_tensor_tensor(batches(m.x, c), h[s][:, :, :], m.tanh[0:LQ, 1:2],
                                                   batches(m.x, c), ALU.mult, ALU.add).then_inc(base_done, 1)

                def take_logits(c, s, first):
                    dve.wait_ge(logits_done, c + 1)
                    nc.vector.tensor_scalar(lT[s][:, :], lp[0:E, 0:CN], m.br[:, 0:1], None, ALU.add
                                            ).then_inc(lT_done, 1)

                over_chunks(dve, normalise, take_logits)

            @block.gpsimd
            def _(pool):
                def step(c, s, first):
                    pool.wait_ge(stats_done, c + 1)
                    nc.gpsimd.tensor_tensor(var[s][:, :], mv[s][:, :, 1], m.eps[0:LQ, 0:CB], ALU.add
                                            ).then_inc(rstd_step, 1)
                    pool.wait_ge(rstd_step, 2 * c + 1)
                    nc.gpsimd.tensor_tensor(rs[s][:, :], var[s][:, :], m.minus_half[0:LQ, 0:CB],
                                            ALU.pow).then_inc(rstd_step, 1)
                    pool.wait_ge(h_done, c + 1)
                    nc.gpsimd.tensor_copy(batches(m.h2, c), h[s][:, :, :]).then_inc(h_kept, 1)
                over_chunks(pool, step, None)

            @block.tensor
            def _(pe):
                def transposes(c, s, first):
                    pe.wait_ge(h_done, c + 1)
                    if not (isinstance(c, int) and c == 0):
                        pe.wait_ge(t_emptied, 2 * c)
                    for k in range(KH):
                        for j in range(CB):
                            last = nc.tensor.transpose(tp[k][:, j * LQ:(j + 1) * LQ],
                                                       h[s][:, j, k * 128:(k + 1) * 128], m.ident[0:LQ, 0:LQ])
                    last.then_inc(t_done, 1)

                def logits(c, s, first):
                    pe.wait_ge(t_emptied, 2 * c + 2)
                    if not (isinstance(c, int) and c == 0):
                        pe.wait_ge(lT_done, c)
                    for k in range(KH):
                        last = nc.tensor.matmul(lp[0:E, 0:CN], m.wr[:, k, :],
                                                m.h2T[:, k, bass.ds(c * CN, CN)],
                                                start=k == 0, stop=k == KH - 1)
                    last.then_inc(logits_done, 1)
                    pe.wait_ge(lT_done, c + 1)
                    if not (isinstance(c, int) and c == 0):
                        pe.wait_ge(back_taken, c)
                    for j in range(CB):
                        last = nc.tensor.matmul(lb[0:LQ, j * E:(j + 1) * E], lT[s][:, j * LQ:(j + 1) * LQ],
                                                m.ident[0:E, 0:E], start=True, stop=True)
                    last.then_inc(back_done, 1)

                over_chunks(pe, transposes, logits)

            @block.scalar
            def _(act):
                def take(c, s, first):
                    act.wait_ge(t_done, c + 1)
                    for k in range(KH):
                        nc.scalar.activation(m.h2T[:, k, bass.ds(c * CN, CN)], tp[k][:, 0:CN], ACT.Copy
                                             ).then_inc(t_emptied, 1)

                def take_logits(c, s, first):
                    act.wait_ge(back_done, c + 1)
                    nc.scalar.activation(batches(m.logits, c).rearrange("p j e -> p (j e)"), lb[0:LQ, 0:CB * E],
                                         ACT.Copy).then_inc(back_taken, 1)

                over_chunks(act, take, take_logits)


def mlp_weights(nc, ctx, name):
    return (ctx.enter_context(nc.sbuf_tensor(f"{name}_gate", [128, KH, F], F32)),
            ctx.enter_context(nc.sbuf_tensor(f"{name}_up", [128, KH, F], F32)),
            ctx.enter_context(nc.sbuf_tensor(f"{name}_down", [128, len(FN), D], F32)))


def route_and_shared(nc, ins, m):
    NF = len(FN)
    with ExitStack() as ctx:
        def sb(name, shape, dt=F32):
            return ctx.enter_context(nc.sbuf_tensor(name, shape, dt))

        def pair(name, shape, dt=F32):
            return [sb(f"{name}{s}", shape, dt) for s in range(2)]

        def sem(name):
            return ctx.enter_context(nc.semaphore(name))

        top = sb("logit_max", [LQ, B])
        pr = sb("router_probs", [LQ, B, E])
        psum_ = sb("prob_sum", [LQ, B])
        rsum = sb("prob_sum_inv", [LQ, B])
        v8 = sb("best_values", [LQ, B, 8])
        i8 = sb("best_experts", [LQ, B, 8], U32)
        best = sb("best2", [LQ, 2, B])
        idx = sb("experts2", [LQ, 2, B])
        oh = sb("one_hot", [LQ, 2, B, E])
        scan = pair("scan", [LQ, B, E])
        before = sb("tiles_before", [LQ, B, E])
        chosen = sb("chosen", [LQ, B, E])
        at = sb("positions_at", [LQ, 2, B, E])
        pos = sb("position", [LQ, 2, B])
        within = sb("within", [LQ, 2, B])
        slot = sb("slot", [LQ, 2, B])
        far = sb("far", [LQ, 2, B])
        den = sb("weight_sum", [LQ, B])
        dinv = sb("weight_sum_inv", [LQ, B])
        wn = sb("weight_norm", [LQ, 2, B])
        wg, wu, wd = mlp_weights(nc, ctx, "shared")
        sg = pair("shared_silu", [128, CN])
        hid = pair("shared_hidden", [128, NF, CN])

        gp = [ctx.enter_context(nc.psum_tensor(f"gate_psum{s}", [128, 512], F32)) for s in range(2)]
        up = [ctx.enter_context(nc.psum_tensor(f"up_psum{s}", [128, 512], F32)) for s in range(2)]
        dn = [ctx.enter_context(nc.psum_tensor(f"down_psum{s}", [128, 2, D], F32)) for s in range(2)]
        pp = ctx.enter_context(nc.psum_tensor("position_psum", [128, 512], F32))

        w_loaded, r, exp_done = sem("shared_loaded"), sem("route_step"), sem("router_exp")
        before_done, counted, routed, scattered = sem("before_done"), sem("counted"), sem("routed"), sem("scattered")
        gu_done, silu_done, hid_done = sem("gate_up_done"), sem("silu_done"), sem("hidden_done")
        down_done, added = sem("down_done"), sem("shared_added")

        with nc.Block() as block:

            @block.sync
            def _(sp):
                load_mlp(sp, (wg, wu, wd), ins["sw_gate"], ins["sw_up"], ins["sw_down"], w_loaded)
                sp.wait_ge(w_loaded, 16 * MLP_LOADS)

            @block.vector
            def _(dve):
                steps = [0]

                def then(ins_):
                    steps[0] += 1
                    ins_.then_inc(r, 1)
                    dve.wait_ge(r, steps[0])

                def wide(t):
                    return t.unsqueeze(2).to_broadcast([LQ, B, E])

                lg = m.logits
                then(nc.vector.reduce_max(top[:, :], lg[:, :, :], axis=X))
                then(nc.vector.tensor_tensor(pr[:, :, :], lg[:, :, :], wide(top[:, :]), ALU.subtract))
                dve.wait_ge(exp_done, 1)
                then(nc.vector.reduce_sum(psum_[:, :], lg[:, :, :], axis=X))
                then(nc.vector.reciprocal(rsum[:, :], psum_[:, :]))
                then(nc.vector.tensor_tensor(pr[:, :, :], lg[:, :, :], wide(rsum[:, :]), ALU.mult))
                for b in range(B):
                    last = nc.vector.max(v8[:, b, :], pr[:, b, :])
                then(last)
                for b in range(B):
                    last = nc.vector.max_index(i8[:, b, :], v8[:, b, :], pr[:, b, :])
                then(last)
                nc.vector.tensor_copy(best[:, :, :], v8[:, :, 0:2].rearrange("p b k -> p k b"))
                then(nc.vector.tensor_copy(idx[:, :, :], i8[:, :, 0:2].rearrange("p b k -> p k b")))
                for k in range(2):
                    last = nc.vector.tensor_tensor(oh[:, k, :, :], wide(idx[:, k, :]),
                                                   m.expert_f[0:LQ, :].unsqueeze(1).to_broadcast([LQ, B, E]),
                                                   ALU.is_equal)
                then(last)
                then(nc.vector.tensor_tensor(chosen[:, :, :], oh[:, 0, :, :], oh[:, 1, :, :], ALU.add))
                src = chosen
                for i, d in enumerate((1, 2, 4, 8, 16)):
                    dst = scan[i % 2]
                    nc.vector.tensor_copy(dst[:, 0:d, :], src[:, 0:d, :])
                    then(nc.vector.tensor_tensor(dst[:, d:B, :], src[:, d:B, :], src[:, 0:B - d, :], ALU.add))
                    src = dst
                nc.vector.memset(before[:, 0, :], 0.0)
                nc.vector.tensor_copy(before[:, 1:B, :], src[:, 0:B - 1, :]).then_inc(before_done, 1)
                dve.wait_ge(counted, 1)
                for k in range(2):
                    last = nc.vector.tensor_tensor(at[:, k, :, :], oh[:, k, :, :],
                                                   pp[0:LQ, 0:B * E].rearrange("p (b e) -> p b e", e=E), ALU.mult)
                then(last)
                then(nc.vector.reduce_sum(pos[:, :, :], at[:, :, :, :], axis=X))
                nc.vector.tensor_scalar(within[:, :, :], pos[:, :, :], float(CAP), None, ALU.is_lt)
                then(nc.vector.scalar_tensor_tensor(slot[:, :, :], idx[:, :, :], float(CAP), pos[:, :, :],
                                                    ALU.mult, ALU.add))
                then(nc.vector.tensor_scalar(far[:, :, :], within[:, :, :], -1e6, 1e6, ALU.mult, ALU.add))
                nc.vector.tensor_tensor(m.scatter_at[:, :, :], slot[:, :, :], far[:, :, :], ALU.add
                                        ).then_inc(routed, 1)
                nc.vector.tensor_tensor(m.gather_at[:, :, :], slot[:, :, :], within[:, :, :], ALU.mult)
                then(nc.vector.tensor_tensor(den[:, :], best[:, 0, :], best[:, 1, :], ALU.add))
                then(nc.vector.tensor_scalar(rsum[:, :], den[:, :], 1e-9, None, ALU.add))
                then(nc.vector.reciprocal(dinv[:, :], rsum[:, :]))
                then(nc.vector.tensor_tensor(wn[:, :, :], best[:, :, :],
                                             dinv[:, :].unsqueeze(1).to_broadcast([LQ, 2, B]), ALU.mult))
                nc.vector.scalar_tensor_tensor(m.weight[:, :, :], wn[:, :, :], m.tanh[0:LQ, 1:2], within[:, :, :],
                                               ALU.mult, ALU.mult)

                def hidden(c, s, first):
                    for f in range(NF):
                        n = NF * c + f
                        dve.wait_ge(silu_done, n + 1)
                        q = (f + s) % 2
                        nc.vector.tensor_tensor(hid[s][0:FN[f], f, :], sg[q][0:FN[f], :], up[q][0:FN[f], 0:CN],
                                                ALU.mult).then_inc(hid_done, 1)

                def add(c, s, first):
                    for i in range(2):
                        dve.wait_ge(down_done, 2 * c + i + 1)
                        rows = m.x[:, bass.ds(c * CB + 2 * i, 2), :]
                        nc.vector.scalar_tensor_tensor(rows, dn[i][0:LQ, :, :], m.tanh[0:LQ, 1:2], rows,
                                                       ALU.mult, ALU.add).then_inc(added, 1)

                over_chunks(dve, hidden, add)

            @block.gpsimd
            def _(pool):
                pool.wait_ge(routed, 1)
                for b in range(B):
                    for k in range(2):
                        nc.gpsimd.indirect_dma_start(
                            out=ins["xg"], out_offset=bass.IndirectOffsetOnAxis(ap=m.scatter_at[:, k, b:b + 1], axis=0),
                            in_=m.h2[:, b, :], in_offset=None, bounds_check=E * CAP - 1, oob_is_err=False
                        ).then_inc(scattered, 16)
                pool.wait_ge(scattered, 16 * 2 * B)

            @block.scalar
            def _(act):
                act.wait_ge(r, 2)
                nc.scalar.activation(m.logits[:, :, :], pr[:, :, :], ACT.Exp).then_inc(exp_done, 1)

                def silus(c, s, first):
                    for f in range(NF):
                        n = NF * c + f
                        q = (f + s) % 2
                        act.wait_ge(gu_done, n + 1)
                        if not (isinstance(c, int) and n < 2):
                            act.wait_ge(hid_done, n - 1)
                        nc.scalar.activation(sg[q][0:FN[f], :], gp[q][0:FN[f], 0:CN], ACT.Silu).then_inc(silu_done, 1)

                over_chunks(act, silus, None)

            @block.tensor
            def _(pe):
                pe.wait_ge(w_loaded, 16 * MLP_LOADS)

                def gate_up(c, s, first):
                    for f in range(NF):
                        n = NF * c + f
                        q = (f + s) % 2
                        if not (isinstance(c, int) and n < 2):
                            pe.wait_ge(hid_done, n - 1)
                        for w, bank in ((wg, gp[q]), (wu, up[q])):
                            for k in range(KH):
                                last = nc.tensor.matmul(bank[0:FN[f], 0:CN], w[:, k, 128 * f:128 * f + FN[f]],
                                                        m.h2T[:, k, bass.ds(c * CN, CN)],
                                                        start=k == 0, stop=k == KH - 1)
                        last.then_inc(gu_done, 1)

                def down(c, s, first):
                    pe.wait_ge(hid_done, NF * (c + 1))
                    for i in range(2):
                        if not (isinstance(c, int) and c == 0):
                            pe.wait_ge(added, 2 * c + i - 1)
                        for j in range(2):
                            for f in range(NF):
                                rows = slice((2 * i + j) * LQ, (2 * i + j + 1) * LQ)
                                last = nc.tensor.matmul(dn[i][0:LQ, j, :], hid[s][0:FN[f], f, rows],
                                                        wd[0:FN[f], f, :], start=f == 0, stop=f == NF - 1)
                        last.then_inc(down_done, 1)

                pe.wait_ge(before_done, 1)
                nc.tensor.matmul(pp[0:LQ, 0:B * E], m.earlier[0:LQ, :], chosen[:, :, :], start=True, stop=False)
                nc.tensor.matmul(pp[0:LQ, 0:B * E], m.ones[0:LQ, 0:LQ], before[:, :, :], start=False, stop=True
                                 ).then_inc(counted, 1)
                over_chunks(pe, gate_up, down)


MLP_LOADS = 4


def load_mlp(sp, weights, gate, up, down, loaded):
    wg, wu, wd = weights
    sp.dma_start(wg[:, :, :], gate.rearrange("(k p) f -> p k f", p=128)).then_inc(loaded, 16)
    sp.dma_start(wu[:, :, :], up.rearrange("(k p) f -> p k f", p=128)).then_inc(loaded, 16)
    sp.dma_start(wd[:, 0:2, :], down[0:256, :].rearrange("(k p) d -> p k d", p=128)).then_inc(loaded, 16)
    sp.dma_start(wd[0:FN[2], 2, :], down[256:F, :]).then_inc(loaded, 16)


def experts(nc, ins, m):
    NF = len(FN)
    with ExitStack() as ctx:
        def sb(name, shape, dt=F32):
            return ctx.enter_context(nc.sbuf_tensor(name, shape, dt))

        def pair(name, shape, dt=F32):
            return [sb(f"{name}{s}", shape, dt) for s in range(2)]

        def sem(name):
            return ctx.enter_context(nc.semaphore(name))

        w = [mlp_weights(nc, ctx, f"expert{s}") for s in range(2)]
        rows = pair("rows", [RN, RT, D])
        xT = pair("rows_T", [128, KH, CAP])
        sg = pair("expert_silu", [128, CAP])
        hid = pair("expert_hidden", [128, NF, CAP])
        y = pair("y", [RN, RT, D])
        gp = [ctx.enter_context(nc.psum_tensor(f"expert_gate_psum{s}", [128, 512], F32)) for s in range(2)]
        up = [ctx.enter_context(nc.psum_tensor(f"expert_up_psum{s}", [128, 512], F32)) for s in range(2)]
        dn = [ctx.enter_context(nc.psum_tensor(f"expert_down_psum{s}", [128, 2, D], F32)) for s in range(2)]
        tp = [ctx.enter_context(nc.psum_tensor(f"rowsT_psum{k}", [128, 512], F32)) for k in range(KH)]

        loaded = [sem(f"weights_loaded{s}") for s in range(2)]
        rows_loaded = [sem(f"rows_loaded{s}") for s in range(2)]
        stored = [sem(f"y_stored{s}") for s in range(2)]
        t_done, t_emptied = sem("rows_t_done"), sem("rows_t_emptied")
        gu_done, silu_done, hid_done = sem("expert_gate_up_done"), sem("expert_silu_done"), sem("expert_hidden_done")
        down_done, y_done = sem("expert_down_done"), [sem(f"y_done{i}") for i in range(2)]

        def over_experts(eng, step):
            for e in range(2):
                step(e, e, 0)
            with eng.Fori(1, E // 2) as it:
                for s in range(2):
                    step(it * 2 + s, s, it)

        def new(use):
            return isinstance(use, int)

        with nc.Block() as block:

            @block.sync
            def _(sp):
                def store(e, s, use):
                    sp.wait_ge(y_done[0], e + 1)
                    sp.wait_ge(y_done[1], e + 1)
                    sp.dma_start(ins["yg"][bass.ds(e * CAP, CAP), :].rearrange("(p t) d -> p t d", t=RT),
                                 y[s][:, :, :]).then_inc(stored[s], 16)

                def load(e, s, use):
                    if not new(use):
                        store(e - 2, s, use - 1)
                        sp.wait_ge(t_done, e - 1)
                        sp.wait_ge(down_done, 2 * e - 2)
                    sp.dma_start(rows[s][:, :, :],
                                 ins["xg"][bass.ds(e * CAP, CAP), :].rearrange("(p t) d -> p t d", t=RT)
                                 ).then_inc(rows_loaded[s], 16)
                    load_mlp(sp, w[s], ins["w_gate"][bass.ds(e, 1), :, :].rearrange("o d f -> (o d) f"),
                             ins["w_up"][bass.ds(e, 1), :, :].rearrange("o d f -> (o d) f"),
                             ins["w_down"][bass.ds(e, 1), :, :].rearrange("o f d -> (o f) d"), loaded[s])

                over_experts(sp, load)
                for s in range(2):
                    store(E - 2 + s, s, E // 2 - 1)
                for s in range(2):
                    sp.wait_ge(stored[s], 16 * (E // 2))

            @block.tensor
            def _(pe):
                def transposes(e, s, use):
                    pe.wait_ge(rows_loaded[s], use * 16 + 16)
                    for k in range(KH):
                        if not (isinstance(e, int) and e == 0):
                            pe.wait_ge(t_emptied, 2 * e - 1 + k)
                        for t in range(RT):
                            last = nc.tensor.transpose(tp[k][:, t * RN:(t + 1) * RN],
                                                       rows[s][:, t, k * 128:(k + 1) * 128], m.ident[0:RN, 0:RN])
                        last.then_inc(t_done, 1)

                def gate_up(e, s, use):
                    pe.wait_ge(loaded[s], use * (16 * MLP_LOADS) + 16 * MLP_LOADS)
                    pe.wait_ge(t_emptied, 2 * e + 2)
                    for f in range(NF):
                        n = NF * e + f
                        q = (f + s) % 2
                        if not (isinstance(e, int) and n < 2):
                            pe.wait_ge(hid_done, n - 1)
                        for wt, bank in ((w[s][0], gp[q]), (w[s][1], up[q])):
                            for k in range(KH):
                                last = nc.tensor.matmul(bank[0:FN[f], 0:CAP], wt[:, k, 128 * f:128 * f + FN[f]],
                                                        xT[s][:, k, :], start=k == 0, stop=k == KH - 1)
                        last.then_inc(gu_done, 1)

                def down(e, s):
                    pe.wait_ge(hid_done, NF * e + NF)
                    for i in range(2):
                        if not (isinstance(e, int) and e == 0):
                            pe.wait_ge(y_done[i], e)
                        for j in range(2):
                            t = 2 * i + j
                            for f in range(NF):
                                last = nc.tensor.matmul(dn[i][0:RN, j, :], hid[s][0:FN[f], f, t * RN:(t + 1) * RN],
                                                        w[s][2][0:FN[f], f, :], start=f == 0, stop=f == NF - 1)
                        last.then_inc(down_done, 1)

                def step(e, s, use):
                    transposes(e, s, use)
                    if not (isinstance(e, int) and e == 0):
                        down(e - 1, 1 - s)
                    gate_up(e, s, use)

                over_experts(pe, step)
                down(E - 1, 1)

            @block.scalar
            def _(act):
                def step(e, s, use):
                    for k in range(KH):
                        act.wait_ge(t_done, 2 * e + k + 1)
                        if not new(use):
                            act.wait_ge(gu_done, NF * e - NF)
                        nc.scalar.activation(xT[s][:, k, :], tp[k][:, 0:CAP], ACT.Copy).then_inc(t_emptied, 1)
                    for f in range(NF):
                        n = NF * e + f
                        q = (f + s) % 2
                        act.wait_ge(gu_done, n + 1)
                        if not (isinstance(e, int) and n < 2):
                            act.wait_ge(hid_done, n - 1)
                        nc.scalar.activation(sg[q][0:FN[f], :], gp[q][0:FN[f], 0:CAP], ACT.Silu).then_inc(silu_done, 1)

                over_experts(act, step)

            @block.vector
            def _(dve):
                def take_y(e, s, use):
                    for i in range(2):
                        dve.wait_ge(down_done, 2 * e + i + 1)
                        if not (isinstance(e, int) and e < 2):
                            dve.wait_ge(stored[s], 16 * use)
                        nc.vector.tensor_copy(y[s][:, 2 * i:2 * i + 2, :], dn[i][0:RN, :, :]).then_inc(y_done[i], 1)

                def step(e, s, use):
                    if not (isinstance(e, int) and e == 0):
                        take_y(e - 1, 1 - s, use if s else use - 1)
                    for f in range(NF):
                        n = NF * e + f
                        q = (f + s) % 2
                        dve.wait_ge(silu_done, n + 1)
                        if not new(use) and f == 0:
                            dve.wait_ge(down_done, 2 * e - 2)
                        nc.vector.tensor_tensor(hid[s][0:FN[f], f, :], sg[q][0:FN[f], :], up[q][0:FN[f], 0:CAP],
                                                ALU.mult).then_inc(hid_done, 1)

                over_experts(dve, step)
                take_y(E - 1, 1, E // 2 - 1)


def combine(nc, ins, m, out):
    with ExitStack() as ctx:
        def sem(name):
            return ctx.enter_context(nc.semaphore(name))

        BUFS = 8
        yb = [ctx.enter_context(nc.sbuf_tensor(f"gathered{i}", [LQ, 2, D], F32)) for i in range(BUFS)]
        gathered = [sem(f"gathered{i}") for i in range(BUFS)]
        first_added, added, stored = sem("first_added"), sem("both_added"), sem("out_stored")
        with nc.Block() as block:

            @block.gpsimd
            def _(pool):
                for b in range(B):
                    i = b % BUFS
                    if b >= BUFS:
                        pool.wait_ge(added, b - BUFS + 1)
                    for k in range(2):
                        nc.gpsimd.indirect_dma_start(
                            out=yb[i][:, k, :], out_offset=None, in_=ins["yg"],
                            in_offset=bass.IndirectOffsetOnAxis(ap=m.gather_at[:, k, b:b + 1], axis=0),
                            bounds_check=E * CAP - 1, oob_is_err=False).then_inc(gathered[i], 16)

            @block.vector
            def _(dve):
                for b in range(B):
                    i = b % BUFS
                    dve.wait_ge(gathered[i], 32 * (b // BUFS + 1))
                    nc.vector.scalar_tensor_tensor(m.x[:, b, :], yb[i][:, 0, :], m.weight[:, 0, b:b + 1],
                                                   m.x[:, b, :], ALU.mult, ALU.add).then_inc(first_added, 1)
                    dve.wait_ge(first_added, b + 1)
                    nc.vector.scalar_tensor_tensor(m.x[:, b, :], yb[i][:, 1, :], m.weight[:, 1, b:b + 1],
                                                   m.x[:, b, :], ALU.mult, ALU.add).then_inc(added, 1)

            @block.sync
            def _(sp):
                for c in range(NC):
                    sp.wait_ge(added, (c + 1) * CB)
                    sp.dma_start(out[c * CB:(c + 1) * CB, :, :].rearrange("b t d -> t b d"),
                                 m.x[:, c * CB:(c + 1) * CB, :]).then_inc(stored, 16)
                sp.wait_ge(stored, 16 * NC)


def build(nc, ins, out):
    with ExitStack() as ctx:
        def sb(name, shape, dt=F32):
            return ctx.enter_context(nc.sbuf_tensor(name, shape, dt))

        m = Memory()
        m.x = sb("x", [LQ, B, D])
        m.h2 = sb("h2", [LQ, B, D])
        m.h2T = sb("h2T", [128, KH, B * LQ])
        m.logits = sb("logits", [LQ, B, E])
        m.wq, m.wk, m.wv, m.wo = (sb(n, [128, KH, D]) for n in ("wq", "wk", "wv", "wo"))
        m.gb_pre = sb("gain_offset_pre", [128, 2, KH])
        m.g_ln, m.b_ln = sb("gain_ln", [LQ, D]), sb("offset_ln", [LQ, D])
        m.wr, m.br = sb("router_w", [128, KH, E]), sb("router_b", [E, 1])
        m.gates, m.tanh = sb("gates", [128, 2]), sb("tanh_gates", [128, 2])
        m.ident, m.ident_b = sb("ident", [128, 128]), sb("ident_bf", [128, 128], BF16)
        m.headmask, m.headmask_b = sb("headmask", [128, HH]), sb("headmask_bf", [128, HH], BF16)
        m.side = sb("side", [128, 2])
        m.earlier = sb("earlier", [LQ, LQ])
        m.expert_u, m.expert_f = sb("expert_ids", [128, E], U32), sb("expert_ids_f", [128, E])
        m.ones, m.ones_b = sb("ones", [128, 128]), sb("ones_bf", [128, 128], BF16)
        m.inside = sb("inside_clip", [1, 1], U32)
        m.minus_half, m.eps = sb("minus_half", [128, 8]), sb("eps", [128, 8])
        m.mv = [sb(f"mean_var{s}", [128, KT + 1, 2]) for s in range(2)]
        m.zeros = sb("zeros", [128, RT * D])
        m.scatter_at, m.gather_at = sb("scatter_at", [LQ, 2, B], U32), sb("gather_at", [LQ, 2, B], U32)
        m.weight = sb("expert_weight", [LQ, 2, B])

        setup(nc, ins, m)
        attention(nc, ins, m)
        output_projection(nc, ins, m)
        tokens_and_logits(nc, ins, m)
        route_and_shared(nc, ins, m)
        experts(nc, ins, m)
        combine(nc, ins, m, out)


def kernel(**inputs):
    import numpy as np
    import concourse.bacc as bacc
    from concourse.bass_utils import run_bass_kernel_spmd

    nc = bacc.Bacc("TRN2", target_bir_lowering=False, num_devices=1)
    given = {
        "x": inputs["x"], "ctx": inputs["ctx_1024"], "g_xattn": inputs["g_xattn"], "g_ffn": inputs["g_ffn"],
        "g_pre": np.asarray(inputs["L0_xattn_g_pre"]).reshape(KH, 128).T,
        "b_pre": np.asarray(inputs["L0_xattn_b_pre"]).reshape(KH, 128).T,
        "g_ln": inputs["L0_xattn_g_ln"], "b_ln": inputs["L0_xattn_b_ln"],
        "wqT": np.asarray(inputs["L0_xattn_Wq"]).T, "wkT": np.asarray(inputs["L0_xattn_Wk"]).T,
        "wvT": np.asarray(inputs["L0_xattn_Wv"]).T, "woT": np.asarray(inputs["L0_xattn_Wo"]).T,
        "router_w": inputs["L0_ffn_router_w"], "router_b": inputs["L0_ffn_router_b"],
        "w_gate": inputs["L0_ffn_w_gate"], "w_up": inputs["L0_ffn_w_up"], "w_down": inputs["L0_ffn_w_down"],
        "sw_gate": inputs["L0_ffn_sw_gate"], "sw_up": inputs["L0_ffn_sw_up"], "sw_down": inputs["L0_ffn_sw_down"],
    }
    arrays, aps = {}, {}
    for name, a in given.items():
        a = np.ascontiguousarray(a)
        arrays[f"in_{name}"] = a
        aps[name] = nc.dram_tensor(f"in_{name}", a.shape, mybir.dt.from_np(a.dtype), kind="ExternalInput").ap()
    aps["xg"] = nc.dram_tensor("expert_rows", (E * CAP, D), F32, kind="Internal").ap()
    aps["yg"] = nc.dram_tensor("expert_outputs", (E * CAP, D), F32, kind="Internal").ap()
    out = nc.dram_tensor("out", (B, LQ, D), F32, kind="ExternalOutput").ap()
    build(nc, aps, out)
    return run_bass_kernel_spmd(nc, [arrays], core_ids=[0]).results[0]["out"]
```

```python
import concourse.bass as bass
from concourse import mybir
from contextlib import ExitStack

F32 = mybir.dt.float32
BF16 = mybir.dt.bfloat16
U32 = mybir.dt.uint32
ALU = mybir.AluOpType
ACT = mybir.ActivationFunctionType
X = mybir.AxisListType.X

B, LQ, LK, D = 32, 100, 361, 256
H, DH = 16, 16
KH = D // 128
HH = H // KH
KT = 3
KN = [121, 120, 120]
KOFF = [0, 121, 241]
EPS = 1e-5
TEMP = 16.0
CLIP = 10000.0 * TEMP
BOUND = 0.99 * CLIP
SHARE = 8
E, F, CAP = 16, 352, 500
FN = [128, 128, 96]
RT, RN = 4, 125
CB = 4
CN = CB * LQ
NC = B // CB


class Memory:
    pass


def setup(nc, ins, m):
    loads = [
        (m.x[:, :, :], ins["x"].rearrange("b t d -> t b d")),
        (m.wq[:, :, :], ins["wqT"].rearrange("(k p) n -> p k n", p=128)),
        (m.wk[:, :, :], ins["wkT"].rearrange("(k p) n -> p k n", p=128)),
        (m.wv[:, :, :], ins["wvT"].rearrange("(k p) n -> p k n", p=128)),
        (m.wo[:, :, :], ins["woT"].rearrange("(k p) n -> p k n", p=128)),
        (m.gb_pre[:, 0, :], ins["g_pre"]),
        (m.gb_pre[:, 1, :], ins["b_pre"]),
        (m.g_ln[:, :], ins["g_ln"].partition_broadcast(LQ)),
        (m.b_ln[:, :], ins["b_ln"].partition_broadcast(LQ)),
        (m.wr[:, :, :], ins["router_w"].rearrange("(k p) n -> p k n", p=128)),
        (m.br[:, :], ins["router_b"].rearrange("(p o) -> p o", o=1)),
        (m.gates[:, 0:1], ins["g_xattn"].partition_broadcast(128)),
        (m.gates[:, 1:2], ins["g_ffn"].partition_broadcast(128)),
    ]
    with ExitStack() as ctx:
        def sb(name, shape, dt=F32):
            return ctx.enter_context(nc.sbuf_tensor(name, shape, dt))

        def sem(name):
            return ctx.enter_context(nc.semaphore(name))

        loaded, made, masks, zeroed = sem("loaded"), sem("made"), sem("masks"), sem("zeroed")
        squared, summed, bound_step = sem("squared"), sem("summed"), sem("bound_step")
        wgain = [sb(f"weight_gain_{n}", [128, KH, D]) for n in "qk"]
        wsq = [sb(f"weight_square_{n}", [128, KH, D]) for n in "qk"]
        norm2 = sb("row_norm2", [1, 2 * D])
        off = sb("row_offset", [1, 2 * D])
        off2 = sb("row_offset2", [1, 2 * D])
        size2 = sb("row_bound2", [1, 2 * D])
        heads = sb("head_sums", [1, 2, H])
        prod = sb("head_bounds", [1, H])
        largest = sb("largest_bound", [1, 1])
        inside = sb("inside_bound", [1, 1])
        np_ = ctx.enter_context(nc.psum_tensor("row_norm_psum", [128, 512], F32))
        op_ = ctx.enter_context(nc.psum_tensor("row_offset_psum", [128, 512], F32))
        block = ctx.enter_context(nc.Block())

        @block.sync
        def _(sp):
            for dst, src in loads:
                sp.dma_start(dst, src).then_inc(loaded, 16)
            sp.wait_ge(loaded, 16 * len(loads))

        @block.gpsimd
        def _(pool):
            nc.gpsimd.memset(m.ident[:, :], 0.0).then_inc(made, 1)
            nc.gpsimd.memset(m.headmask[:, :], 1.0).then_inc(made, 1)
            nc.gpsimd.memset(m.earlier[:, :], 1.0).then_inc(made, 1)
            nc.gpsimd.iota(m.expert_u[:, :], pattern=[[1, E]], base=0, channel_multiplier=0).then_inc(made, 1)
            pool.wait_ge(made, 4)
            nc.gpsimd.affine_select(out=m.ident[:, :], in_=m.ident[:, :], compare_op=ALU.not_equal, fill=1.0,
                                    base=0, pattern=[[-1, 128]], channel_multiplier=1).then_inc(masks, 1)
            nc.gpsimd.affine_select(out=m.headmask[:, :], in_=m.headmask[:, :], compare_op=ALU.is_ge, fill=0.0,
                                    base=0, pattern=[[-DH, HH]], channel_multiplier=1).then_inc(masks, 1)
            nc.gpsimd.affine_select(out=m.earlier[:, :], in_=m.earlier[:, :], compare_op=ALU.is_ge, fill=0.0,
                                    base=-1, pattern=[[1, LQ]], channel_multiplier=-1).then_inc(masks, 1)
            pool.wait_ge(masks, 3)
            nc.gpsimd.affine_select(out=m.headmask[:, :], in_=m.headmask[:, :], compare_op=ALU.is_ge, fill=0.0,
                                    base=DH - 1, pattern=[[DH, HH]], channel_multiplier=-1).then_inc(masks, 1)

        @block.vector
        def _(dve):
            nc.vector.memset(m.ones[:, :], 1.0)
            nc.vector.memset(m.ones_b[:, :], 1.0)
            nc.vector.memset(m.minus_half[:, :], -0.5)
            nc.vector.memset(m.eps[:, :], EPS)
            for s in range(2):
                nc.vector.memset(m.mv[s][:, :, :], 1.0)
            nc.vector.memset(m.zeros[:, :], 0.0).then_inc(zeroed, 1)
            dve.wait_ge(masks, 4)
            nc.vector.reduce_sum(m.side[:, 0:1], m.headmask[:, 0:HH:2], axis=X)
            nc.vector.reduce_sum(m.side[:, 1:2], m.headmask[:, 1:HH:2], axis=X)
            nc.vector.tensor_copy(m.ident_b[:, :], m.ident[:, :])
            nc.vector.tensor_copy(m.headmask_b[:, :], m.headmask[:, :])
            nc.vector.tensor_copy(m.expert_f[:, :], m.expert_u[:, :])
            dve.wait_ge(loaded, 16 * len(loads))
            for i, w in enumerate((m.wq, m.wk)):
                for k in range(KH):
                    last = nc.vector.tensor_scalar(wgain[i][:, k, :], w[:, k, :], m.gb_pre[:, 0, k:k + 1], None,
                                                   ALU.mult)
            last.then_inc(squared, 1)
            dve.wait_ge(squared, 1)
            for i in range(2):
                last = nc.vector.tensor_tensor(wsq[i][:, :, :], wgain[i][:, :, :], wgain[i][:, :, :], ALU.mult)
            last.then_inc(squared, 1)
            dve.wait_ge(summed, 1)
            nc.vector.tensor_scalar(off[:, :], op_[0:1, :], 1.0, None, ALU.mult)
            nc.vector.tensor_scalar(norm2[:, :], np_[0:1, :], (1 + 1 / SHARE) * D, None, ALU.mult
                                    ).then_inc(bound_step, 1)
            dve.wait_ge(bound_step, 1)
            nc.vector.tensor_tensor(off2[:, :], off[:, :], off[:, :], ALU.mult).then_inc(bound_step, 1)
            dve.wait_ge(bound_step, 2)
            nc.vector.scalar_tensor_tensor(size2[:, :], off2[:, :], 1.0 + SHARE, norm2[:, :], ALU.mult, ALU.add
                                           ).then_inc(bound_step, 1)
            dve.wait_ge(bound_step, 3)
            nc.vector.reduce_sum(heads[:, :, :], size2[:, :].rearrange("p (w h d) -> p w h d", w=2, d=DH), axis=X
                                 ).then_inc(bound_step, 1)
            dve.wait_ge(bound_step, 4)
            nc.vector.tensor_tensor(prod[:, :], heads[:, 0, :], heads[:, 1, :], ALU.mult).then_inc(bound_step, 1)
            dve.wait_ge(bound_step, 5)
            nc.vector.reduce_max(largest[:, :], prod[:, :], axis=X).then_inc(bound_step, 1)
            dve.wait_ge(bound_step, 6)
            nc.vector.tensor_scalar(inside[:, :], largest[:, :], BOUND * BOUND, None, ALU.is_lt).then_inc(bound_step, 1)
            dve.wait_ge(bound_step, 7)
            nc.vector.tensor_copy(m.inside[:, :], inside[:, :])

        @block.tensor
        def _(pe):
            pe.wait_ge(squared, 2)
            for i, w in enumerate((m.wq, m.wk)):
                cols = slice(i * D, (i + 1) * D)
                for k in range(KH):
                    nc.tensor.matmul(np_[0:1, cols], m.ones[:, 0:1], wsq[i][:, k, :], start=k == 0, stop=k == KH - 1)
                for k in range(KH):
                    last = nc.tensor.matmul(op_[0:1, cols], m.gb_pre[:, 1, k:k + 1], w[:, k, :],
                                            start=k == 0, stop=k == KH - 1)
            last.then_inc(summed, 1)

        @block.scalar
        def _(act):
            act.wait_ge(loaded, 16 * len(loads))
            nc.scalar.activation(m.tanh[:, :], m.gates[:, :], ACT.Tanh)


def attention(nc, ins, m):
    OT, OP = 24, 27
    RING = 10 + H + 2
    with ExitStack() as ctx:
        def sb(name, shape, dt=F32):
            return ctx.enter_context(nc.sbuf_tensor(name, shape, dt))

        def pair(name, shape, dt=F32):
            return [sb(f"{name}{s}", shape, dt) for s in range(2)]

        def sem(name):
            return ctx.enter_context(nc.semaphore(name))

        raw = pair("ctx_raw", [128, KT, D])
        norm = pair("ctx_norm", [128, KT, D])
        zq = pair("x_norm", [LQ, D])
        st = pair("stats", [128, KT + 1, 6])
        st2 = pair("stats2", [LQ, 6])
        mv2 = pair("mean_var2", [LQ, 2])
        var = pair("var_eps", [128, KT + 1])
        rs = pair("rstd", [128, KT + 1])
        shift = pair("minus_mean_rstd", [128, KT])
        z1 = sb("x_once_normed", [LQ, D])
        var2 = pair("var_eps2", [LQ, 1])
        rs2 = pair("rstd2", [LQ, 1])
        qnT = sb("qnT", [128, KH, LQ])
        knT = sb("knT", [128, KH, LK])
        cT = sb("cT", [128, KH, LK])
        qh = sb("q_hi", [128, KH, LQ], BF16)
        ql = sb("q_lo", [128, KH, LQ], BF16)
        kh = pair("k_hi", [128, KH, LK], BF16)
        kl = pair("k_lo", [128, KH, LK], BF16)
        v = pair("v", [128, KT, D])
        qbh = pair("q_block_hi", [128, KH, HH, LQ], BF16)
        qbl = pair("q_block_lo", [128, KH, HH, LQ], BF16)
        mx = pair("score_max", [LQ, H])
        mxn = pair("minus_max", [LQ, H])
        mneg = pair("minus_max_bf", [LQ, H], BF16)
        mdiag = pair("minus_max_diag", [LQ, H, LQ], BF16)
        probs = pair("probs", [128, HH, LQ])
        dsel0 = sb("den_first", [128, KH, LQ])
        dsel = sb("den", [128, KH, LQ])
        osel0 = sb("o_first", [128, KH, LQ])
        osel = sb("o_sum", [128, KH, LQ])
        rden = sb("den_inv", [128, KH, LQ])
        onT = sb("oT", [128, KH, LQ])
        oraw = pair("o_raw", [LQ, D])
        ost = pair("o_stats", [LQ, 6])
        omv = pair("o_mean_var", [LQ, 2])
        ovar = pair("o_var_eps", [LQ, 1])
        ors = pair("o_rstd", [LQ, 1])
        oz = sb("o_norm", [LQ, D])
        og = sb("o_gained", [LQ, D])
        ol = pair("o_ln", [LQ, D])
        olT = sb("o_lnT", [128, KH, LQ])
        carrier_p, carrier_v = sb("carrier_pool", [1, 1]), sb("carrier_vector", [1, 1])

        scores = ctx.enter_context(nc.psum_tensor("scores", [128, 4, 512], F32))
        ring = [ctx.enter_context(nc.psum_tensor(f"ring{s}", [128, 512], F32)) for s in range(2)]
        ob = ctx.enter_context(nc.psum_tensor("o_bank", [128, 512], F32))
        db = ctx.enter_context(nc.psum_tensor("den_bank", [128, 512], F32))

        raw_loaded = [sem(f"raw_loaded{s}") for s in range(2)]
        xg_zeroed = sem("xg_zeroed")
        bn_done = sem("bn_done")
        stats_done = sem("stats_done")
        rstd_step = sem("rstd_step")
        shift_done = sem("shift_done")
        z1_done = sem("z1_done")
        norm_done = sem("norm_done")
        bn2_done = sem("bn2_done")
        stats2_done = sem("stats2_done")
        rstd2_step = sem("rstd2_step")
        z2_done = sem("z2_done")
        filled = [sem(f"ring_filled{s}") for s in range(2)]
        emptied = [sem(f"ring_emptied{s}") for s in range(2)]
        qh_done = sem("qh_done")
        qb_done = sem("q_block_done")
        kh_done = sem("kh_done")
        max_clipped = sem("max_clipped")
        mneg_done = sem("mneg_done")
        mdiag_done = sem("mdiag_done")
        raw_done = sem("raw_scores_done")
        clipped = sem("scores_clipped")
        scores_done = sem("scores_done")
        exp_done = sem("exp_done")
        pv_done = sem("pv_done")
        fin_step = sem("fin_step")
        on_done = sem("on_done")
        ot_done = sem("ot_done")
        ot_emptied = sem("ot_emptied")
        obn_done = sem("o_bn_done")
        ostats_done = sem("o_stats_done")
        orstd_step = sem("o_rstd_step")
        oln_step = sem("o_ln_step")
        ol_done = sem("o_ln_done")
        ol_kept = sem("o_ln_kept")

        def nth(r, pos):
            if isinstance(r, int) and r < 2:
                return (RING // 2 - 1) * r + pos // 2 + 1 - (pos > OT and pos % 2 == OT % 2)
            if isinstance(r, int) and r >= B:
                return (RING // 2) * B - 2 + (r - B) + 1
            return (RING // 2) * r - 2 + pos // 2 + 1

        BETWEEN = [("score", 3, 2), ("score", 3, 3), ("sum", 2, 0), ("sum", 2, 1),
                   ("score", 4, 0), ("score", 4, 1), ("score", 4, 2), ("score", 4, 3), ("sum", 3, 0), ("sum", 3, 1),
                   ("score", 5, 0), ("score", 5, 1), ("score", 5, 2), ("score", 5, 3), ("sum", 4, 0), ("sum", 4, 1),
                   ("sum", 5, 0), ("sum", 5, 1)]
        CLIP_AT = {i + 1 - (i + 11 > OT): u for i, (kind, u, part) in enumerate(BETWEEN)
                   if kind == "score" and part == 3}

        def at(h):
            return 10 + h + (10 + h >= OT)

        def over_batches(eng, step):
            step(-1, 1, False, False, True, False)
            step(0, 0, False, True, True, True)
            step(1, 1, True, True, True, True)
            with eng.Fori(1, B // 2 - 1) as it:
                for s in range(2):
                    step(it * 2 + s, s, True, True, True, True)
            step(B - 2, 0, True, True, True, False)
            step(B - 1, 1, True, True, False, False)
            step(B, 0, True, False, False, False)

        def either(eng, program):
            inside = eng.value_load(m.inside[0:1, 0:1], min_val=0, max_val=1)
            with eng.If(inside > 0):
                program(False)
            with eng.Else():
                program(True)

        with nc.Block() as block:

            @block.sync
            def _(sp):
                def load(b, s, use):
                    sp.dma_start(raw[s][0:120, :, :],
                                 ins["ctx"][bass.ds(b, 1), 0:360, :].rearrange("o (p t) d -> p (o t) d", t=KT)
                                 ).then_inc(raw_loaded[s], 16)
                    sp.dma_start(raw[s][120:121, 0, :],
                                 ins["ctx"][bass.ds(b, 1), 360:361, :].rearrange("o p d -> p (o d)")
                                 ).then_inc(raw_loaded[s], 16)

                load(0, 0, 0)
                load(1, 1, 0)
                for e in range(E):
                    sp.dma_start(ins["xg"][e * CAP:(e + 1) * CAP, :].rearrange("(p t) d -> p (t d)", t=RT),
                                 m.zeros[0:RN, :]).then_inc(xg_zeroed, 16)
                for b in range(2, 4):
                    sp.wait_ge(filled[1], nth(b - 2, 5))
                    load(b, b % 2, 1)
                with sp.Fori(2, B // 2) as it:
                    for s in range(2):
                        sp.wait_ge(filled[1], nth(it * 2 + s - 2, 5))
                        load(it * 2 + s, s, it)
                sp.wait_ge(xg_zeroed, 16 * E)

            @block.gpsimd
            def _(pool):
                def rstd(b, s):
                    pool.wait_ge(stats_done, b + 1)
                    nc.gpsimd.tensor_tensor(var[s][:, :], m.mv[s][:, :, 1], m.eps[:, 0:KT + 1], ALU.add
                                            ).then_inc(rstd_step, 1)
                    pool.wait_ge(rstd_step, 2 * b + 1)
                    nc.gpsimd.tensor_tensor(rs[s][:, :], var[s][:, :], m.minus_half[:, 0:KT + 1],
                                            ALU.pow).then_inc(rstd_step, 1)

                def rstd_again(b, s):
                    pool.wait_ge(stats2_done, b + 1)
                    nc.gpsimd.tensor_tensor(var2[s][:, :], mv2[s][:, 1:2], m.eps[0:LQ, 0:1], ALU.add
                                            ).then_inc(rstd2_step, 1)
                    pool.wait_ge(rstd2_step, 2 * b + 1)
                    nc.gpsimd.tensor_tensor(rs2[s][:, :], var2[s][:, :], m.minus_half[0:LQ, 0:1],
                                            ALU.pow).then_inc(rstd2_step, 1)

                def q_blocks(b, s, src, dst):
                    if src is qh:
                        pool.wait_ge(qh_done, b + 1)
                    else:
                        pool.wait_ge(emptied[1], nth(b, 3))
                    for k in range(KH):
                        last = nc.gpsimd.tensor_tensor(
                            dst[:, k, :, :], src[:, k, :].unsqueeze(1).to_broadcast([128, HH, LQ]),
                            m.headmask_b[:, :].unsqueeze(2).to_broadcast([128, HH, LQ]), ALU.mult)
                    last.then_inc(qb_done, 1)

                def max_diagonal(b, s, k):
                    pool.wait_ge(mneg_done, 2 * b + k + 1)
                    nc.gpsimd.tensor_tensor(
                        mdiag[s][:, HH * k:HH * (k + 1), :],
                        mneg[s][:, HH * k:HH * (k + 1)].unsqueeze(2).to_broadcast([LQ, HH, LQ]),
                        m.ident_b[0:LQ, 0:LQ].unsqueeze(1).to_broadcast([LQ, HH, LQ]),
                        ALU.mult).then_inc(mdiag_done, 1)

                def o_rstd(b, s):
                    pool.wait_ge(ostats_done, b + 1)
                    nc.gpsimd.tensor_tensor(ovar[s][:, :], omv[s][:, 1:2], m.eps[0:LQ, 0:1], ALU.add
                                            ).then_inc(orstd_step, 1)
                    pool.wait_ge(orstd_step, 2 * b + 1)
                    nc.gpsimd.tensor_tensor(ors[s][:, :], ovar[s][:, :], m.minus_half[0:LQ, 0:1],
                                            ALU.pow).then_inc(orstd_step, 1)

                def step(b, s, prev, this, following, after):
                    if following:
                        q_blocks(b + 1, 1 - s, qh, qbh[1 - s])
                    if prev:
                        o_rstd(b - 1, 1 - s)
                    if after:
                        rstd(b + 2, s)
                    if following:
                        q_blocks(b + 1, 1 - s, ql, qbl[1 - s])
                    if after:
                        rstd_again(b + 2, s)
                    if following:
                        for k in range(KH):
                            max_diagonal(b + 1, 1 - s, k)

                for b in range(2):
                    rstd(b, b)
                    rstd_again(b, b)
                over_batches(pool, step)

            @block.vector
            def _(dve):
                def after_wait(semaphore, count):
                    dve.wait_ge(semaphore, count)
                    nc.vector.memset(carrier_v[:, :], 0.0)

                def statistics(b, s, use):
                    dve.wait_ge(raw_loaded[s], 32 * (use + 1))
                    for t in range(KT):
                        nc.vector.bn_stats(st[s][0:KN[t], t, :], raw[s][0:KN[t], t, :])
                    nc.vector.bn_stats(st[s][0:LQ, KT, :], m.x[:, bass.ds(b, 1), :].rearrange("p o d -> p (o d)")
                                       ).then_inc(bn_done, 1)
                    after_wait(bn_done, b + 1)
                    for t in range(KT):
                        nc.vector.bn_aggr(m.mv[s][0:KN[t], t, :], st[s][0:KN[t], t, :])
                    nc.vector.bn_aggr(m.mv[s][0:LQ, KT, :], st[s][0:LQ, KT, :]).then_inc(stats_done, 1)

                def statistics_again(b, s):
                    dve.wait_ge(rstd_step, 2 * b + 2)
                    nc.vector.scalar_tensor_tensor(shift[s][:, :], m.mv[s][:, 0:KT, 0], -1.0, rs[s][:, 0:KT],
                                                   ALU.mult, ALU.mult).then_inc(shift_done, 1)
                    nc.vector.tensor_scalar(z1[:, :], m.x[:, bass.ds(b, 1), :].rearrange("p o d -> p (o d)"),
                                            m.mv[s][0:LQ, KT, 0:1], rs[s][0:LQ, KT:KT + 1],
                                            ALU.subtract, ALU.mult).then_inc(z1_done, 1)
                    dve.wait_ge(z1_done, b + 1)
                    nc.vector.bn_stats(st2[s][:, :], z1[:, :]).then_inc(bn2_done, 1)
                    after_wait(bn2_done, b + 1)
                    nc.vector.bn_aggr(mv2[s][:, :], st2[s][:, :]).then_inc(stats2_done, 1)

                def normalise_again(b, s):
                    dve.wait_ge(rstd2_step, 2 * b + 2)
                    nc.vector.tensor_scalar(zq[s][:, :], z1[:, :], mv2[s][:, 0:1], rs2[s][:, :],
                                            ALU.subtract, ALU.mult).then_inc(z2_done, 1)

                def affine(b, pos, dst, n, halves):
                    dve.wait_ge(filled[pos % 2], nth(b, pos))
                    for i, k in enumerate(halves):
                        last = nc.vector.tensor_scalar(dst[:, k, :], ring[pos % 2][:, i * n:(i + 1) * n],
                                                       m.gb_pre[:, 0, k:k + 1], m.gb_pre[:, 1, k:k + 1],
                                                       ALU.mult, ALU.add)
                    last.then_inc(emptied[pos % 2], 1)

                def low_part(b, pos, dst, hi, n, hi_done, count):
                    dve.wait_ge(filled[pos % 2], nth(b, pos))
                    dve.wait_ge(hi_done, count)
                    nc.vector.tensor_tensor(dst, ring[pos % 2][:, 0:n], hi, ALU.subtract).then_inc(emptied[pos % 2], 1)

                def clip(b, u):
                    k, t = u // KT, u % KT
                    dve.wait_ge(raw_done, 6 * b + u + 1)
                    bank = scores[0:KN[t], 2 * (u % 2):2 * (u % 2) + 2, 0:4 * LQ]
                    nc.vector.tensor_scalar(bank, bank, CLIP, -CLIP, ALU.min, ALU.max).then_inc(clipped, 1)

                def maxima(b, s, k, clips):
                    for h in range(HH * k, HH * (k + 1)):
                        if clips is not None and h in CLIP_AT:
                            clip(clips, CLIP_AT[h])
                        pos = at(h)
                        dve.wait_ge(filled[pos % 2], nth(b, pos))
                        nc.vector.reduce_max(mx[s][:, h:h + 1], ring[pos % 2][0:LQ, 0:LK], axis=X
                                             ).then_inc(emptied[pos % 2], 1)
                    half = slice(HH * k, HH * (k + 1))
                    last2 = [at(HH * (k + 1) - 2), at(HH * (k + 1) - 1)]
                    for pos in last2:
                        dve.wait_ge(emptied[pos % 2], nth(b, pos))
                    nc.vector.tensor_scalar(mxn[s][:, half], mx[s][:, half], -1.0, CLIP, ALU.mult, ALU.min
                                            ).then_inc(max_clipped, 1)
                    dve.wait_ge(max_clipped, 2 * b + k + 1)
                    nc.vector.tensor_scalar(mneg[s][:, half], mxn[s][:, half], -CLIP, None, ALU.max
                                            ).then_inc(mneg_done, 1)

                def select(b):
                    dve.wait_ge(pv_done, 6 * b + 6)
                    den = db[:, 0:4 * LQ].rearrange("p (m e q) -> p m e q", m=KH, e=2)
                    out = ob[:, 0:4 * LQ].rearrange("p (m e q) -> p m e q", m=KH, e=2)
                    nc.vector.tensor_scalar(dsel0[:, :, :], den[:, :, 0, :], m.side[:, 0:1], None, ALU.mult)
                    nc.vector.tensor_scalar(osel0[:, :, :], out[:, :, 0, :], m.side[:, 0:1], None, ALU.mult
                                            ).then_inc(fin_step, 1)
                    dve.wait_ge(fin_step, 3 * b + 1)
                    nc.vector.scalar_tensor_tensor(dsel[:, :, :], den[:, :, 1, :], m.side[:, 1:2], dsel0[:, :, :],
                                                   ALU.mult, ALU.add)
                    nc.vector.scalar_tensor_tensor(osel[:, :, :], out[:, :, 1, :], m.side[:, 1:2], osel0[:, :, :],
                                                   ALU.mult, ALU.add).then_inc(fin_step, 1)

                def divide(b):
                    dve.wait_ge(fin_step, 3 * b + 2)
                    nc.vector.reciprocal(rden[:, :, :], dsel[:, :, :]).then_inc(fin_step, 1)
                    dve.wait_ge(fin_step, 3 * b + 3)
                    nc.vector.tensor_tensor(onT[:, :, :], osel[:, :, :], rden[:, :, :], ALU.mult).then_inc(on_done, 1)

                def o_statistics(b, s):
                    dve.wait_ge(ot_emptied, b + 1)
                    nc.vector.bn_stats(ost[s][:, :], oraw[s][:, :]).then_inc(obn_done, 1)
                    after_wait(obn_done, b + 1)
                    nc.vector.bn_aggr(omv[s][:, :], ost[s][:, :]).then_inc(ostats_done, 1)

                def o_normalise(b, s):
                    dve.wait_ge(orstd_step, 2 * b + 2)
                    nc.vector.tensor_scalar(oz[:, :], oraw[s][:, :], omv[s][:, 0:1], ors[s][:, :],
                                            ALU.subtract, ALU.mult).then_inc(oln_step, 1)
                    dve.wait_ge(oln_step, 2 * b + 1)
                    nc.vector.tensor_tensor(og[:, :], oz[:, :], m.g_ln[:, :], ALU.mult).then_inc(oln_step, 1)
                    dve.wait_ge(oln_step, 2 * b + 2)
                    if not (isinstance(b, int) and b < 2):
                        dve.wait_ge(ol_kept, b - 1)
                    nc.vector.tensor_tensor(ol[s][:, :], og[:, :], m.b_ln[:, :], ALU.add).then_inc(ol_done, 1)

                def step(b, s, prev, this, following, after, clips):
                    n = 1 - s
                    clips = clips and this
                    if clips:
                        clip(b, 0)
                    if prev:
                        select(b - 1)
                    if following:
                        affine(b + 1, 0, qnT, LQ, range(KH))
                        affine(b + 1, 1, knT, LK, [0])
                        affine(b + 1, 2, knT, LK, [1])
                    if prev:
                        divide(b - 1)
                    if clips:
                        clip(b, 1)
                    if following:
                        low_part(b + 1, 3, ql[:, :, :].rearrange("p k q -> p (k q)"),
                                 qh[:, :, :].rearrange("p k q -> p (k q)"), KH * LQ, qh_done, b + 2)
                    if prev:
                        o_statistics(b - 1, n)
                    if after:
                        statistics(b + 2, s, (b + 2 - s) // 2)
                    if following:
                        low_part(b + 1, 6, kl[n][:, 0, :], kh[n][:, 0, :], LK, kh_done, 2 * (b + 1) + 1)
                    if clips:
                        clip(b, 2)
                    if following:
                        low_part(b + 1, 7, kl[n][:, 1, :], kh[n][:, 1, :], LK, kh_done, 2 * (b + 1) + 2)
                    if prev:
                        o_normalise(b - 1, n)
                    if after:
                        statistics_again(b + 2, s)
                    if following:
                        maxima(b + 1, n, 0, b if clips else None)
                        maxima(b + 1, n, 1, b if clips else None)
                    elif clips:
                        for u in range(3, 6):
                            clip(b, u)
                    if after:
                        normalise_again(b + 2, s)

                for b in range(2):
                    statistics(b, b, 0)
                    statistics_again(b, b)
                    normalise_again(b, b)
                either(dve, lambda clips: over_batches(dve, lambda *a: step(*a, clips)))

            @block.scalar
            def _(act):
                def evacuate(b, pos, dst, src, then=None):
                    act.wait_ge(filled[pos % 2], nth(b, pos))
                    nc.scalar.activation(dst, src, ACT.Copy).then_inc(then or emptied[pos % 2], 1)

                def exps(b, u):
                    k, t = u // KT, u % KT
                    act.wait_ge(scores_done, 6 * b + u + 1)
                    if not (isinstance(b, int) and b == 0 and u < 2):
                        act.wait_ge(pv_done, 6 * b + u - 1)
                    nc.scalar.activation(probs[u % 2][0:KN[t], :, :].rearrange("p (c h) q -> p c (h q)", c=2),
                                         scores[0:KN[t], 2 * (u % 2):2 * (u % 2) + 2, 0:4 * LQ],
                                         ACT.Exp, scale=1.0 / TEMP).then_inc(exp_done, 1)

                def normalise(b, s):
                    act.wait_ge(shift_done, b + 1)
                    if not (isinstance(b, int) and b < 2):
                        act.wait_ge(filled[0], nth(b - 2, 2))
                    for t in range(KT):
                        last = nc.scalar.activation(norm[s][0:KN[t], t, :], raw[s][0:KN[t], t, :], ACT.Identity,
                                                    bias=shift[s][0:KN[t], t:t + 1], scale=rs[s][0:KN[t], t:t + 1])
                    last.then_inc(norm_done, 1)

                def take_o(b, s):
                    act.wait_ge(ot_done, b + 1)
                    nc.scalar.activation(oraw[s][:, :], ob[0:LQ, 0:D], ACT.Copy).then_inc(ot_emptied, 1)

                def batch(t, b):
                    return t[:, bass.ds(b, 1), :].rearrange("p o d -> p (o d)")

                def step(b, s, prev, this, following, after):
                    n = 1 - s
                    if this:
                        exps(b, 0)
                        exps(b, 1)
                    if following:
                        if not (isinstance(b, int) and b == -1):
                            act.wait_ge(qb_done, 2 * b + 2)
                        evacuate(b + 1, 3, qh[:, :, :].rearrange("p k q -> p (k q)"), ring[1][:, 0:KH * LQ], qh_done)
                        evacuate(b + 1, 4, cT[:, 0, :], ring[0][:, 0:LK])
                    if prev:
                        take_o(b - 1, n)
                    if following:
                        evacuate(b + 1, 5, cT[:, 1, :], ring[1][:, 0:LK])
                        evacuate(b + 1, 6, kh[n][:, 0, :], ring[0][:, 0:LK], kh_done)
                    if this:
                        exps(b, 2)
                    if following:
                        evacuate(b + 1, 7, kh[n][:, 1, :], ring[1][:, 0:LK], kh_done)
                        evacuate(b + 1, 8, v[n][0:KN[0], 0, :], ring[0][0:KN[0], 0:D])
                        evacuate(b + 1, 9, v[n][0:KN[1], 1:3, :].rearrange("p t d -> p (t d)"),
                                 ring[1][0:KN[1], 0:2 * D])
                    if this:
                        exps(b, 3)
                        exps(b, 4)
                    if prev:
                        evacuate(b + 1, OT, olT[:, :, :].rearrange("p k q -> p (k q)"), ring[OT % 2][:, 0:KH * LQ])
                    if this:
                        exps(b, 5)
                    if prev:
                        evacuate(b + 1, OP, batch(m.proj, b - 1), ring[OP % 2][0:LQ, 0:D])
                        nc.scalar.activation(batch(m.h2, b - 1), ol[n][:, :], ACT.Copy).then_inc(ol_kept, 1)
                    if after:
                        normalise(b + 2, s)

                for b in range(2):
                    normalise(b, b)
                over_batches(act, step)

            @block.tensor
            def _(pe):
                def free_ring(b, pos):
                    if not (isinstance(b, int) and b == 0 and pos < 2):
                        pe.wait_ge(emptied[pos % 2], nth(b, pos) - 1)

                def transpose_x(b, s):
                    pe.wait_ge(z2_done, b + 1)
                    free_ring(b, 0)
                    for k in range(KH):
                        last = nc.tensor.transpose(ring[0][:, k * LQ:(k + 1) * LQ], zq[s][:, k * 128:(k + 1) * 128],
                                                   m.ident[0:LQ, 0:LQ])
                    last.then_inc(filled[0], 1)

                def transpose_ctx(b, pos, src, k, ready):
                    if ready is not None:
                        pe.wait_ge(ready, b + 1)
                    free_ring(b, pos)
                    for t in range(KT):
                        last = nc.tensor.transpose(ring[pos % 2][:, KOFF[t]:KOFF[t] + KN[t]],
                                                   src[0:KN[t], t, k * 128:(k + 1) * 128],
                                                   m.ident[0:KN[t], 0:KN[t]])
                    last.then_inc(filled[pos % 2], 1)

                def project(b, pos, w, src, mts, n, inputs):
                    for p in inputs:
                        pe.wait_ge(emptied[p % 2], nth(b, p))
                    free_ring(b, pos)
                    for i, mt in enumerate(mts):
                        for k in range(KH):
                            last = nc.tensor.matmul(ring[pos % 2][:, i * n:(i + 1) * n],
                                                    w[:, k, mt * 128:(mt + 1) * 128], src[:, k, :],
                                                    start=k == 0, stop=k == KH - 1)
                    last.then_inc(filled[pos % 2], 1)

                def project_v(b, pos, tiles):
                    if pos == 8:
                        pe.wait_ge(emptied[1], nth(b, 5))
                    free_ring(b, pos)
                    for i, t in enumerate(tiles):
                        for k in range(KH):
                            last = nc.tensor.matmul(ring[pos % 2][0:KN[t], i * D:(i + 1) * D],
                                                    cT[:, k, KOFF[t]:KOFF[t] + KN[t]], m.wv[:, k, :],
                                                    start=k == 0, stop=k == KH - 1)
                    last.then_inc(filled[pos % 2], 1)

                def scores_for_max(b, s, h, clips):
                    pos = at(h)
                    k, j = h // HH, h % HH
                    pe.wait_ge(qb_done, 2 * b + 1)
                    pe.wait_ge(kh_done, 2 * b + 1 + k)
                    free_ring(b, pos)
                    bank = ring[pos % 2][0:LQ, 0:LK]
                    if clips:
                        nc.tensor.matmul(bank, qbh[s][:, k, j, :], kl[s][:, k, :], start=True, stop=False)
                        if h == 0:
                            pe.wait_ge(qb_done, 2 * b + 2)
                        nc.tensor.matmul(bank, qbl[s][:, k, j, :], kh[s][:, k, :], start=False, stop=False)
                    nc.tensor.matmul(bank, qbh[s][:, k, j, :], kh[s][:, k, :], start=not clips, stop=True
                                     ).then_inc(filled[pos % 2], 1)

                def score_part(b, s, u, part, clips):
                    k, t = u // KT, u % KT
                    c = part // 2
                    if part == 0:
                        if u % KT == 0:
                            pe.wait_ge(qb_done, 2 * b + 2)
                            pe.wait_ge(emptied[k], nth(b, 6 + k))
                            pe.wait_ge(mdiag_done, 2 * b + k + 1)
                        if not (isinstance(b, int) and b == 0 and u < 2):
                            pe.wait_ge(exp_done, 6 * b + u - 1)
                    keys = slice(KOFF[t], KOFF[t] + KN[t])
                    banks = [scores[0:KN[t], 2 * (u % 2) + i, 0:4 * LQ] for i in range(2)]
                    heads = slice(4 * c, 4 * c + 4)

                    def minus_max(c):
                        return nc.tensor.matmul(banks[c], m.ones_b[0:LQ, 0:KN[t]],
                                                mdiag[s][:, HH * k + 4 * c:HH * k + 4 * c + 4, :],
                                                start=False, stop=True, skip_group_check=clips)

                    if part % 2 == 0:
                        nc.tensor.matmul(banks[c], kh[s][:, k, keys], qbh[s][:, k, heads, :], start=True, stop=False)
                        nc.tensor.matmul(banks[c], kh[s][:, k, keys], qbl[s][:, k, heads, :], start=False, stop=False)
                        return
                    last = nc.tensor.matmul(banks[c], kl[s][:, k, keys], qbh[s][:, k, heads, :],
                                            start=False, stop=clips)
                    if not clips:
                        last = minus_max(c)
                    elif part == 3:
                        last.then_inc(raw_done, 1)
                        pe.wait_ge(clipped, 6 * b + u + 1)
                        minus_max(0)
                        last = minus_max(1)
                    if part == 3:
                        last.then_inc(scores_done, 1)

                def score_unit(b, s, u, clips):
                    for part in range(4):
                        score_part(b, s, u, part, clips)

                def weighted_part(b, s, u, part):
                    k, t = u // KT, u % KT
                    if part == 0:
                        pe.wait_ge(exp_done, 6 * b + u + 1)
                        if u == 0:
                            pe.wait_ge(emptied[0], nth(b, 8))
                            pe.wait_ge(emptied[1], nth(b, 9))
                            if not (isinstance(b, int) and b == 0):
                                pe.wait_ge(ot_emptied, b)
                    for g in range(4):
                        w = m.ones[0:KN[t], 0:32] if part else \
                            v[s][0:KN[t], t, 128 * k + 32 * g:128 * k + 32 * g + 32]
                        last = nc.tensor.matmul((db if part else ob)[32 * g:32 * g + 32,
                                                                     2 * LQ * k:2 * LQ * (k + 1)], w,
                                                probs[u % 2][0:KN[t], 2 * g:2 * g + 2, :],
                                                start=t == 0, stop=t == KT - 1)
                    if part:
                        last.then_inc(pv_done, 1)

                def transpose_o(b):
                    pe.wait_ge(on_done, b + 1)
                    for k in range(KH):
                        last = nc.tensor.transpose(ob[0:LQ, 128 * k:128 * (k + 1)], onT[:, k, :], m.ident[:, :])
                    last.then_inc(ot_done, 1)

                def transpose_o_ln(b, s, r):
                    pe.wait_ge(ol_done, b + 1)
                    free_ring(r, OT)
                    for k in range(KH):
                        last = nc.tensor.transpose(ring[OT % 2][:, k * LQ:(k + 1) * LQ],
                                                   ol[s][:, k * 128:(k + 1) * 128], m.ident[0:LQ, 0:LQ])
                    last.then_inc(filled[OT % 2], 1)

                def project_o(b, s, r):
                    pe.wait_ge(emptied[OT % 2], nth(r, OT))
                    free_ring(r, OP)
                    for k in range(KH):
                        last = nc.tensor.matmul(ring[OP % 2][0:LQ, 0:D], olT[:, k, :], m.wo[:, k, :],
                                                start=k == 0, stop=k == KH - 1)
                    last.then_inc(filled[OP % 2], 1)

                def step(b, s, prev, this, following, after, clips):
                    n = 1 - s
                    if this:
                        score_unit(b, s, 0, clips)
                    if following:
                        transpose_x(b + 1, n)
                        transpose_ctx(b + 1, 1, norm[n], 0, norm_done)
                        transpose_ctx(b + 1, 2, norm[n], 1, None)
                    if this:
                        score_unit(b, s, 1, clips)
                    if following:
                        project(b + 1, 3, m.wq, qnT, range(KH), LQ, [0])
                        transpose_ctx(b + 1, 4, raw[n], 0, None)
                    if prev:
                        transpose_o(b - 1)
                    if following:
                        transpose_ctx(b + 1, 5, raw[n], 1, None)
                        project(b + 1, 6, m.wk, knT, [0], LK, [1])
                    if this:
                        weighted_part(b, s, 0, 0)
                        weighted_part(b, s, 0, 1)
                        score_unit(b, s, 2, clips)
                    if following:
                        project(b + 1, 7, m.wk, knT, [1], LK, [])
                        project_v(b + 1, 8, [0])
                    if this:
                        weighted_part(b, s, 1, 0)
                        weighted_part(b, s, 1, 1)
                    if following:
                        project_v(b + 1, 9, [1, 2])
                    if this:
                        score_part(b, s, 3, 0, clips)
                        score_part(b, s, 3, 1, clips)
                    for i in range(10, RING):
                        if following and i not in (OT, OP):
                            scores_for_max(b + 1, n, i - 10 - (i > OT), clips)
                        if prev and i == OT:
                            transpose_o_ln(b - 1, n, b + 1)
                        if prev and i == OP:
                            project_o(b - 1, n, b + 1)
                        if this:
                            kind, u, part = BETWEEN[i - 10]
                            if kind == "score":
                                score_part(b, s, u, part, clips)
                            else:
                                weighted_part(b, s, u, part)

                either(pe, lambda clips: over_batches(pe, lambda *a: step(*a, clips)))


def over_chunks(eng, lead, trail):
    for c in range(4):
        lead(c, c % 2, c < 2)
        if trail and c:
            trail(c - 1, (c - 1) % 2, c < 3)
    with eng.Fori(2, NC // 2) as it:
        for s in range(2):
            lead(it * 2 + s, s, False)
            if trail:
                trail(it * 2 + s - 1, 1 - s, False)
    if trail:
        trail(NC - 1, 1, False)


def tokens_and_logits(nc, ins, m):
    with ExitStack() as ctx:
        def sb(name, shape, dt=F32):
            return ctx.enter_context(nc.sbuf_tensor(name, shape, dt))

        def pair(name, shape, dt=F32):
            return [sb(f"{name}{s}", shape, dt) for s in range(2)]

        def sem(name):
            return ctx.enter_context(nc.semaphore(name))

        st = sb("h_stats", [LQ, CB, 6])
        carrier = sb("h_carrier", [1, 1])
        mv = pair("h_mean_var", [LQ, CB, 2])
        var = pair("h_var_eps", [LQ, CB])
        rs = pair("h_rstd", [LQ, CB])
        h = pair("h_chunk", [LQ, CB, D])
        ge = pair("gelu", [LQ, CB, D])
        y = pair("attention_out", [LQ, CB, D])
        lT = pair("logits_T", [E, CN])
        tp = [ctx.enter_context(nc.psum_tensor(f"hT_psum{k}", [128, 512], F32)) for k in range(KH)]
        lp = ctx.enter_context(nc.psum_tensor("logits_T_psum", [128, 512], F32))
        lb = ctx.enter_context(nc.psum_tensor("logits_psum", [128, 512], F32))

        gelu_done, y_done, x1_done = sem("gelu_done"), sem("y_done"), sem("x1_done")
        bn_done, stats_done, rstd_step = sem("h_bn_done"), sem("h_stats_done"), sem("h_rstd_step")
        h_done, base_done, h_kept = sem("h_done"), sem("base_done"), sem("h_kept")
        t_done, t_emptied, logits_done = sem("h_t_done"), sem("h_t_emptied"), sem("logits_done")
        lT_done, back_done, back_taken = sem("lT_done"), sem("logits_back"), sem("logits_taken")

        def batches(t, c):
            return t[:, bass.ds(c * CB, CB), :]

        def batch(t, c, j):
            return t[:, bass.ds(c * CB + j, 1), :].rearrange("p o d -> p (o d)")

        with nc.Block() as block:

            @block.vector
            def _(dve):
                def normalise(c, s, first):
                    dve.wait_ge(gelu_done, c + 1)
                    nc.vector.tensor_tensor(y[s][:, :, :], ge[s][:, :, :], batches(m.h2, c), ALU.add
                                            ).then_inc(y_done, 1)
                    dve.wait_ge(y_done, c + 1)
                    nc.vector.scalar_tensor_tensor(batches(m.x, c), y[s][:, :, :], m.tanh[0:LQ, 0:1],
                                                   batches(m.x, c), ALU.mult, ALU.add).then_inc(x1_done, 1)
                    dve.wait_ge(x1_done, c + 1)
                    nc.vector.memset(carrier[:, :], 0.0)
                    for j in range(CB):
                        last = nc.vector.bn_stats(st[:, j, :], batch(m.x, c, j))
                    last.then_inc(bn_done, 1)
                    dve.wait_ge(bn_done, c + 1)
                    nc.vector.memset(carrier[:, :], 0.0)
                    for j in range(CB):
                        last = nc.vector.bn_aggr(mv[s][:, j, :], st[:, j, :])
                    last.then_inc(stats_done, 1)
                    dve.wait_ge(rstd_step, 2 * c + 2)
                    if not first:
                        dve.wait_ge(t_done, c - 1)
                        dve.wait_ge(h_kept, c - 1)
                    for j in range(CB):
                        last = nc.vector.tensor_scalar(h[s][:, j, :], batch(m.x, c, j), mv[s][:, j, 0:1],
                                                       rs[s][:, j:j + 1], ALU.subtract, ALU.mult)
                    last.then_inc(h_done, 1)
                    dve.wait_ge(h_done, c + 1)
                    nc.vector.scalar_tensor_tensor(batches(m.x, c), h[s][:, :, :], m.tanh[0:LQ, 1:2],
                                                   batches(m.x, c), ALU.mult, ALU.add).then_inc(base_done, 1)

                def take_logits(c, s, first):
                    dve.wait_ge(logits_done, c + 1)
                    nc.vector.tensor_scalar(lT[s][:, :], lp[0:E, 0:CN], m.br[:, 0:1], None, ALU.add
                                            ).then_inc(lT_done, 1)

                over_chunks(dve, normalise, take_logits)

            @block.gpsimd
            def _(pool):
                def step(c, s, first):
                    pool.wait_ge(stats_done, c + 1)
                    nc.gpsimd.tensor_tensor(var[s][:, :], mv[s][:, :, 1], m.eps[0:LQ, 0:CB], ALU.add
                                            ).then_inc(rstd_step, 1)
                    pool.wait_ge(rstd_step, 2 * c + 1)
                    nc.gpsimd.tensor_tensor(rs[s][:, :], var[s][:, :], m.minus_half[0:LQ, 0:CB],
                                            ALU.pow).then_inc(rstd_step, 1)
                    pool.wait_ge(h_done, c + 1)
                    nc.gpsimd.tensor_copy(batches(m.h2, c), h[s][:, :, :]).then_inc(h_kept, 1)
                over_chunks(pool, step, None)

            @block.tensor
            def _(pe):
                def transposes(c, s, first):
                    pe.wait_ge(h_done, c + 1)
                    if not (isinstance(c, int) and c == 0):
                        pe.wait_ge(t_emptied, 2 * c)
                    for k in range(KH):
                        for j in range(CB):
                            last = nc.tensor.transpose(tp[k][:, j * LQ:(j + 1) * LQ],
                                                       h[s][:, j, k * 128:(k + 1) * 128], m.ident[0:LQ, 0:LQ])
                    last.then_inc(t_done, 1)

                def logits(c, s, first):
                    pe.wait_ge(t_emptied, 2 * c + 2)
                    if not (isinstance(c, int) and c == 0):
                        pe.wait_ge(lT_done, c)
                    for k in range(KH):
                        last = nc.tensor.matmul(lp[0:E, 0:CN], m.wr[:, k, :],
                                                m.h2T[:, k, bass.ds(c * CN, CN)],
                                                start=k == 0, stop=k == KH - 1)
                    last.then_inc(logits_done, 1)
                    pe.wait_ge(lT_done, c + 1)
                    if not (isinstance(c, int) and c == 0):
                        pe.wait_ge(back_taken, c)
                    for j in range(CB):
                        last = nc.tensor.matmul(lb[0:LQ, j * E:(j + 1) * E], lT[s][:, j * LQ:(j + 1) * LQ],
                                                m.ident[0:E, 0:E], start=True, stop=True)
                    last.then_inc(back_done, 1)

                over_chunks(pe, transposes, logits)

            @block.scalar
            def _(act):
                def gelu(c, s, first):
                    if not first:
                        act.wait_ge(y_done, c - 1)
                    nc.scalar.activation(ge[s][:, :, :], batches(m.proj, c), ACT.Gelu).then_inc(gelu_done, 1)

                def take(c, s, first):
                    act.wait_ge(t_done, c + 1)
                    for k in range(KH):
                        nc.scalar.activation(m.h2T[:, k, bass.ds(c * CN, CN)], tp[k][:, 0:CN], ACT.Copy
                                             ).then_inc(t_emptied, 1)

                    act.wait_ge(back_done, c + 1)
                    nc.scalar.activation(batches(m.logits, c).rearrange("p j e -> p (j e)"), lb[0:LQ, 0:CB * E],
                                         ACT.Copy).then_inc(back_taken, 1)

                over_chunks(act, gelu, take)


def mlp_weights(nc, ctx, name):
    return (ctx.enter_context(nc.sbuf_tensor(f"{name}_gate", [128, KH, F], F32)),
            ctx.enter_context(nc.sbuf_tensor(f"{name}_up", [128, KH, F], F32)),
            ctx.enter_context(nc.sbuf_tensor(f"{name}_down", [128, len(FN), D], F32)))


def route_and_shared(nc, ins, m):
    NF = len(FN)
    with ExitStack() as ctx:
        def sb(name, shape, dt=F32):
            return ctx.enter_context(nc.sbuf_tensor(name, shape, dt))

        def pair(name, shape, dt=F32):
            return [sb(f"{name}{s}", shape, dt) for s in range(2)]

        def sem(name):
            return ctx.enter_context(nc.semaphore(name))

        top = sb("logit_max", [LQ, B])
        pr = sb("router_probs", [LQ, B, E])
        psum_ = sb("prob_sum", [LQ, B])
        rsum = sb("prob_sum_inv", [LQ, B])
        v8 = sb("best_values", [LQ, B, 8])
        i8 = sb("best_experts", [LQ, B, 8], U32)
        best = sb("best2", [LQ, 2, B])
        idx = sb("experts2", [LQ, 2, B])
        oh = sb("one_hot", [LQ, 2, B, E])
        scan = pair("scan", [LQ, B, E])
        before = sb("tiles_before", [LQ, B, E])
        chosen = sb("chosen", [LQ, B, E])
        at = sb("positions_at", [LQ, 2, B, E])
        pos = sb("position", [LQ, 2, B])
        within = sb("within", [LQ, 2, B])
        slot = sb("slot", [LQ, 2, B])
        far = sb("far", [LQ, 2, B])
        den = sb("weight_sum", [LQ, B])
        dinv = sb("weight_sum_inv", [LQ, B])
        wn = sb("weight_norm", [LQ, 2, B])
        wg, wu, wd = mlp_weights(nc, ctx, "shared")
        sg = pair("shared_silu", [128, CN])
        hid = pair("shared_hidden", [128, NF, CN])

        gp = [ctx.enter_context(nc.psum_tensor(f"gate_psum{s}", [128, 512], F32)) for s in range(2)]
        up = [ctx.enter_context(nc.psum_tensor(f"up_psum{s}", [128, 512], F32)) for s in range(2)]
        dn = [ctx.enter_context(nc.psum_tensor(f"down_psum{s}", [128, 2, D], F32)) for s in range(2)]
        pp = ctx.enter_context(nc.psum_tensor("position_psum", [128, 512], F32))

        w_loaded, r, exp_done = sem("shared_loaded"), sem("route_step"), sem("router_exp")
        before_done, counted, routed, scattered = sem("before_done"), sem("counted"), sem("routed"), sem("scattered")
        gu_done, silu_done, hid_done = sem("gate_up_done"), sem("silu_done"), sem("hidden_done")
        down_done, added = sem("down_done"), sem("shared_added")

        with nc.Block() as block:

            @block.sync
            def _(sp):
                load_mlp(sp, (wg, wu, wd), ins["sw_gate"], ins["sw_up"], ins["sw_down"], w_loaded)
                sp.wait_ge(w_loaded, 16 * MLP_LOADS)

            @block.vector
            def _(dve):
                steps = [0]

                def then(ins_):
                    steps[0] += 1
                    ins_.then_inc(r, 1)
                    dve.wait_ge(r, steps[0])

                def wide(t):
                    return t.unsqueeze(2).to_broadcast([LQ, B, E])

                lg = m.logits
                then(nc.vector.reduce_max(top[:, :], lg[:, :, :], axis=X))
                then(nc.vector.tensor_tensor(pr[:, :, :], lg[:, :, :], wide(top[:, :]), ALU.subtract))
                dve.wait_ge(exp_done, 1)
                then(nc.vector.reduce_sum(psum_[:, :], lg[:, :, :], axis=X))
                then(nc.vector.reciprocal(rsum[:, :], psum_[:, :]))
                then(nc.vector.tensor_tensor(pr[:, :, :], lg[:, :, :], wide(rsum[:, :]), ALU.mult))
                for b in range(B):
                    last = nc.vector.max(v8[:, b, :], pr[:, b, :])
                then(last)
                for b in range(B):
                    last = nc.vector.max_index(i8[:, b, :], v8[:, b, :], pr[:, b, :])
                then(last)
                nc.vector.tensor_copy(best[:, :, :], v8[:, :, 0:2].rearrange("p b k -> p k b"))
                then(nc.vector.tensor_copy(idx[:, :, :], i8[:, :, 0:2].rearrange("p b k -> p k b")))
                for k in range(2):
                    last = nc.vector.tensor_tensor(oh[:, k, :, :], wide(idx[:, k, :]),
                                                   m.expert_f[0:LQ, :].unsqueeze(1).to_broadcast([LQ, B, E]),
                                                   ALU.is_equal)
                then(last)
                then(nc.vector.tensor_tensor(chosen[:, :, :], oh[:, 0, :, :], oh[:, 1, :, :], ALU.add))
                src = chosen
                for i, d in enumerate((1, 2, 4, 8, 16)):
                    dst = scan[i % 2]
                    nc.vector.tensor_copy(dst[:, 0:d, :], src[:, 0:d, :])
                    then(nc.vector.tensor_tensor(dst[:, d:B, :], src[:, d:B, :], src[:, 0:B - d, :], ALU.add))
                    src = dst
                nc.vector.memset(before[:, 0, :], 0.0)
                nc.vector.tensor_copy(before[:, 1:B, :], src[:, 0:B - 1, :]).then_inc(before_done, 1)
                dve.wait_ge(counted, 1)
                for k in range(2):
                    last = nc.vector.tensor_tensor(at[:, k, :, :], oh[:, k, :, :],
                                                   pp[0:LQ, 0:B * E].rearrange("p (b e) -> p b e", e=E), ALU.mult)
                then(last)
                then(nc.vector.reduce_sum(pos[:, :, :], at[:, :, :, :], axis=X))
                nc.vector.tensor_scalar(within[:, :, :], pos[:, :, :], float(CAP), None, ALU.is_lt)
                then(nc.vector.scalar_tensor_tensor(slot[:, :, :], idx[:, :, :], float(CAP), pos[:, :, :],
                                                    ALU.mult, ALU.add))
                then(nc.vector.tensor_scalar(far[:, :, :], within[:, :, :], -1e6, 1e6, ALU.mult, ALU.add))
                nc.vector.tensor_tensor(m.scatter_at[:, :, :], slot[:, :, :], far[:, :, :], ALU.add
                                        ).then_inc(routed, 1)
                nc.vector.tensor_tensor(m.gather_at[:, :, :], slot[:, :, :], within[:, :, :], ALU.mult)
                then(nc.vector.tensor_tensor(den[:, :], best[:, 0, :], best[:, 1, :], ALU.add))
                then(nc.vector.tensor_scalar(rsum[:, :], den[:, :], 1e-9, None, ALU.add))
                then(nc.vector.reciprocal(dinv[:, :], rsum[:, :]))
                then(nc.vector.tensor_tensor(wn[:, :, :], best[:, :, :],
                                             dinv[:, :].unsqueeze(1).to_broadcast([LQ, 2, B]), ALU.mult))
                nc.vector.scalar_tensor_tensor(m.weight[:, :, :], wn[:, :, :], m.tanh[0:LQ, 1:2], within[:, :, :],
                                               ALU.mult, ALU.mult)

                def hidden(c, s, first):
                    for f in range(NF):
                        n = NF * c + f
                        dve.wait_ge(silu_done, n + 1)
                        q = (f + s) % 2
                        nc.vector.tensor_tensor(hid[s][0:FN[f], f, :], sg[q][0:FN[f], :], up[q][0:FN[f], 0:CN],
                                                ALU.mult).then_inc(hid_done, 1)

                def add(c, s, first):
                    for i in range(2):
                        dve.wait_ge(down_done, 2 * c + i + 1)
                        rows = m.x[:, bass.ds(c * CB + 2 * i, 2), :]
                        nc.vector.scalar_tensor_tensor(rows, dn[i][0:LQ, :, :], m.tanh[0:LQ, 1:2], rows,
                                                       ALU.mult, ALU.add).then_inc(added, 1)

                over_chunks(dve, hidden, add)

            @block.gpsimd
            def _(pool):
                pool.wait_ge(routed, 1)
                for b in range(B):
                    for k in range(2):
                        nc.gpsimd.indirect_dma_start(
                            out=ins["xg"], out_offset=bass.IndirectOffsetOnAxis(ap=m.scatter_at[:, k, b:b + 1], axis=0),
                            in_=m.h2[:, b, :], in_offset=None, bounds_check=E * CAP - 1, oob_is_err=False
                        ).then_inc(scattered, 16)
                pool.wait_ge(scattered, 16 * 2 * B)

            @block.scalar
            def _(act):
                act.wait_ge(r, 2)
                nc.scalar.activation(m.logits[:, :, :], pr[:, :, :], ACT.Exp).then_inc(exp_done, 1)

                def silus(c, s, first):
                    for f in range(NF):
                        n = NF * c + f
                        q = (f + s) % 2
                        act.wait_ge(gu_done, n + 1)
                        if not (isinstance(c, int) and n < 2):
                            act.wait_ge(hid_done, n - 1)
                        nc.scalar.activation(sg[q][0:FN[f], :], gp[q][0:FN[f], 0:CN], ACT.Silu).then_inc(silu_done, 1)

                over_chunks(act, silus, None)

            @block.tensor
            def _(pe):
                pe.wait_ge(w_loaded, 16 * MLP_LOADS)

                def gate_up(c, s, first):
                    for f in range(NF):
                        n = NF * c + f
                        q = (f + s) % 2
                        if not (isinstance(c, int) and n < 2):
                            pe.wait_ge(hid_done, n - 1)
                        for w, bank in ((wg, gp[q]), (wu, up[q])):
                            for k in range(KH):
                                last = nc.tensor.matmul(bank[0:FN[f], 0:CN], w[:, k, 128 * f:128 * f + FN[f]],
                                                        m.h2T[:, k, bass.ds(c * CN, CN)],
                                                        start=k == 0, stop=k == KH - 1)
                        last.then_inc(gu_done, 1)

                def down(c, s, first):
                    pe.wait_ge(hid_done, NF * (c + 1))
                    for i in range(2):
                        if not (isinstance(c, int) and c == 0):
                            pe.wait_ge(added, 2 * c + i - 1)
                        for j in range(2):
                            for f in range(NF):
                                rows = slice((2 * i + j) * LQ, (2 * i + j + 1) * LQ)
                                last = nc.tensor.matmul(dn[i][0:LQ, j, :], hid[s][0:FN[f], f, rows],
                                                        wd[0:FN[f], f, :], start=f == 0, stop=f == NF - 1)
                        last.then_inc(down_done, 1)

                pe.wait_ge(before_done, 1)
                nc.tensor.matmul(pp[0:LQ, 0:B * E], m.earlier[0:LQ, :], chosen[:, :, :], start=True, stop=False)
                nc.tensor.matmul(pp[0:LQ, 0:B * E], m.ones[0:LQ, 0:LQ], before[:, :, :], start=False, stop=True
                                 ).then_inc(counted, 1)
                over_chunks(pe, gate_up, down)


MLP_LOADS = 4


def load_mlp(sp, weights, gate, up, down, loaded):
    wg, wu, wd = weights
    sp.dma_start(wg[:, :, :], gate.rearrange("(k p) f -> p k f", p=128)).then_inc(loaded, 16)
    sp.dma_start(wu[:, :, :], up.rearrange("(k p) f -> p k f", p=128)).then_inc(loaded, 16)
    sp.dma_start(wd[:, 0:2, :], down[0:256, :].rearrange("(k p) d -> p k d", p=128)).then_inc(loaded, 16)
    sp.dma_start(wd[0:FN[2], 2, :], down[256:F, :]).then_inc(loaded, 16)


def experts(nc, ins, m):
    NF = len(FN)
    with ExitStack() as ctx:
        def sb(name, shape, dt=F32):
            return ctx.enter_context(nc.sbuf_tensor(name, shape, dt))

        def pair(name, shape, dt=F32):
            return [sb(f"{name}{s}", shape, dt) for s in range(2)]

        def sem(name):
            return ctx.enter_context(nc.semaphore(name))

        w = [mlp_weights(nc, ctx, f"expert{s}") for s in range(2)]
        rows = pair("rows", [RN, RT, D])
        xT = pair("rows_T", [128, KH, CAP])
        sg = pair("expert_silu", [128, CAP])
        hid = pair("expert_hidden", [128, NF, CAP])
        y = pair("y", [RN, RT, D])
        gp = [ctx.enter_context(nc.psum_tensor(f"expert_gate_psum{s}", [128, 512], F32)) for s in range(2)]
        up = [ctx.enter_context(nc.psum_tensor(f"expert_up_psum{s}", [128, 512], F32)) for s in range(2)]
        dn = [ctx.enter_context(nc.psum_tensor(f"expert_down_psum{s}", [128, 2, D], F32)) for s in range(2)]
        tp = [ctx.enter_context(nc.psum_tensor(f"rowsT_psum{k}", [128, 512], F32)) for k in range(KH)]

        loaded = [sem(f"weights_loaded{s}") for s in range(2)]
        rows_loaded = [sem(f"rows_loaded{s}") for s in range(2)]
        stored = [sem(f"y_stored{s}") for s in range(2)]
        t_done, t_emptied = sem("rows_t_done"), sem("rows_t_emptied")
        gu_done, silu_done, hid_done = sem("expert_gate_up_done"), sem("expert_silu_done"), sem("expert_hidden_done")
        down_done, y_done = sem("expert_down_done"), [sem(f"y_done{i}") for i in range(2)]

        def over_experts(eng, step):
            for e in range(4):
                step(e, e % 2, e // 2)
            with eng.Fori(2, E // 2) as it:
                for s in range(2):
                    step(it * 2 + s, s, it)

        def new(e):
            return isinstance(e, int) and e < 2

        with nc.Block() as block:

            @block.sync
            def _(sp):
                def store(e, s, use):
                    sp.wait_ge(y_done[0], e + 1)
                    sp.wait_ge(y_done[1], e + 1)
                    sp.dma_start(ins["yg"][bass.ds(e * CAP, CAP), :].rearrange("(p t) d -> p t d", t=RT),
                                 y[s][:, :, :]).then_inc(stored[s], 16)

                def load(e, s, use):
                    if not new(e):
                        store(e - 2, s, use - 1)
                        sp.wait_ge(down_done, 2 * e - 2)
                    sp.dma_start(rows[s][:, :, :],
                                 ins["xg"][bass.ds(e * CAP, CAP), :].rearrange("(p t) d -> p t d", t=RT)
                                 ).then_inc(rows_loaded[s], 16)
                    load_mlp(sp, w[s], ins["w_gate"][bass.ds(e, 1), :, :].rearrange("o d f -> (o d) f"),
                             ins["w_up"][bass.ds(e, 1), :, :].rearrange("o d f -> (o d) f"),
                             ins["w_down"][bass.ds(e, 1), :, :].rearrange("o f d -> (o f) d"), loaded[s])

                over_experts(sp, load)
                for s in range(2):
                    store(E - 2 + s, s, E // 2 - 1)
                for s in range(2):
                    sp.wait_ge(stored[s], 16 * (E // 2))

            @block.tensor
            def _(pe):
                def transposes(e, s, use):
                    pe.wait_ge(rows_loaded[s], use * 16 + 16)
                    for k in range(KH):
                        if not (isinstance(e, int) and e == 0):
                            pe.wait_ge(t_emptied, 2 * e - 1 + k)
                        for t in range(RT):
                            last = nc.tensor.transpose(tp[k][:, t * RN:(t + 1) * RN],
                                                       rows[s][:, t, k * 128:(k + 1) * 128], m.ident[0:RN, 0:RN])
                        last.then_inc(t_done, 1)

                def gate_up(e, s, use):
                    pe.wait_ge(loaded[s], use * (16 * MLP_LOADS) + 16 * MLP_LOADS)
                    pe.wait_ge(t_emptied, 2 * e + 2)
                    for f in range(NF):
                        n = NF * e + f
                        q = (f + s) % 2
                        if not (isinstance(e, int) and n < 2):
                            pe.wait_ge(hid_done, n - 1)
                        for wt, bank in ((w[s][0], gp[q]), (w[s][1], up[q])):
                            for k in range(KH):
                                last = nc.tensor.matmul(bank[0:FN[f], 0:CAP], wt[:, k, 128 * f:128 * f + FN[f]],
                                                        xT[s][:, k, :], start=k == 0, stop=k == KH - 1)
                        last.then_inc(gu_done, 1)

                def down(e, s):
                    pe.wait_ge(hid_done, NF * e + NF)
                    for i in range(2):
                        if not (isinstance(e, int) and e == 0):
                            pe.wait_ge(y_done[i], e)
                        for j in range(2):
                            t = 2 * i + j
                            for f in range(NF):
                                last = nc.tensor.matmul(dn[i][0:RN, j, :], hid[s][0:FN[f], f, t * RN:(t + 1) * RN],
                                                        w[s][2][0:FN[f], f, :], start=f == 0, stop=f == NF - 1)
                        last.then_inc(down_done, 1)

                def step(e, s, use):
                    transposes(e, s, use)
                    if not (isinstance(e, int) and e == 0):
                        down(e - 1, 1 - s)
                    gate_up(e, s, use)

                over_experts(pe, step)
                down(E - 1, 1)

            @block.scalar
            def _(act):
                def step(e, s, use):
                    for k in range(KH):
                        act.wait_ge(t_done, 2 * e + k + 1)
                        if not new(e):
                            act.wait_ge(gu_done, NF * e - NF)
                        nc.scalar.activation(xT[s][:, k, :], tp[k][:, 0:CAP], ACT.Copy).then_inc(t_emptied, 1)
                    for f in range(NF):
                        n = NF * e + f
                        q = (f + s) % 2
                        act.wait_ge(gu_done, n + 1)
                        if not (isinstance(e, int) and n < 2):
                            act.wait_ge(hid_done, n - 1)
                        nc.scalar.activation(sg[q][0:FN[f], :], gp[q][0:FN[f], 0:CAP], ACT.Silu).then_inc(silu_done, 1)

                over_experts(act, step)

            @block.vector
            def _(dve):
                def take_y(e, s, use):
                    for i in range(2):
                        dve.wait_ge(down_done, 2 * e + i + 1)
                        if not (isinstance(e, int) and e < 2):
                            dve.wait_ge(stored[s], 16 * use)
                        nc.vector.tensor_copy(y[s][:, 2 * i:2 * i + 2, :], dn[i][0:RN, :, :]).then_inc(y_done[i], 1)

                def step(e, s, use):
                    if not (isinstance(e, int) and e == 0):
                        take_y(e - 1, 1 - s, use if s else use - 1)
                    for f in range(NF):
                        n = NF * e + f
                        q = (f + s) % 2
                        dve.wait_ge(silu_done, n + 1)
                        if not new(e) and f == 0:
                            dve.wait_ge(down_done, 2 * e - 2)
                        nc.vector.tensor_tensor(hid[s][0:FN[f], f, :], sg[q][0:FN[f], :], up[q][0:FN[f], 0:CAP],
                                                ALU.mult).then_inc(hid_done, 1)

                over_experts(dve, step)
                take_y(E - 1, 1, E // 2 - 1)


def combine(nc, ins, m, out):
    with ExitStack() as ctx:
        def sem(name):
            return ctx.enter_context(nc.semaphore(name))

        BUFS = 8
        yb = [ctx.enter_context(nc.sbuf_tensor(f"gathered{i}", [LQ, 2, D], F32)) for i in range(BUFS)]
        gathered = [sem(f"gathered{i}") for i in range(BUFS)]
        first_added, added, stored = sem("first_added"), sem("both_added"), sem("out_stored")
        with nc.Block() as block:

            @block.gpsimd
            def _(pool):
                for b in range(B):
                    i = b % BUFS
                    if b >= BUFS:
                        pool.wait_ge(added, b - BUFS + 1)
                    for k in range(2):
                        nc.gpsimd.indirect_dma_start(
                            out=yb[i][:, k, :], out_offset=None, in_=ins["yg"],
                            in_offset=bass.IndirectOffsetOnAxis(ap=m.gather_at[:, k, b:b + 1], axis=0),
                            bounds_check=E * CAP - 1, oob_is_err=False).then_inc(gathered[i], 16)

            @block.vector
            def _(dve):
                for b in range(B):
                    i = b % BUFS
                    dve.wait_ge(gathered[i], 32 * (b // BUFS + 1))
                    nc.vector.scalar_tensor_tensor(m.x[:, b, :], yb[i][:, 0, :], m.weight[:, 0, b:b + 1],
                                                   m.x[:, b, :], ALU.mult, ALU.add).then_inc(first_added, 1)
                    dve.wait_ge(first_added, b + 1)
                    nc.vector.scalar_tensor_tensor(m.x[:, b, :], yb[i][:, 1, :], m.weight[:, 1, b:b + 1],
                                                   m.x[:, b, :], ALU.mult, ALU.add).then_inc(added, 1)

            @block.sync
            def _(sp):
                for c in range(NC):
                    sp.wait_ge(added, (c + 1) * CB)
                    sp.dma_start(out[c * CB:(c + 1) * CB, :, :].rearrange("b t d -> t b d"),
                                 m.x[:, c * CB:(c + 1) * CB, :]).then_inc(stored, 16)
                sp.wait_ge(stored, 16 * NC)


def build(nc, ins, out):
    with ExitStack() as ctx:
        def sb(name, shape, dt=F32):
            return ctx.enter_context(nc.sbuf_tensor(name, shape, dt))

        m = Memory()
        m.x = sb("x", [LQ, B, D])
        m.h2 = sb("h2", [LQ, B, D])
        m.proj = sb("o_projection", [LQ, B, D])
        m.logits = sb("logits", [LQ, B, E])
        m.wq, m.wk, m.wv, m.wo = (sb(n, [128, KH, D]) for n in ("wq", "wk", "wv", "wo"))
        m.gb_pre = sb("gain_offset_pre", [128, 2, KH])
        m.g_ln, m.b_ln = sb("gain_ln", [LQ, D]), sb("offset_ln", [LQ, D])
        m.wr, m.br = sb("router_w", [128, KH, E]), sb("router_b", [E, 1])
        m.gates, m.tanh = sb("gates", [128, 2]), sb("tanh_gates", [128, 2])
        m.ident, m.ident_b = sb("ident", [128, 128]), sb("ident_bf", [128, 128], BF16)
        m.headmask, m.headmask_b = sb("headmask", [128, HH]), sb("headmask_bf", [128, HH], BF16)
        m.side = sb("side", [128, 2])
        m.earlier = sb("earlier", [LQ, LQ])
        m.expert_u, m.expert_f = sb("expert_ids", [128, E], U32), sb("expert_ids_f", [128, E])
        m.ones, m.ones_b = sb("ones", [128, 128]), sb("ones_bf", [128, 128], BF16)
        m.inside = sb("inside_clip", [1, 1], U32)
        m.minus_half, m.eps = sb("minus_half", [128, 8]), sb("eps", [128, 8])
        m.mv = [sb(f"mean_var{s}", [128, KT + 1, 2]) for s in range(2)]
        m.zeros = sb("zeros", [128, RT * D])
        m.scatter_at, m.gather_at = sb("scatter_at", [LQ, 2, B], U32), sb("gather_at", [LQ, 2, B], U32)
        m.weight = sb("expert_weight", [LQ, 2, B])

        setup(nc, ins, m)
        attention(nc, ins, m)
        m.h2T = sb("h2T", [128, KH, B * LQ])
        tokens_and_logits(nc, ins, m)
        route_and_shared(nc, ins, m)
        experts(nc, ins, m)
        combine(nc, ins, m, out)


def kernel(**inputs):
    import numpy as np
    import concourse.bacc as bacc
    from concourse.bass_utils import run_bass_kernel_spmd

    nc = bacc.Bacc("TRN2", target_bir_lowering=False, num_devices=1)
    given = {
        "x": inputs["x"], "ctx": inputs["ctx_1024"], "g_xattn": inputs["g_xattn"], "g_ffn": inputs["g_ffn"],
        "g_pre": np.asarray(inputs["L0_xattn_g_pre"]).reshape(KH, 128).T,
        "b_pre": np.asarray(inputs["L0_xattn_b_pre"]).reshape(KH, 128).T,
        "g_ln": inputs["L0_xattn_g_ln"], "b_ln": inputs["L0_xattn_b_ln"],
        "wqT": np.asarray(inputs["L0_xattn_Wq"]).T, "wkT": np.asarray(inputs["L0_xattn_Wk"]).T,
        "wvT": np.asarray(inputs["L0_xattn_Wv"]).T, "woT": np.asarray(inputs["L0_xattn_Wo"]).T,
        "router_w": inputs["L0_ffn_router_w"], "router_b": inputs["L0_ffn_router_b"],
        "w_gate": inputs["L0_ffn_w_gate"], "w_up": inputs["L0_ffn_w_up"], "w_down": inputs["L0_ffn_w_down"],
        "sw_gate": inputs["L0_ffn_sw_gate"], "sw_up": inputs["L0_ffn_sw_up"], "sw_down": inputs["L0_ffn_sw_down"],
    }
    arrays, aps = {}, {}
    for name, a in given.items():
        a = np.ascontiguousarray(a)
        arrays[f"in_{name}"] = a
        aps[name] = nc.dram_tensor(f"in_{name}", a.shape, mybir.dt.from_np(a.dtype), kind="ExternalInput").ap()
    aps["xg"] = nc.dram_tensor("expert_rows", (E * CAP, D), F32, kind="Internal").ap()
    aps["yg"] = nc.dram_tensor("expert_outputs", (E * CAP, D), F32, kind="Internal").ap()
    out = nc.dram_tensor("out", (B, LQ, D), F32, kind="ExternalOutput").ap()
    build(nc, aps, out)
    return run_bass_kernel_spmd(nc, [arrays], core_ids=[0]).results[0]["out"]
```

```python
import concourse.bass as bass
from concourse import mybir
from contextlib import ExitStack

F32 = mybir.dt.float32
BF16 = mybir.dt.bfloat16
U32 = mybir.dt.uint32
ALU = mybir.AluOpType
ACT = mybir.ActivationFunctionType
X = mybir.AxisListType.X

B, LQ, LK, D = 32, 100, 361, 256
H, DH = 16, 16
KH = D // 128
HH = H // KH
HG = H // 4
KT = 3
KN = [121, 120, 120]
KOFF = [0, 121, 241]
EPS = 1e-5
TEMP = 16.0
CLIP = 10000.0 * TEMP
BOUND = 0.99 * CLIP
SHARE = 8
FAR = 1e6
E, F, CAP = 16, 352, 500
FN = [128, 128, 96]
RT, RN = 4, 125
CB = 4
CN = CB * LQ
NC = B // CB
N = B * LQ


class Memory:
    pass


def load_ctx(sp, ins, m, b, s):
    sp.dma_start(m.raw[s][0:120, :, :],
                 ins["ctx"][bass.ds(b, 1), 0:360, :].rearrange("o (p t) d -> p (o t) d", t=KT)
                 ).then_inc(m.raw_loaded[s], 16)
    sp.dma_start(m.raw[s][120:121, 0, :], ins["ctx"][bass.ds(b, 1), 360:361, :].rearrange("o p d -> p (o d)")
                 ).then_inc(m.raw_loaded[s], 16)


def setup(nc, ins, m):
    bound_loads = [
        (m.wq[:, :, :], ins["wqT"].rearrange("(k p) n -> p k n", p=128)),
        (m.wk[:, :, :], ins["wkT"].rearrange("(k p) n -> p k n", p=128)),
        (m.gb_pre[:, 0, :], ins["g_pre"]),
        (m.gb_pre[:, 1, :], ins["b_pre"]),
    ]
    loads = [
        (m.wv[:, :, :], ins["wvT"].rearrange("(k p) n -> p k n", p=128)),
        (m.wo[:, :, :], ins["woT"].rearrange("(k p) n -> p k n", p=128)),
        (m.g_ln[:, :], ins["g_ln"].partition_broadcast(LQ)),
        (m.b_ln[:, :], ins["b_ln"].partition_broadcast(LQ)),
        (m.wr[:, :, :], ins["router_w"].rearrange("(k p) n -> p k n", p=128)),
        (m.br[:, :], ins["router_b"].partition_broadcast(LQ)),
        (m.gates[:, 0:1], ins["g_xattn"].partition_broadcast(128)),
        (m.gates[:, 1:2], ins["g_ffn"].partition_broadcast(128)),
    ]
    x_loads = [(m.x[:, c * CB:(c + 1) * CB, :], ins["x"][c * CB:(c + 1) * CB, :, :].rearrange("b t d -> t b d"))
               for c in range(NC)]
    with ExitStack() as ctx:
        def sb(name, shape, dt=F32):
            return ctx.enter_context(nc.sbuf_tensor(name, shape, dt))

        def sem(name):
            return ctx.enter_context(nc.semaphore(name))

        bound_loaded, loaded, x_loaded = sem("bound_loaded"), sem("loaded"), sem("x_loaded")
        made, masks, zeroed = sem("made"), sem("masks"), sem("zeroed")
        squared, summed, bound_step = sem("squared"), sem("summed"), sem("bound_step")
        wgain = [sb(f"weight_gain_{n}", [128, KH, D]) for n in "qk"]
        wsq = [sb(f"weight_square_{n}", [128, KH, D]) for n in "qk"]
        norm2 = sb("row_norm2", [1, 2 * D])
        off = sb("row_offset", [1, 2 * D])
        off2 = sb("row_offset2", [1, 2 * D])
        size2 = sb("row_bound2", [1, 2 * D])
        heads = sb("head_sums", [1, 2, H])
        prod = sb("head_bounds", [1, H])
        largest = sb("largest_bound", [1, 1])
        inside = sb("inside_bound", [1, 1])
        np_ = ctx.enter_context(nc.psum_tensor("row_norm_psum", [128, 512], F32))
        op_ = ctx.enter_context(nc.psum_tensor("row_offset_psum", [128, 512], F32))
        block = ctx.enter_context(nc.Block())

        @block.sync
        def _(sp):
            for dst, src in bound_loads:
                sp.dma_start(dst, src).then_inc(bound_loaded, 16)
            for b in range(2):
                load_ctx(sp, ins, m, b, b)
            for dst, src in x_loads:
                sp.dma_start(dst, src).then_inc(x_loaded, 16)
            sp.wait_ge(x_loaded, 16 * len(x_loads))

        @block.gpsimd
        def _(pool):
            nc.gpsimd.memset(m.ident[:, :], 0.0).then_inc(made, 1)
            nc.gpsimd.memset(m.headmask[:, :], 1.0).then_inc(made, 1)
            nc.gpsimd.memset(m.earlier[:, :], 1.0).then_inc(made, 1)
            nc.gpsimd.iota(m.expert_u[:, :], pattern=[[1, E]], base=0, channel_multiplier=0).then_inc(made, 1)
            nc.gpsimd.iota(m.token_u[:, :, :], pattern=[[N, 2], [LQ, B]], base=0, channel_multiplier=1
                           ).then_inc(made, 1)
            pool.wait_ge(made, 5)
            nc.gpsimd.affine_select(out=m.ident[:, :], in_=m.ident[:, :], compare_op=ALU.not_equal, fill=1.0,
                                    base=0, pattern=[[-1, 128]], channel_multiplier=1).then_inc(masks, 1)
            nc.gpsimd.affine_select(out=m.headmask[:, :], in_=m.headmask[:, :], compare_op=ALU.is_ge, fill=0.0,
                                    base=0, pattern=[[-DH, HH]], channel_multiplier=1).then_inc(masks, 1)
            nc.gpsimd.affine_select(out=m.earlier[:, :], in_=m.earlier[:, :], compare_op=ALU.is_ge, fill=0.0,
                                    base=-1, pattern=[[1, LQ]], channel_multiplier=-1).then_inc(masks, 1)
            pool.wait_ge(masks, 3)
            nc.gpsimd.affine_select(out=m.headmask[:, :], in_=m.headmask[:, :], compare_op=ALU.is_ge, fill=0.0,
                                    base=DH - 1, pattern=[[DH, HH]], channel_multiplier=-1).then_inc(masks, 1)

        @block.vector
        def _(dve):
            nc.vector.memset(m.ones[:, :], 1.0)
            nc.vector.memset(m.ones_b[:, :], 1.0)
            nc.vector.memset(m.minus_half[:, :], -0.5)
            nc.vector.memset(m.eps[:, :], EPS)
            for s in range(2):
                nc.vector.memset(m.mv[s][:, :, :], 1.0)
            nc.vector.memset(m.zeros[:, :, 0:D], 0.0)
            nc.vector.memset(m.zeros[:, :, D:D + 1], FAR).then_inc(zeroed, 1)
            dve.wait_ge(masks, 4)
            nc.vector.tensor_copy(m.ident_b[:, :], m.ident[:, :])
            nc.vector.tensor_copy(m.headmask_b[:, :], m.headmask[:, :])
            for c in range(2):
                nc.vector.tensor_tensor(m.pairmask_b[:, 4 * c:4 * c + 4], m.headmask[:, 0:4], m.headmask[:, 4:8],
                                        ALU.add)
            nc.vector.tensor_copy(m.expert_f[:, :], m.expert_u[:, :])
            nc.vector.tensor_copy(m.token[:, :, :], m.token_u[:, :, :])
            nc.vector.tensor_copy(m.earlier_b[:, :], m.earlier[:, :])
            dve.wait_ge(bound_loaded, 16 * len(bound_loads))
            for i, w in enumerate((m.wq, m.wk)):
                for k in range(KH):
                    last = nc.vector.tensor_scalar(wgain[i][:, k, :], w[:, k, :], m.gb_pre[:, 0, k:k + 1], None,
                                                   ALU.mult)
            last.then_inc(squared, 1)
            dve.wait_ge(squared, 1)
            for i in range(2):
                last = nc.vector.tensor_tensor(wsq[i][:, :, :], wgain[i][:, :, :], wgain[i][:, :, :], ALU.mult)
            last.then_inc(squared, 1)
            dve.wait_ge(summed, 1)
            nc.vector.tensor_scalar(off[:, :], op_[0:1, :], 1.0, None, ALU.mult)
            nc.vector.tensor_scalar(norm2[:, :], np_[0:1, :], (1 + 1 / SHARE) * D, None, ALU.mult
                                    ).then_inc(bound_step, 1)
            dve.wait_ge(bound_step, 1)
            nc.vector.tensor_tensor(off2[:, :], off[:, :], off[:, :], ALU.mult).then_inc(bound_step, 1)
            dve.wait_ge(bound_step, 2)
            nc.vector.scalar_tensor_tensor(size2[:, :], off2[:, :], 1.0 + SHARE, norm2[:, :], ALU.mult, ALU.add
                                           ).then_inc(bound_step, 1)
            dve.wait_ge(bound_step, 3)
            nc.vector.reduce_sum(heads[:, :, :], size2[:, :].rearrange("p (w h d) -> p w h d", w=2, d=DH), axis=X
                                 ).then_inc(bound_step, 1)
            dve.wait_ge(bound_step, 4)
            nc.vector.tensor_tensor(prod[:, :], heads[:, 0, :], heads[:, 1, :], ALU.mult).then_inc(bound_step, 1)
            dve.wait_ge(bound_step, 5)
            nc.vector.reduce_max(largest[:, :], prod[:, :], axis=X).then_inc(bound_step, 1)
            dve.wait_ge(bound_step, 6)
            nc.vector.tensor_scalar(inside[:, :], largest[:, :], BOUND * BOUND, None, ALU.is_lt).then_inc(bound_step, 1)
            dve.wait_ge(bound_step, 7)
            nc.vector.tensor_copy(m.inside[:, :], inside[:, :])

        @block.tensor
        def _(pe):
            pe.wait_ge(bound_loaded, 16 * len(bound_loads))
            for i, w in enumerate((m.wq, m.wk)):
                for k in range(KH):
                    nc.tensor.matmul(op_[0:1, i * D:(i + 1) * D], m.gb_pre[:, 1, k:k + 1], w[:, k, :],
                                     start=k == 0, stop=k == KH - 1)
            pe.wait_ge(squared, 2)
            for i in range(2):
                for k in range(KH):
                    last = nc.tensor.matmul(np_[0:1, i * D:(i + 1) * D], m.ones[:, 0:1], wsq[i][:, k, :],
                                            start=k == 0, stop=k == KH - 1)
            last.then_inc(summed, 1)

        @block.scalar
        def _(act):
            for dst, src in loads:
                act.dma_start(dst, src).then_inc(loaded, 16)
            act.wait_ge(loaded, 16 * len(loads))
            nc.scalar.activation(m.tanh[:, :], m.gates[:, :], ACT.Tanh)


def attention(nc, ins, m):
    VT = 10
    OT, OP = 24, 27
    RING = 10 + H + 2
    HEADS_AT = [pos for pos in range(9, RING) if pos not in (VT, OT, OP)]
    with ExitStack() as ctx:
        def sb(name, shape, dt=F32):
            return ctx.enter_context(nc.sbuf_tensor(name, shape, dt))

        def pair(name, shape, dt=F32):
            return [sb(f"{name}{s}", shape, dt) for s in range(2)]

        def sem(name):
            return ctx.enter_context(nc.semaphore(name))

        raw, raw_loaded = m.raw, m.raw_loaded
        norm = pair("ctx_norm", [128, KT, D])
        zq = pair("x_norm", [LQ, D])
        st = pair("stats", [128, KT + 1, 6])
        st2 = pair("stats2", [LQ, 6])
        mv2 = pair("mean_var2", [LQ, 2])
        var = pair("var_eps", [128, KT + 1])
        rs = pair("rstd", [128, KT + 1])
        shift = pair("minus_mean_rstd", [128, KT])
        z1 = sb("x_once_normed", [LQ, D])
        var2 = pair("var_eps2", [LQ, 1])
        rs2 = pair("rstd2", [LQ, 1])
        qnT = sb("qnT", [128, KH, LQ])
        knT = sb("knT", [128, KH, LK])
        cT = sb("cT", [128, KH, LK])
        qd = sb("q_hi_twice", [128, KH, 2, LQ], BF16)
        ql = sb("q_lo", [128, KH, LQ], BF16)
        ks = pair("k_hi_and_lo", [128, HG, LK], BF16)
        v = pair("v", [128, KT, H, 2 * DH])
        qbh = pair("q_block_hi", [128, KH, HH, LQ], BF16)
        qbl = pair("q_block_lo", [128, KH, HH, LQ], BF16)
        mx = pair("score_max", [LQ, H])
        mxn = pair("minus_max", [LQ, H])
        mneg = pair("minus_max_bf", [LQ, H], BF16)
        mdiag = pair("minus_max_diag", [LQ, H, LQ], BF16)
        probs = pair("probs", [128, HH, LQ])
        sums = sb("sums", [128, HG, LQ])
        rden = sb("den_inv", [LQ, H])
        oraw = pair("o_raw", [LQ, D])
        ost = pair("o_stats", [LQ, 6])
        omv = pair("o_mean_var", [LQ, 2])
        ovar = pair("o_var_eps", [LQ, 1])
        ors = pair("o_rstd", [LQ, 1])
        oz = sb("o_norm", [LQ, D])
        og = sb("o_gained", [LQ, D])
        ol = pair("o_ln", [LQ, D])
        olT = sb("o_lnT", [128, KH, LQ])
        carrier_v = sb("carrier_vector", [1, 1])

        scores = ctx.enter_context(nc.psum_tensor("scores", [128, 4, 512], F32))
        ring = [ctx.enter_context(nc.psum_tensor(f"ring{s}", [128, 512], F32)) for s in range(2)]
        ob = ctx.enter_context(nc.psum_tensor("sum_bank", [128, 512], F32))
        ot = ctx.enter_context(nc.psum_tensor("sum_T_bank", [128, H, 2 * DH], F32))

        xg_zeroed, yt_zeroed = sem("xg_zeroed"), sem("yt_zeroed")
        bn_done = sem("bn_done")
        stats_done = sem("stats_done")
        rstd_step = sem("rstd_step")
        shift_done = sem("shift_done")
        z1_done = sem("z1_done")
        norm_done = sem("norm_done")
        bn2_done = sem("bn2_done")
        stats2_done = sem("stats2_done")
        rstd2_step = sem("rstd2_step")
        z2_done = sem("z2_done")
        filled = [sem(f"ring_filled{s}") for s in range(2)]
        emptied = [sem(f"ring_emptied{s}") for s in range(2)]
        qh_done, qh_twice = sem("qh_done"), sem("qh_twice_done")
        qb_done = sem("q_block_done")
        kh_done = sem("kh_done")
        max_clipped = sem("max_clipped")
        mneg_done = sem("mneg_done")
        mdiag_done = sem("mdiag_done")
        raw_done = sem("raw_scores_done")
        clipped = sem("scores_clipped")
        scores_done = sem("scores_done")
        exp_done = sem("exp_done")
        pv_done = sem("pv_done")
        ones_set = sem("v_ones_set")
        sums_taken = sem("sums_taken")
        ot_done = sem("sums_T_done")
        rden_done = sem("den_inv_done")
        oraw_done = sem("o_raw_done")
        obn_done = sem("o_bn_done")
        ostats_done = sem("o_stats_done")
        orstd_step = sem("o_rstd_step")
        oln_step = sem("o_ln_step")
        ol_done = sem("o_ln_done")
        ol_kept = sem("o_ln_kept")

        def nth(r, pos):
            if isinstance(r, int) and r < 2:
                return (RING // 2 - 1) * r + pos // 2 + 1 - (pos > OT and pos % 2 == OT % 2)
            if isinstance(r, int) and r >= B:
                return (RING // 2) * B - 2 + (r - B) + 1
            return (RING // 2) * r - 2 + pos // 2 + 1

        BETWEEN = [("score", 3, 2), ("score", 3, 3), ("sum", 2, 0), ("sum", 2, 1),
                   ("score", 4, 0), ("score", 4, 1), ("score", 4, 2), ("score", 4, 3), ("sum", 3, 0), ("sum", 3, 1),
                   ("score", 5, 0), ("score", 5, 1), ("score", 5, 2), ("score", 5, 3), ("sum", 4, 0), ("sum", 4, 1)]
        CLIP_AT = {min(h for h in range(H) if HEADS_AT[h] > 10 + i): u for i, (kind, u, part) in enumerate(BETWEEN)
                   if kind == "score" and part == 3}

        def at(h):
            return HEADS_AT[h]

        def over_batches(eng, step):
            step(-1, 1, False, False, True, False)
            step(0, 0, False, True, True, True)
            step(1, 1, True, True, True, True)
            with eng.Fori(1, B // 2 - 1) as it:
                for s in range(2):
                    step(it * 2 + s, s, True, True, True, True)
            step(B - 2, 0, True, True, True, False)
            step(B - 1, 1, True, True, False, False)
            step(B, 0, True, False, False, False)

        def either(eng, program):
            inside = eng.value_load(m.inside[0:1, 0:1], min_val=0, max_val=1)
            with eng.If(inside > 0):
                program(False)
            with eng.Else():
                program(True)

        with nc.Block() as block:

            @block.sync
            def _(sp):
                for e in range(E):
                    sp.dma_start(ins["xg"][e * CAP:(e + 1) * CAP, :].rearrange("(p t) d -> p t d", t=RT),
                                 m.zeros[0:RN, :, :]).then_inc(xg_zeroed, 16)
                for c in range(2 * NC):
                    sp.dma_start(ins["yt"][c * CN:(c + 1) * CN, :].rearrange("(p t) d -> p t d", t=CB),
                                 m.zeros[0:LQ, 0:CB, 0:D]).then_inc(yt_zeroed, 16)
                for b in range(2, 4):
                    sp.wait_ge(filled[1], nth(b - 2, 5))
                    load_ctx(sp, ins, m, b, b % 2)
                with sp.Fori(2, B // 2) as it:
                    for s in range(2):
                        sp.wait_ge(filled[1], nth(it * 2 + s - 2, 5))
                        load_ctx(sp, ins, m, it * 2 + s, s)
                sp.wait_ge(xg_zeroed, 16 * E)
                sp.wait_ge(yt_zeroed, 16 * 2 * NC)

            @block.gpsimd
            def _(pool):
                def rstd(b, s):
                    pool.wait_ge(stats_done, b + 1)
                    nc.gpsimd.tensor_tensor(var[s][:, :], m.mv[s][:, :, 1], m.eps[:, 0:KT + 1], ALU.add
                                            ).then_inc(rstd_step, 1)
                    pool.wait_ge(rstd_step, 2 * b + 1)
                    nc.gpsimd.tensor_tensor(rs[s][:, :], var[s][:, :], m.minus_half[:, 0:KT + 1],
                                            ALU.pow).then_inc(rstd_step, 1)

                def rstd_again(b, s):
                    pool.wait_ge(stats2_done, b + 1)
                    nc.gpsimd.tensor_tensor(var2[s][:, :], mv2[s][:, 1:2], m.eps[0:LQ, 0:1], ALU.add
                                            ).then_inc(rstd2_step, 1)
                    pool.wait_ge(rstd2_step, 2 * b + 1)
                    nc.gpsimd.tensor_tensor(rs2[s][:, :], var2[s][:, :], m.minus_half[0:LQ, 0:1],
                                            ALU.pow).then_inc(rstd2_step, 1)

                def q_blocks(b, s, src, dst):
                    if src is qd:
                        pool.wait_ge(qh_twice, b + 1)
                    else:
                        pool.wait_ge(emptied[1], nth(b, 3))
                    for k in range(KH):
                        if src is qd:
                            last = nc.gpsimd.tensor_tensor(
                                dst[:, k, :, :].rearrange("p (c h) q -> p c h q", c=2),
                                src[:, k, :, :].unsqueeze(2).to_broadcast([128, 2, 4, LQ]),
                                m.pairmask_b[:, :].rearrange("p (c h) -> p c h", c=2).unsqueeze(3)
                                .to_broadcast([128, 2, 4, LQ]), ALU.mult)
                        else:
                            last = nc.gpsimd.tensor_tensor(
                                dst[:, k, :, :], src[:, k, :].unsqueeze(1).to_broadcast([128, HH, LQ]),
                                m.headmask_b[:, :].unsqueeze(2).to_broadcast([128, HH, LQ]), ALU.mult)
                    last.then_inc(qb_done, 1)

                def max_diagonal(b, s, k):
                    pool.wait_ge(mneg_done, 2 * b + k + 1)
                    nc.gpsimd.tensor_tensor(
                        mdiag[s][:, HH * k:HH * (k + 1), :],
                        mneg[s][:, HH * k:HH * (k + 1)].unsqueeze(2).to_broadcast([LQ, HH, LQ]),
                        m.ident_b[0:LQ, 0:LQ].unsqueeze(1).to_broadcast([LQ, HH, LQ]),
                        ALU.mult).then_inc(mdiag_done, 1)

                def o_rstd(b, s):
                    pool.wait_ge(ostats_done, b + 1)
                    nc.gpsimd.tensor_tensor(ovar[s][:, :], omv[s][:, 1:2], m.eps[0:LQ, 0:1], ALU.add
                                            ).then_inc(orstd_step, 1)
                    pool.wait_ge(orstd_step, 2 * b + 1)
                    nc.gpsimd.tensor_tensor(ors[s][:, :], ovar[s][:, :], m.minus_half[0:LQ, 0:1],
                                            ALU.pow).then_inc(orstd_step, 1)

                def step(b, s, prev, this, following, after):
                    if following:
                        q_blocks(b + 1, 1 - s, qd, qbh[1 - s])
                    if prev:
                        o_rstd(b - 1, 1 - s)
                    if after:
                        rstd(b + 2, s)
                    if following:
                        q_blocks(b + 1, 1 - s, ql, qbl[1 - s])
                    if after:
                        rstd_again(b + 2, s)
                    if following:
                        for k in range(KH):
                            max_diagonal(b + 1, 1 - s, k)

                for s in range(2):
                    for t in range(KT):
                        last = nc.gpsimd.memset(v[s][:, t, :, DH:2 * DH], 1.0)
                last.then_inc(ones_set, 1)
                for b in range(2):
                    rstd(b, b)
                    rstd_again(b, b)
                over_batches(pool, step)

            @block.vector
            def _(dve):
                def after_wait(semaphore, count):
                    dve.wait_ge(semaphore, count)
                    nc.vector.memset(carrier_v[:, :], 0.0)

                def statistics(b, s, use):
                    dve.wait_ge(raw_loaded[s], 32 * (use + 1))
                    for t in range(KT):
                        nc.vector.bn_stats(st[s][0:KN[t], t, :], raw[s][0:KN[t], t, :])
                    nc.vector.bn_stats(st[s][0:LQ, KT, :], m.x[:, bass.ds(b, 1), :].rearrange("p o d -> p (o d)")
                                       ).then_inc(bn_done, 1)
                    after_wait(bn_done, b + 1)
                    for t in range(KT):
                        nc.vector.bn_aggr(m.mv[s][0:KN[t], t, :], st[s][0:KN[t], t, :])
                    nc.vector.bn_aggr(m.mv[s][0:LQ, KT, :], st[s][0:LQ, KT, :]).then_inc(stats_done, 1)

                def statistics_again(b, s):
                    dve.wait_ge(rstd_step, 2 * b + 2)
                    nc.vector.scalar_tensor_tensor(shift[s][:, :], m.mv[s][:, 0:KT, 0], -1.0, rs[s][:, 0:KT],
                                                   ALU.mult, ALU.mult).then_inc(shift_done, 1)
                    nc.vector.tensor_scalar(z1[:, :], m.x[:, bass.ds(b, 1), :].rearrange("p o d -> p (o d)"),
                                            m.mv[s][0:LQ, KT, 0:1], rs[s][0:LQ, KT:KT + 1],
                                            ALU.subtract, ALU.mult).then_inc(z1_done, 1)
                    dve.wait_ge(z1_done, b + 1)
                    nc.vector.bn_stats(st2[s][:, :], z1[:, :]).then_inc(bn2_done, 1)
                    after_wait(bn2_done, b + 1)
                    nc.vector.bn_aggr(mv2[s][:, :], st2[s][:, :]).then_inc(stats2_done, 1)

                def normalise_again(b, s):
                    dve.wait_ge(rstd2_step, 2 * b + 2)
                    nc.vector.tensor_scalar(zq[s][:, :], z1[:, :], mv2[s][:, 0:1], rs2[s][:, :],
                                            ALU.subtract, ALU.mult).then_inc(z2_done, 1)

                def affine(b, pos, dst, n, halves):
                    dve.wait_ge(filled[pos % 2], nth(b, pos))
                    for i, k in enumerate(halves):
                        last = nc.vector.tensor_scalar(dst[:, k, :], ring[pos % 2][:, i * n:(i + 1) * n],
                                                       m.gb_pre[:, 0, k:k + 1], m.gb_pre[:, 1, k:k + 1],
                                                       ALU.mult, ALU.add)
                    last.then_inc(emptied[pos % 2], 1)

                def own(c):
                    return slice(64 * c, 64 * c + 64)

                def q_low(b):
                    dve.wait_ge(filled[1], nth(b, 3))
                    dve.wait_ge(qh_done, b + 1)
                    for c in range(2):
                        last = nc.vector.tensor_tensor(
                            ql[own(c), :, :], ring[1][own(c), 0:KH * LQ].rearrange("p (k q) -> p k q", k=KH),
                            qd[own(c), :, c, :], ALU.subtract)
                    last.then_inc(emptied[1], 1)

                def k_low(b, s, k):
                    dve.wait_ge(filled[k], nth(b, 6 + k))
                    for c in range(2):
                        dve.wait_ge(kh_done, 4 * b + 2 * k + c + 1)
                        last = nc.vector.tensor_tensor(ks[s][own(1 - c), 2 * k + c, :], ring[k][own(c), 0:LK],
                                                       ks[s][own(c), 2 * k + c, :], ALU.subtract)
                    last.then_inc(emptied[k], 1)

                def clip(b, u):
                    k, t = u // KT, u % KT
                    dve.wait_ge(raw_done, 6 * b + u + 1)
                    bank = scores[0:KN[t], 2 * (u % 2):2 * (u % 2) + 2, 0:4 * LQ]
                    nc.vector.tensor_scalar(bank, bank, CLIP, -CLIP, ALU.min, ALU.max).then_inc(clipped, 1)

                def minus_max(b, s, k, stage):
                    half = slice(HH * k, HH * (k + 1))
                    if stage == 0:
                        for pos in (at(HH * (k + 1) - 2), at(HH * (k + 1) - 1)):
                            dve.wait_ge(emptied[pos % 2], nth(b, pos))
                        nc.vector.tensor_scalar(mxn[s][:, half], mx[s][:, half], -1.0, CLIP, ALU.mult, ALU.min
                                                ).then_inc(max_clipped, 1)
                    else:
                        dve.wait_ge(max_clipped, 2 * b + k + 1)
                        nc.vector.tensor_scalar(mneg[s][:, half], mxn[s][:, half], -CLIP, None, ALU.max
                                                ).then_inc(mneg_done, 1)

                def maxima(b, s, k, clips, heads=range(HH)):
                    for h in range(HH * k + heads[0], HH * k + heads[-1] + 1):
                        if h == HH + 2:
                            minus_max(b, s, 0, 0)
                        if h == HH + 3:
                            minus_max(b, s, 0, 1)
                        if clips is not None and h in CLIP_AT:
                            clip(clips, CLIP_AT[h])
                        pos = at(h)
                        dve.wait_ge(filled[pos % 2], nth(b, pos))
                        nc.vector.reduce_max(mx[s][:, h:h + 1], ring[pos % 2][0:LQ, 0:LK], axis=X
                                             ).then_inc(emptied[pos % 2], 1)
                    if k:
                        minus_max(b, s, 1, 0)
                        minus_max(b, s, 1, 1)

                def take_sums(b):
                    dve.wait_ge(pv_done, 6 * b + 6)
                    nc.vector.tensor_copy(sums[:, :, :].rearrange("p g q -> p (g q)"), ob[:, 0:HG * LQ]
                                          ).then_inc(sums_taken, 1)

                def divide(b, s):
                    dve.wait_ge(ot_done, b + 1)
                    nc.vector.reciprocal(rden[:, :], ot[0:LQ, :, DH]).then_inc(rden_done, 1)
                    dve.wait_ge(rden_done, b + 1)
                    nc.vector.tensor_tensor(oraw[s][:, :].rearrange("p (h d) -> p h d", d=DH), ot[0:LQ, :, 0:DH],
                                            rden[:, :].unsqueeze(2).to_broadcast([LQ, H, DH]), ALU.mult
                                            ).then_inc(oraw_done, 1)

                def o_statistics(b, s):
                    dve.wait_ge(oraw_done, b + 1)
                    nc.vector.bn_stats(ost[s][:, :], oraw[s][:, :]).then_inc(obn_done, 1)
                    after_wait(obn_done, b + 1)
                    nc.vector.bn_aggr(omv[s][:, :], ost[s][:, :]).then_inc(ostats_done, 1)

                def o_normalise(b, s):
                    dve.wait_ge(orstd_step, 2 * b + 2)
                    nc.vector.tensor_scalar(oz[:, :], oraw[s][:, :], omv[s][:, 0:1], ors[s][:, :],
                                            ALU.subtract, ALU.mult).then_inc(oln_step, 1)
                    dve.wait_ge(oln_step, 2 * b + 1)
                    nc.vector.tensor_tensor(og[:, :], oz[:, :], m.g_ln[:, :], ALU.mult).then_inc(oln_step, 1)
                    dve.wait_ge(oln_step, 2 * b + 2)
                    if not (isinstance(b, int) and b < 2):
                        dve.wait_ge(ol_kept, b - 1)
                    nc.vector.tensor_tensor(ol[s][:, :], og[:, :], m.b_ln[:, :], ALU.add).then_inc(ol_done, 1)

                def step(b, s, prev, this, following, after, clips):
                    n = 1 - s
                    clips = clips and this
                    if following:
                        affine(b + 1, 0, qnT, LQ, range(KH))
                    if clips:
                        clip(b, 0)
                    if prev:
                        take_sums(b - 1)
                    if following:
                        affine(b + 1, 1, knT, LK, [0])
                        affine(b + 1, 2, knT, LK, [1])
                    if following:
                        q_low(b + 1)
                    if clips:
                        clip(b, 1)
                    if prev:
                        divide(b - 1, n)
                    if prev:
                        o_statistics(b - 1, n)
                    if after:
                        statistics(b + 2, s, (b + 2 - s) // 2)
                    if following:
                        k_low(b + 1, n, 0)
                    if clips:
                        clip(b, 2)
                    if following:
                        k_low(b + 1, n, 1)
                    if prev:
                        o_normalise(b - 1, n)
                    if following:
                        maxima(b + 1, n, 0, b if clips else None, range(0, 1))
                    if after:
                        statistics_again(b + 2, s)
                    if following:
                        maxima(b + 1, n, 0, b if clips else None, range(1, HH))
                    if after:
                        normalise_again(b + 2, s)
                    if following:
                        maxima(b + 1, n, 1, b if clips else None)
                    elif clips:
                        for u in range(3, 6):
                            clip(b, u)

                for b in range(2):
                    statistics(b, b, 0)
                    statistics_again(b, b)
                    normalise_again(b, b)
                either(dve, lambda clips: over_batches(dve, lambda *a: step(*a, clips)))

            @block.scalar
            def _(act):
                def evacuate(b, pos, dst, src):
                    act.wait_ge(filled[pos % 2], nth(b, pos))
                    nc.scalar.activation(dst, src, ACT.Copy).then_inc(emptied[pos % 2], 1)

                def q_high(b):
                    act.wait_ge(filled[1], nth(b, 3))
                    for c in range(2):
                        last = nc.scalar.activation(qd[64 * c:64 * c + 64, :, c, :],
                                                    ring[1][64 * c:64 * c + 64, 0:KH * LQ]
                                                    .rearrange("p (k q) -> p k q", k=KH), ACT.Copy)
                    last.then_inc(qh_done, 1)

                def q_high_again(b):
                    act.wait_ge(qh_done, b + 1)
                    for c in range(2):
                        last = nc.scalar.activation(qd[64 * (1 - c):64 * (1 - c) + 64, :, c, :],
                                                    qd[64 * c:64 * c + 64, :, c, :], ACT.Copy)
                    last.then_inc(qh_twice, 1)

                def k_high(b, s, k):
                    act.wait_ge(filled[k], nth(b, 6 + k))
                    for c in range(2):
                        own = slice(64 * c, 64 * c + 64)
                        nc.scalar.activation(ks[s][own, 2 * k + c, :], ring[k][own, 0:LK], ACT.Copy).then_inc(kh_done, 1)

                def exps(b, u):
                    k, t = u // KT, u % KT
                    act.wait_ge(scores_done, 6 * b + u + 1)
                    if not (isinstance(b, int) and b == 0 and u < 2):
                        act.wait_ge(pv_done, 6 * b + u - 1)
                    nc.scalar.activation(probs[u % 2][0:KN[t], :, :].rearrange("p (c h) q -> p c (h q)", c=2),
                                         scores[0:KN[t], 2 * (u % 2):2 * (u % 2) + 2, 0:4 * LQ],
                                         ACT.Exp, scale=1.0 / TEMP).then_inc(exp_done, 1)

                def normalise(b, s):
                    act.wait_ge(shift_done, b + 1)
                    if not (isinstance(b, int) and b < 2):
                        act.wait_ge(filled[0], nth(b - 2, 2))
                    for t in range(KT):
                        last = nc.scalar.activation(norm[s][0:KN[t], t, :], raw[s][0:KN[t], t, :], ACT.Identity,
                                                    bias=shift[s][0:KN[t], t:t + 1], scale=rs[s][0:KN[t], t:t + 1])
                    last.then_inc(norm_done, 1)

                def batch(t, b):
                    return t[:, bass.ds(b, 1), 0:D].rearrange("p o d -> p (o d)")

                def step(b, s, prev, this, following, after):
                    n = 1 - s
                    if this:
                        exps(b, 0)
                    if following:
                        if not (isinstance(b, int) and b == -1):
                            act.wait_ge(qb_done, 2 * b + 2)
                        q_high(b + 1)
                    if this:
                        exps(b, 1)
                    if following:
                        evacuate(b + 1, 4, cT[:, 0, :], ring[0][:, 0:LK])
                        q_high_again(b + 1)
                        evacuate(b + 1, 5, cT[:, 1, :], ring[1][:, 0:LK])
                        k_high(b + 1, n, 0)
                    if this:
                        exps(b, 2)
                    if following:
                        k_high(b + 1, n, 1)
                        evacuate(b + 1, 8, v[n][0:KN[0], 0, :, 0:DH],
                                 ring[0][0:KN[0], 0:D].rearrange("p (h d) -> p h d", d=DH))
                        evacuate(b + 1, VT, v[n][0:KN[1], 1:3, :, 0:DH].rearrange("p t h d -> p (t h) d"),
                                 ring[VT % 2][0:KN[1], 0:2 * D].rearrange("p (h d) -> p h d", d=DH))
                    if this:
                        exps(b, 3)
                    if after:
                        normalise(b + 2, s)
                    if this:
                        exps(b, 4)
                    if prev:
                        evacuate(b + 1, OT, olT[:, :, :].rearrange("p k q -> p (k q)"), ring[OT % 2][:, 0:KH * LQ])
                    if this:
                        exps(b, 5)
                    if prev:
                        evacuate(b + 1, OP, batch(m.proj, b - 1), ring[OP % 2][0:LQ, 0:D])
                        nc.scalar.activation(batch(m.h2, b - 1), ol[n][:, :], ACT.Copy).then_inc(ol_kept, 1)

                for b in range(2):
                    normalise(b, b)
                over_batches(act, step)

            @block.tensor
            def _(pe):
                def free_ring(b, pos):
                    if not (isinstance(b, int) and b == 0 and pos < 2):
                        pe.wait_ge(emptied[pos % 2], nth(b, pos) - 1)

                def transpose_x(b, s):
                    pe.wait_ge(z2_done, b + 1)
                    free_ring(b, 0)
                    for k in range(KH):
                        last = nc.tensor.transpose(ring[0][:, k * LQ:(k + 1) * LQ], zq[s][:, k * 128:(k + 1) * 128],
                                                   m.ident[0:LQ, 0:LQ])
                    last.then_inc(filled[0], 1)

                def transpose_ctx(b, pos, src, k, ready):
                    if ready is not None:
                        pe.wait_ge(ready, b + 1)
                    free_ring(b, pos)
                    for t in range(KT):
                        last = nc.tensor.transpose(ring[pos % 2][:, KOFF[t]:KOFF[t] + KN[t]],
                                                   src[0:KN[t], t, k * 128:(k + 1) * 128],
                                                   m.ident[0:KN[t], 0:KN[t]])
                    last.then_inc(filled[pos % 2], 1)

                def project(b, pos, w, src, mts, n, inputs):
                    for p in inputs:
                        pe.wait_ge(emptied[p % 2], nth(b, p))
                    free_ring(b, pos)
                    for i, mt in enumerate(mts):
                        for k in range(KH):
                            last = nc.tensor.matmul(ring[pos % 2][:, i * n:(i + 1) * n],
                                                    w[:, k, mt * 128:(mt + 1) * 128], src[:, k, :],
                                                    start=k == 0, stop=k == KH - 1)
                    last.then_inc(filled[pos % 2], 1)

                def project_v(b, pos, tiles):
                    if pos == 8:
                        pe.wait_ge(emptied[1], nth(b, 5))
                    free_ring(b, pos)
                    for i, t in enumerate(tiles):
                        for k in range(KH):
                            last = nc.tensor.matmul(ring[pos % 2][0:KN[t], i * D:(i + 1) * D],
                                                    cT[:, k, KOFF[t]:KOFF[t] + KN[t]], m.wv[:, k, :],
                                                    start=k == 0, stop=k == KH - 1)
                    last.then_inc(filled[pos % 2], 1)

                def scores_for_max(b, s, h, clips):
                    pos = at(h)
                    k, j = h // HH, h % HH
                    pe.wait_ge(qb_done, 2 * b + 1)
                    if pos % 2 != k:
                        pe.wait_ge(emptied[k], nth(b, 6 + k))
                    free_ring(b, pos)
                    bank = ring[pos % 2][0:LQ, 0:LK]
                    keys = ks[s][:, h // 4, :]
                    if clips:
                        if h == 0:
                            pe.wait_ge(qb_done, 2 * b + 2)
                        nc.tensor.matmul(bank, qbl[s][:, k, j, :], keys, start=True, stop=False)
                    nc.tensor.matmul(bank, qbh[s][:, k, j, :], keys, start=not clips, stop=True
                                     ).then_inc(filled[pos % 2], 1)

                def score_part(b, s, u, part, clips):
                    k, t = u // KT, u % KT
                    c = part // 2
                    if part == 0:
                        if u % KT == 0:
                            pe.wait_ge(qb_done, 2 * b + 2)
                            pe.wait_ge(emptied[k], nth(b, 6 + k))
                            pe.wait_ge(mdiag_done, 2 * b + k + 1)
                        if not (isinstance(b, int) and b == 0 and u < 2):
                            pe.wait_ge(exp_done, 6 * b + u - 1)
                    keys = slice(KOFF[t], KOFF[t] + KN[t])
                    banks = [scores[0:KN[t], 2 * (u % 2) + i, 0:4 * LQ] for i in range(2)]
                    heads = slice(4 * c, 4 * c + 4)

                    def minus_max(c):
                        return nc.tensor.matmul(banks[c], m.ones_b[0:LQ, 0:KN[t]],
                                                mdiag[s][:, HH * k + 4 * c:HH * k + 4 * c + 4, :],
                                                start=False, stop=True, skip_group_check=clips)

                    group = 2 * k + c
                    if part % 2 == 0:
                        nc.tensor.matmul(banks[c], ks[s][:, group, keys], qbh[s][:, k, heads, :], start=True, stop=False)
                        return
                    last = nc.tensor.matmul(banks[c], ks[s][:, group, keys], qbl[s][:, k, heads, :],
                                            start=False, stop=clips)
                    if not clips:
                        last = minus_max(c)
                    elif part == 3:
                        last.then_inc(raw_done, 1)
                        pe.wait_ge(clipped, 6 * b + u + 1)
                        minus_max(0)
                        last = minus_max(1)
                    if part == 3:
                        last.then_inc(scores_done, 1)

                def score_unit(b, s, u, clips):
                    for part in range(4):
                        score_part(b, s, u, part, clips)

                def weighted_part(b, s, u, part):
                    k, t = u // KT, u % KT
                    if part == 0:
                        pe.wait_ge(exp_done, 6 * b + u + 1)
                        if u == 0:
                            pe.wait_ge(emptied[VT % 2], nth(b, VT))
                            if not (isinstance(b, int) and b == 0):
                                pe.wait_ge(sums_taken, b)
                    group = 2 * k + part
                    for g in range(4):
                        last = nc.tensor.matmul(ob[32 * g:32 * g + 32, group * LQ:(group + 1) * LQ],
                                                v[s][0:KN[t], t, 4 * group + g, :],
                                                probs[u % 2][0:KN[t], 4 * part + g, :],
                                                start=t == 0 and part == 0, stop=t == KT - 1 and part == 1)
                    if part:
                        last.then_inc(pv_done, 1)

                def transpose_o(b):
                    pe.wait_ge(sums_taken, b + 1)
                    if not (isinstance(b, int) and b == 0):
                        pe.wait_ge(oraw_done, b)
                    for g in range(HG):
                        last = nc.tensor.transpose(ot[0:LQ, 4 * g:4 * g + 4, :].rearrange("p h d -> p (h d)"),
                                                   sums[:, g, :], m.ident[:, :])
                    last.then_inc(ot_done, 1)

                def transpose_o_ln(b, s, r):
                    pe.wait_ge(ol_done, b + 1)
                    free_ring(r, OT)
                    for k in range(KH):
                        last = nc.tensor.transpose(ring[OT % 2][:, k * LQ:(k + 1) * LQ],
                                                   ol[s][:, k * 128:(k + 1) * 128], m.ident[0:LQ, 0:LQ])
                    last.then_inc(filled[OT % 2], 1)

                def project_o(b, s, r):
                    pe.wait_ge(emptied[OT % 2], nth(r, OT))
                    free_ring(r, OP)
                    for k in range(KH):
                        last = nc.tensor.matmul(ring[OP % 2][0:LQ, 0:D], olT[:, k, :], m.wo[:, k, :],
                                                start=k == 0, stop=k == KH - 1)
                    last.then_inc(filled[OP % 2], 1)

                def step(b, s, prev, this, following, after, clips):
                    n = 1 - s
                    if following:
                        transpose_x(b + 1, n)
                    if prev:
                        for part in range(2):
                            weighted_part(b - 1, n, 5, part)
                    if following:
                        transpose_ctx(b + 1, 1, norm[n], 0, norm_done)
                    if this:
                        score_unit(b, s, 0, clips)
                    if following:
                        transpose_ctx(b + 1, 2, norm[n], 1, None)
                    if this:
                        score_part(b, s, 1, 0, clips)
                        score_part(b, s, 1, 1, clips)
                    if following:
                        project(b + 1, 3, m.wq, qnT, range(KH), LQ, [0])
                    if this:
                        score_part(b, s, 1, 2, clips)
                        score_part(b, s, 1, 3, clips)
                    if following:
                        transpose_ctx(b + 1, 4, raw[n], 0, None)
                    if prev:
                        transpose_o(b - 1)
                    if following:
                        transpose_ctx(b + 1, 5, raw[n], 1, None)
                        project(b + 1, 6, m.wk, knT, [0], LK, [1])
                    if this:
                        weighted_part(b, s, 0, 0)
                        weighted_part(b, s, 0, 1)
                        score_unit(b, s, 2, clips)
                    if following:
                        project(b + 1, 7, m.wk, knT, [1], LK, [])
                        project_v(b + 1, 8, [0])
                    if this:
                        weighted_part(b, s, 1, 0)
                        weighted_part(b, s, 1, 1)
                        score_part(b, s, 3, 0, clips)
                        score_part(b, s, 3, 1, clips)
                    if following:
                        scores_for_max(b + 1, n, 0, clips)
                    for i in range(10, RING):
                        if following and i == VT:
                            project_v(b + 1, VT, [1, 2])
                        elif following and i not in (OT, OP):
                            scores_for_max(b + 1, n, HEADS_AT.index(i), clips)
                        if prev and i == OT:
                            transpose_o_ln(b - 1, n, b + 1)
                        if prev and i == OP:
                            project_o(b - 1, n, b + 1)
                        if this and i - 10 < len(BETWEEN):
                            kind, u, part = BETWEEN[i - 10]
                            if kind == "score":
                                score_part(b, s, u, part, clips)
                            else:
                                weighted_part(b, s, u, part)

                pe.wait_ge(ones_set, 1)
                either(pe, lambda clips: over_batches(pe, lambda *a: step(*a, clips)))


def mlp_weights(nc, ctx, name):
    return (ctx.enter_context(nc.sbuf_tensor(f"{name}_gate", [128, KH, F], F32)),
            ctx.enter_context(nc.sbuf_tensor(f"{name}_up", [128, KH, F], F32)),
            ctx.enter_context(nc.sbuf_tensor(f"{name}_down", [128, len(FN), D], F32)))


def tokens(nc, ins, m):
    NF = len(FN)
    with ExitStack() as ctx:
        def sb(name, shape, dt=F32):
            return ctx.enter_context(nc.sbuf_tensor(name, shape, dt))

        def pair(name, shape, dt=F32):
            return [sb(f"{name}{s}", shape, dt) for s in range(2)]

        def psum(name, shape):
            return ctx.enter_context(nc.psum_tensor(name, shape, F32))

        def sem(name):
            return ctx.enter_context(nc.semaphore(name))

        st = sb("h_stats", [LQ, CB, 6])
        carrier = sb("h_carrier", [1, 1])
        mv = pair("h_mean_var", [LQ, CB, 2])
        var = pair("h_var_eps", [LQ, CB])
        rs = pair("h_rstd", [LQ, CB])
        h = pair("h_chunk", [LQ, CB, D])
        hT = pair("h_T", [128, KH, CN])
        ge = pair("gelu", [LQ, CB, D])
        y = pair("attention_out", [LQ, CB, D])
        lg = sb("logits", [LQ, CB, E])
        top = sb("logit_max", [LQ, CB])
        below = sb("logits_minus_max", [LQ, CB, E])
        ex = sb("logits_exp", [LQ, CB, E])
        total = sb("exp_sum", [LQ, CB])
        pr = sb("router_probs", [LQ, CB, E])
        v8 = sb("best_values", [LQ, CB, 8])
        i8 = sb("best_experts", [LQ, CB, 8], U32)
        idx = sb("experts2", [LQ, 2, CB])
        oh = sb("one_hot", [LQ, 2, CB, E])
        chosen = sb("chosen", [LQ, CB, E], BF16)
        extra = sb("chosen_sum", [LQ, E])
        run = pair("chosen_before", [LQ, E])
        run_b = sb("chosen_before_bf", [LQ, E], BF16)
        at = sb("positions_at", [LQ, 2, CB, E])
        pos = sb("position", [LQ, 2, CB])
        within = sb("within", [LQ, 2, CB])
        slot = sb("slot", [LQ, 2, CB])
        far = sb("far", [LQ, 2, CB])
        inverse = sb("exp_sum_inv", [LQ, CB])
        den, den_eps, den_inv = (sb(f"weight_sum{n}", [LQ, CB]) for n in ("", "_eps", "_inv"))
        wn = sb("weight_norm", [LQ, 2, CB])
        wg, wu, wd = mlp_weights(nc, ctx, "shared")
        sg = pair("shared_silu", [128, CN])
        hid = pair("shared_hidden", [128, NF, CN])

        gp = [psum(f"gate_psum{s}", [128, 512]) for s in range(2)]
        up = [psum(f"up_psum{s}", [128, 512]) for s in range(2)]
        dn = psum("down_psum", [128, 2, D])
        tp = [psum(f"hT_psum{k}", [128, 512]) for k in range(KH)]
        pp = psum("positions_psum", [128, 512])
        lpart, ppart = tp[0][0:LQ, CN:CN + CB * E], pp[0:LQ, 0:CB * E]

        w_loaded = sem("shared_loaded")
        gelu_done, y_done, x1_done = sem("gelu_done"), sem("y_done"), sem("x1_done")
        bn_done, stats_done, rstd_step = sem("h_bn_done"), sem("h_stats_done"), sem("h_rstd_step")
        h_done, base_done, h_kept = sem("h_done"), sem("base_done"), sem("h_kept")
        t_done, t_emptied, logits_done = sem("h_t_done"), sem("h_t_emptied"), sem("logits_done")
        r, below_done, exp_done = sem("route_step"), sem("below_max_done"), sem("router_exp_done")
        chosen_done, counted, routed = sem("chosen_done"), sem("counted"), sem("routed")
        scattered = sem("scattered")
        gu_done, silu_done, hid_done = sem("gate_up_done"), sem("silu_done"), sem("hidden_done")
        down_done, added = sem("down_done"), sem("shared_added")

        def batches(t, c):
            return t[:, bass.ds(c * CB, CB), 0:D]

        def batch(t, c, j):
            return t[:, bass.ds(c * CB + j, 1), 0:D].rearrange("p o d -> p (o d)")

        def over_chunks(eng, step):
            for c in range(2):
                step(c, c % 2, True, c > 0)
            with eng.Fori(1, NC // 2 - 1) as it:
                for s in range(2):
                    step(it * 2 + s, s, True, True)
            for c in range(NC - 2, NC + 1):
                step(c, c % 2, c < NC, True)

        def after_first(c, n=1):
            return not (isinstance(c, int) and c < n)

        with nc.Block() as block:

            @block.sync
            def _(sp):
                load_mlp(sp, (wg, wu, wd), ins["sw_gate"], ins["sw_up"], ins["sw_down"], w_loaded)
                for e in range(2):
                    load_expert(sp, ins, m, e, e)
                sp.wait_ge(w_loaded, 16 * MLP_LOADS)

            @block.vector
            def _(dve):
                def statistics(c, s):
                    dve.wait_ge(y_done, c + 1)
                    nc.vector.scalar_tensor_tensor(batches(m.x, c), y[s][:, :, :], m.tanh[0:LQ, 0:1],
                                                   batches(m.x, c), ALU.mult, ALU.add).then_inc(x1_done, 1)
                    dve.wait_ge(x1_done, c + 1)
                    nc.vector.memset(carrier[:, :], 0.0)
                    for j in range(CB):
                        last = nc.vector.bn_stats(st[:, j, :], batch(m.x, c, j))
                    last.then_inc(bn_done, 1)
                    dve.wait_ge(bn_done, c + 1)
                    nc.vector.memset(carrier[:, :], 0.0)
                    for j in range(CB):
                        last = nc.vector.bn_aggr(mv[s][:, j, :], st[:, j, :])
                    last.then_inc(stats_done, 1)

                def normalise(c, s):
                    dve.wait_ge(rstd_step, 2 * c + 2)
                    if after_first(c, 2):
                        dve.wait_ge(t_done, c - 1)
                        dve.wait_ge(h_kept, c - 1)
                    for j in range(CB):
                        last = nc.vector.tensor_scalar(h[s][:, j, :], batch(m.x, c, j), mv[s][:, j, 0:1],
                                                       rs[s][:, j:j + 1], ALU.subtract, ALU.mult)
                    last.then_inc(h_done, 1)

                def base(c, s):
                    dve.wait_ge(h_done, c + 1)
                    nc.vector.scalar_tensor_tensor(batches(m.x, c), h[s][:, :, :], m.tanh[0:LQ, 1:2],
                                                   batches(m.x, c), ALU.mult, ALU.add).then_inc(base_done, 1)

                def wide(t):
                    return t.unsqueeze(2).to_broadcast([LQ, CB, E])

                STEPS = 19

                def then(c, i, ins_, carry=False):
                    ins_.then_inc(r, 1)
                    dve.wait_ge(r, STEPS * c + i)
                    if carry:
                        nc.vector.memset(carrier[:, :], 0.0)

                def below_max(c):
                    dve.wait_ge(logits_done, c + 1)
                    then(c, 1, nc.vector.tensor_tensor(lg[:, :, :], lpart.rearrange("p (j e) -> p j e", e=E),
                                                       m.br[:, :].unsqueeze(1).to_broadcast([LQ, CB, E]), ALU.add))
                    then(c, 2, nc.vector.reduce_max(top[:, :], lg[:, :, :], axis=X))
                    nc.vector.tensor_tensor(below[:, :, :], lg[:, :, :], wide(top[:, :]), ALU.subtract
                                            ).then_inc(below_done, 1)

                def choose(c):
                    dve.wait_ge(exp_done, c + 1)
                    then(c, 3, nc.vector.reduce_sum(total[:, :], ex[:, :, :], axis=X))
                    then(c, 4, nc.vector.reciprocal(inverse[:, :], total[:, :]))
                    then(c, 5, nc.vector.tensor_tensor(pr[:, :, :], ex[:, :, :], wide(inverse[:, :]), ALU.mult), True)
                    for j in range(CB):
                        last = nc.vector.max(v8[:, j, :], pr[:, j, :])
                    then(c, 6, last, True)
                    for j in range(CB):
                        last = nc.vector.max_index(i8[:, j, :], v8[:, j, :], pr[:, j, :])
                    then(c, 7, last)
                    then(c, 8, nc.vector.tensor_copy(idx[:, :, :], i8[:, :, 0:2].rearrange("p b k -> p k b")))
                    for k in range(2):
                        last = nc.vector.tensor_tensor(oh[:, k, :, :], wide(idx[:, k, :]),
                                                       m.expert_f[0:LQ, :].unsqueeze(1).to_broadcast([LQ, CB, E]),
                                                       ALU.is_equal)
                    then(c, 9, last)
                    nc.vector.tensor_tensor(chosen[:, :, :], oh[:, 0, :, :], oh[:, 1, :, :], ALU.add
                                            ).then_inc(chosen_done, 1)

                def place(c, s):
                    dve.wait_ge(chosen_done, c + 1)
                    then(c, 10, nc.vector.reduce_sum(extra[:, :], chosen[:, :, :].rearrange("p j e -> p e j"), axis=X))
                    dve.wait_ge(counted, c + 1)
                    nc.vector.tensor_tensor(run[1 - s][:, :], run[s][:, :], extra[:, :], ALU.add)
                    for k in range(2):
                        last = nc.vector.tensor_tensor(at[:, k, :, :], oh[:, k, :, :],
                                                       ppart.rearrange("p (j e) -> p j e", e=E), ALU.mult)
                    then(c, 11, last)
                    nc.vector.tensor_copy(run_b[:, :], run[1 - s][:, :])
                    then(c, 12, nc.vector.reduce_sum(pos[:, :, :], at[:, :, :, :], axis=X))
                    nc.vector.tensor_scalar(within[:, :, :], pos[:, :, :], float(CAP), None, ALU.is_lt)
                    then(c, 13, nc.vector.scalar_tensor_tensor(slot[:, :, :], idx[:, :, :], float(CAP), pos[:, :, :],
                                                               ALU.mult, ALU.add))
                    then(c, 14, nc.vector.tensor_scalar(far[:, :, :], within[:, :, :], -FAR, FAR, ALU.mult, ALU.add))
                    nc.vector.tensor_tensor(m.scatter_at[:, :, bass.ds(c * CB, CB)], slot[:, :, :], far[:, :, :],
                                            ALU.add).then_inc(routed, 1)
                    then(c, 15, nc.vector.tensor_tensor(den[:, :], v8[:, :, 0], v8[:, :, 1], ALU.add))
                    then(c, 16, nc.vector.tensor_scalar(den_eps[:, :], den[:, :], 1e-9, None, ALU.add))
                    then(c, 17, nc.vector.reciprocal(den_inv[:, :], den_eps[:, :]))
                    then(c, 18, nc.vector.tensor_tensor(wn[:, :, :], v8[:, :, 0:2].rearrange("p b k -> p k b"),
                                                        den_inv[:, :].unsqueeze(1).to_broadcast([LQ, 2, CB]),
                                                        ALU.mult))
                    then(c, 19, nc.vector.scalar_tensor_tensor(m.weight[:, :, bass.ds(c * CB, CB)], wn[:, :, :],
                                                               m.tanh[0:LQ, 1:2], within[:, :, :],
                                                               ALU.mult, ALU.mult))

                def hidden(c, s, f):
                    n = NF * c + f
                    dve.wait_ge(silu_done, n + 1)
                    if f == 0 and after_first(c, 2):
                        dve.wait_ge(down_done, 2 * c - 2)
                    q = (f + s) % 2
                    nc.vector.tensor_tensor(hid[s][0:FN[f], f, :], sg[q][0:FN[f], :], up[q][0:FN[f], 0:CN],
                                            ALU.mult).then_inc(hid_done, 1)

                def add(c, i):
                    dve.wait_ge(down_done, 2 * c + i + 1)
                    rows = m.x[:, bass.ds(c * CB + 2 * i, 2), :]
                    nc.vector.scalar_tensor_tensor(rows, dn[0:LQ, :, :], m.tanh[0:LQ, 1:2], rows,
                                                   ALU.mult, ALU.add).then_inc(added, 1)

                def step(c, s, lead, trail):
                    t = 1 - s
                    if not lead:
                        below_max(c - 1)
                        hidden(c - 1, t, 0)
                        choose(c - 1)
                        hidden(c - 1, t, 1)
                        place(c - 1, t)
                        hidden(c - 1, t, 2)
                        add(c - 2, 1)
                        add(c - 1, 0)
                        return
                    if trail:
                        below_max(c - 1)
                        hidden(c - 1, t, 0)
                    statistics(c, s)
                    if trail:
                        hidden(c - 1, t, 1)
                    normalise(c, s)
                    if trail:
                        hidden(c - 1, t, 2)
                        if after_first(c, 2):
                            add(c - 2, 1)
                        choose(c - 1)
                    base(c, s)
                    if trail:
                        add(c - 1, 0)
                        place(c - 1, t)

                nc.vector.memset(run[0][:, :], 0.0)
                nc.vector.memset(run_b[:, :], 0.0)
                over_chunks(dve, step)
                add(NC - 1, 1)

            @block.gpsimd
            def _(pool):
                def residual(c, s):
                    pool.wait_ge(gelu_done, c + 1)
                    if after_first(c, 2):
                        pool.wait_ge(x1_done, c - 1)
                    nc.gpsimd.tensor_tensor(y[s][:, :, :], ge[s][:, :, :], batches(m.h2, c), ALU.add
                                            ).then_inc(y_done, 1)

                def rstd(c, s):
                    pool.wait_ge(stats_done, c + 1)
                    nc.gpsimd.tensor_tensor(var[s][:, :], mv[s][:, :, 1], m.eps[0:LQ, 0:CB], ALU.add
                                            ).then_inc(rstd_step, 1)
                    pool.wait_ge(rstd_step, 2 * c + 1)
                    nc.gpsimd.tensor_tensor(rs[s][:, :], var[s][:, :], m.minus_half[0:LQ, 0:CB],
                                            ALU.pow).then_inc(rstd_step, 1)

                def scatter(c):
                    pool.wait_ge(routed, c + 1)
                    pool.wait_ge(h_kept, c + 1)
                    for k, src in enumerate((m.h2, m.proj)):
                        for b in range(c * CB, (c + 1) * CB):
                            nc.gpsimd.indirect_dma_start(
                                out=ins["xg"],
                                out_offset=bass.IndirectOffsetOnAxis(ap=m.scatter_at[:, k, b:b + 1], axis=0),
                                in_=src[:, b, :], in_offset=None, bounds_check=E * CAP - 1, oob_is_err=False
                            ).then_inc(scattered, 16)

                residual(0, 0)
                for c in range(NC + 2):
                    if c < NC:
                        rstd(c, c % 2)
                    if c > 1:
                        scatter(c - 2)
                    if c + 1 < NC:
                        residual(c + 1, (c + 1) % 2)
                pool.wait_ge(scattered, 16 * 2 * B)

            @block.tensor
            def _(pe):
                pe.wait_ge(w_loaded, 16 * MLP_LOADS)

                def transposes(c, s):
                    pe.wait_ge(h_done, c + 1)
                    if after_first(c):
                        pe.wait_ge(t_emptied, 2 * c)
                    for k in range(KH):
                        for j in range(CB):
                            last = nc.tensor.transpose(tp[k][:, j * LQ:(j + 1) * LQ],
                                                       h[s][:, j, k * 128:(k + 1) * 128], m.ident[0:LQ, 0:LQ])
                    last.then_inc(t_done, 1)

                def logits(c, s):
                    pe.wait_ge(t_emptied, 2 * c + 2)
                    for j in range(CB):
                        for k in range(KH):
                            last = nc.tensor.matmul(lpart[:, j * E:(j + 1) * E], hT[s][:, k, j * LQ:(j + 1) * LQ],
                                                    m.wr[:, k, :], start=k == 0, stop=k == KH - 1)
                    last.then_inc(logits_done, 1)

                def positions(c):
                    pe.wait_ge(chosen_done, c + 1)
                    nc.tensor.matmul(ppart, m.earlier_b[0:LQ, :], chosen[:, :, :], start=True, stop=False)
                    for j in range(CB - 1):
                        n = CB - 1 - j
                        nc.tensor.matmul(ppart[:, (j + 1) * E:CB * E], m.ones_b[0:LQ, 0:LQ],
                                         chosen[:, j, :].unsqueeze(1).to_broadcast([LQ, n, E]),
                                         start=False, stop=False)
                    nc.tensor.matmul(ppart, m.ones_b[0:LQ, 0:LQ],
                                     run_b[:, :].unsqueeze(1).to_broadcast([LQ, CB, E]),
                                     start=False, stop=True).then_inc(counted, 1)

                def gate_up(c, s, f):
                    n = NF * c + f
                    q = (f + s) % 2
                    if not (isinstance(c, int) and n < 2):
                        pe.wait_ge(hid_done, n - 1)
                    for w, bank in ((wg, gp[q]), (wu, up[q])):
                        for k in range(KH):
                            last = nc.tensor.matmul(bank[0:FN[f], 0:CN], w[:, k, 128 * f:128 * f + FN[f]],
                                                    hT[s][:, k, :], start=k == 0, stop=k == KH - 1)
                    last.then_inc(gu_done, 1)

                def down(c, s, i):
                    if i == 0:
                        pe.wait_ge(hid_done, NF * (c + 1))
                    if i or after_first(c):
                        pe.wait_ge(added, 2 * c + i)
                    for j in range(2):
                        for f in range(NF):
                            rows = slice((2 * i + j) * LQ, (2 * i + j + 1) * LQ)
                            last = nc.tensor.matmul(dn[0:LQ, j, :], hid[s][0:FN[f], f, rows],
                                                    wd[0:FN[f], f, :], start=f == 0, stop=f == NF - 1)
                    last.then_inc(down_done, 1)

                def step(c, s, lead, trail):
                    t = 1 - s
                    if trail:
                        for f in range(NF):
                            gate_up(c - 1, t, f)
                            if not lead and f == 2:
                                positions(c - 1)
                        if after_first(c, 2):
                            down(c - 2, s, 1)
                    if lead:
                        transposes(c, s)
                    if trail:
                        down(c - 1, t, 0)
                        if lead:
                            positions(c - 1)
                    if lead:
                        logits(c, s)

                over_chunks(pe, step)
                down(NC - 1, (NC - 1) % 2, 1)

            @block.scalar
            def _(act):
                def gelu(c, s):
                    if after_first(c, 2):
                        act.wait_ge(y_done, c - 1)
                    nc.scalar.activation(ge[s][:, :, :], batches(m.proj, c), ACT.Gelu).then_inc(gelu_done, 1)

                def silu(c, s, f):
                    n = NF * c + f
                    q = (f + s) % 2
                    act.wait_ge(gu_done, n + 1)
                    if not (isinstance(c, int) and n < 2):
                        act.wait_ge(hid_done, n - 1)
                    nc.scalar.activation(sg[q][0:FN[f], :], gp[q][0:FN[f], 0:CN], ACT.Silu).then_inc(silu_done, 1)

                def take(c, s):
                    act.wait_ge(t_done, c + 1)
                    for k in range(KH):
                        nc.scalar.activation(hT[s][:, k, :], tp[k][:, 0:CN], ACT.Copy).then_inc(t_emptied, 1)

                def keep(c, s):
                    act.wait_ge(h_done, c + 1)
                    for k, dst in enumerate((m.h2, m.proj)):
                        nc.scalar.activation(batches(dst, c), h[s][:, :, :], ACT.Copy)
                        last = nc.scalar.activation(dst[:, bass.ds(c * CB, CB), D], m.token[0:LQ, k, bass.ds(c * CB, CB)],
                                                    ACT.Copy)
                    last.then_inc(h_kept, 1)

                def step(c, s, lead, trail):
                    t = 1 - s
                    if trail:
                        if lead:
                            silu(c - 1, t, 0)
                        act.wait_ge(below_done, c)
                        nc.scalar.activation(ex[:, :, :], below[:, :, :], ACT.Exp).then_inc(exp_done, 1)
                        if not lead:
                            silu(c - 1, t, 0)
                        silu(c - 1, t, 1)
                        silu(c - 1, t, 2)
                    if lead:
                        take(c, s)
                    if not isinstance(c, int) or c + 1 < NC:
                        gelu(c + 1, t)
                    if lead:
                        keep(c, s)

                gelu(0, 0)
                over_chunks(act, step)


MLP_LOADS = 4


def load_mlp(sp, weights, gate, up, down, loaded):
    wg, wu, wd = weights
    sp.dma_start(wg[:, :, :], gate.rearrange("(k p) f -> p k f", p=128)).then_inc(loaded, 16)
    sp.dma_start(wu[:, :, :], up.rearrange("(k p) f -> p k f", p=128)).then_inc(loaded, 16)
    sp.dma_start(wd[:, 0:2, :], down[0:256, :].rearrange("(k p) d -> p k d", p=128)).then_inc(loaded, 16)
    sp.dma_start(wd[0:FN[2], 2, :], down[256:F, :]).then_inc(loaded, 16)


def load_expert(sp, ins, m, e, s):
    load_mlp(sp, m.expert_w[s], ins["w_gate"][bass.ds(e, 1), :, :].rearrange("o d f -> (o d) f"),
             ins["w_up"][bass.ds(e, 1), :, :].rearrange("o d f -> (o d) f"),
             ins["w_down"][bass.ds(e, 1), :, :].rearrange("o f d -> (o f) d"), m.expert_loaded[s])


def experts(nc, ins, m):
    NF = len(FN)
    with ExitStack() as ctx:
        def sb(name, shape, dt=F32):
            return ctx.enter_context(nc.sbuf_tensor(name, shape, dt))

        def pair(name, shape, dt=F32):
            return [sb(f"{name}{s}", shape, dt) for s in range(2)]

        def sem(name):
            return ctx.enter_context(nc.semaphore(name))

        w, loaded = m.expert_w, m.expert_loaded
        rows = pair("rows", [RN, RT, D + 1])
        output_row = pair("output_row", [RN, RT], U32)
        xT = pair("rows_T", [128, KH, CAP])
        sg = pair("expert_silu", [128, CAP])
        hid = pair("expert_hidden", [128, NF, CAP])
        y = pair("y", [RN, RT, D])
        carrier = sb("expert_carrier", [1, 5])
        gp = [ctx.enter_context(nc.psum_tensor(f"expert_gate_psum{s}", [128, 512], F32)) for s in range(2)]
        up = [ctx.enter_context(nc.psum_tensor(f"expert_up_psum{s}", [128, 512], F32)) for s in range(2)]
        dn = [ctx.enter_context(nc.psum_tensor(f"expert_down_psum{s}", [128, 2, D], F32)) for s in range(2)]
        tp = [ctx.enter_context(nc.psum_tensor(f"rowsT_psum{k}", [128, 512], F32)) for k in range(KH)]

        rows_loaded = [sem(f"rows_loaded{s}") for s in range(2)]
        numbered = sem("output_row_done")
        scattered = [sem(f"y_scattered{s}") for s in range(2)]
        t_done, t_emptied = sem("rows_t_done"), sem("rows_t_emptied")
        gu_done, silu_done, hid_done = sem("expert_gate_up_done"), sem("expert_silu_done"), sem("expert_hidden_done")
        down_done, y_done = sem("expert_down_done"), [sem(f"y_done{i}") for i in range(2)]

        def over_experts(eng, step):
            for e in range(4):
                step(e, e % 2, e // 2)
            with eng.Fori(2, E // 2 - 1) as it:
                for s in range(2):
                    step(it * 2 + s, s, it)
            for e in range(E - 2, E):
                step(e, e % 2, e // 2)

        def new(e):
            return isinstance(e, int) and e < 2

        with nc.Block() as block:

            @block.sync
            def _(sp):
                def load(e, s, use):
                    if not new(e):
                        sp.wait_ge(numbered, e - 1)
                        sp.wait_ge(t_done, 2 * e - 2)
                    sp.dma_start(rows[s][:, :, :],
                                 ins["xg"][bass.ds(e * CAP, CAP), :].rearrange("(p t) d -> p t d", t=RT)
                                 ).then_inc(rows_loaded[s], 16)
                    if not new(e):
                        sp.wait_ge(down_done, 2 * e - 2)
                        load_expert(sp, ins, m, e, s)

                over_experts(sp, load)

            @block.gpsimd
            def _(pool):
                def after_wait(i, semaphore, count):
                    pool.wait_ge(semaphore, count)
                    nc.gpsimd.tensor_tensor(carrier[:, i:i + 1], m.eps[0:1, 0:1], m.eps[0:1, 0:1], ALU.add)

                def numbers(e, s, use):
                    after_wait(0, rows_loaded[s], use * 16 + 16)
                    if not new(e):
                        after_wait(1, scattered[s], use * (16 * RT))
                    nc.gpsimd.tensor_copy(output_row[s][:, :], rows[s][:, :, D]).then_inc(numbered, 1)

                def scatter(e, s, use):
                    for t in range(RT):
                        if t == 0:
                            after_wait(4, numbered, e + 1)
                        if t % 2 == 0:
                            after_wait(2 + t // 2, y_done[t // 2], e + 1)
                        nc.gpsimd.indirect_dma_start(
                            out=ins["yt"], out_offset=bass.IndirectOffsetOnAxis(ap=output_row[s][:, t:t + 1], axis=0),
                            in_=y[s][:, t, :], in_offset=None, bounds_check=2 * N - 1, oob_is_err=False
                        ).then_inc(scattered[s], 16)

                def step(e, s, use):
                    if not (isinstance(e, int) and e == 0):
                        scatter(e - 1, 1 - s, use if s else use - 1)
                    numbers(e, s, use)

                over_experts(pool, step)
                scatter(E - 1, 1, E // 2 - 1)
                for s in range(2):
                    pool.wait_ge(scattered[s], 16 * RT * (E // 2))

            @block.tensor
            def _(pe):
                def transposes(e, s, use):
                    pe.wait_ge(rows_loaded[s], use * 16 + 16)
                    for k in range(KH):
                        if not (isinstance(e, int) and e == 0):
                            pe.wait_ge(t_emptied, 2 * e - 1 + k)
                        for t in range(RT):
                            last = nc.tensor.transpose(tp[k][:, t * RN:(t + 1) * RN],
                                                       rows[s][:, t, k * 128:(k + 1) * 128], m.ident[0:RN, 0:RN])
                        last.then_inc(t_done, 1)

                def gate_up(e, s, use, f):
                    if f == 0:
                        pe.wait_ge(loaded[s], use * (16 * MLP_LOADS) + 16 * MLP_LOADS)
                        pe.wait_ge(t_emptied, 2 * e + 2)
                    n = NF * e + f
                    q = (f + s) % 2
                    if not (isinstance(e, int) and n < 2):
                        pe.wait_ge(hid_done, n - 1)
                    for wt, bank in ((w[s][0], gp[q]), (w[s][1], up[q])):
                        for k in range(KH):
                            last = nc.tensor.matmul(bank[0:FN[f], 0:CAP], wt[:, k, 128 * f:128 * f + FN[f]],
                                                    xT[s][:, k, :], start=k == 0, stop=k == KH - 1)
                    last.then_inc(gu_done, 1)

                def down(e, s):
                    pe.wait_ge(hid_done, NF * e + NF)
                    for i in range(2):
                        if not (isinstance(e, int) and e == 0):
                            pe.wait_ge(y_done[i], e)
                        for j in range(2):
                            t = 2 * i + j
                            for f in range(NF):
                                last = nc.tensor.matmul(dn[i][0:RN, j, :], hid[s][0:FN[f], f, t * RN:(t + 1) * RN],
                                                        w[s][2][0:FN[f], f, :], start=f == 0, stop=f == NF - 1)
                        last.then_inc(down_done, 1)

                def step(e, s, use):
                    gate_up(e, s, use, 0)
                    if not (isinstance(e, int) and e == 0):
                        down(e - 1, 1 - s)
                    gate_up(e, s, use, 1)
                    if not (isinstance(e, int) and e == E - 1):
                        transposes(e + 1, 1 - s, use + s)
                    gate_up(e, s, use, 2)

                transposes(0, 0, 0)
                over_experts(pe, step)
                down(E - 1, 1)

            @block.scalar
            def _(act):
                def take(e, s):
                    for k in range(KH):
                        act.wait_ge(t_done, 2 * e + k + 1)
                        if not new(e):
                            act.wait_ge(gu_done, NF * e - NF)
                        nc.scalar.activation(xT[s][:, k, :], tp[k][:, 0:CAP], ACT.Copy).then_inc(t_emptied, 1)

                def silu(e, s, f):
                    n = NF * e + f
                    q = (f + s) % 2
                    act.wait_ge(gu_done, n + 1)
                    if not (isinstance(e, int) and n < 2):
                        act.wait_ge(hid_done, n - 1)
                    nc.scalar.activation(sg[q][0:FN[f], :], gp[q][0:FN[f], 0:CAP], ACT.Silu).then_inc(silu_done, 1)

                def step(e, s, use):
                    silu(e, s, 0)
                    silu(e, s, 1)
                    if not (isinstance(e, int) and e == E - 1):
                        take(e + 1, 1 - s)
                    silu(e, s, 2)

                take(0, 0)
                over_experts(act, step)

            @block.vector
            def _(dve):
                def take_y(e, s, use):
                    for i in range(2):
                        dve.wait_ge(down_done, 2 * e + i + 1)
                        if not (isinstance(e, int) and e < 2):
                            dve.wait_ge(scattered[s], (16 * RT) * use)
                        nc.vector.tensor_copy(y[s][:, 2 * i:2 * i + 2, :], dn[i][0:RN, :, :]).then_inc(y_done[i], 1)

                def hidden(e, s, f):
                    n = NF * e + f
                    q = (f + s) % 2
                    dve.wait_ge(silu_done, n + 1)
                    if not new(e) and f == 0:
                        dve.wait_ge(down_done, 2 * e - 2)
                    nc.vector.tensor_tensor(hid[s][0:FN[f], f, :], sg[q][0:FN[f], :], up[q][0:FN[f], 0:CAP],
                                            ALU.mult).then_inc(hid_done, 1)

                def step(e, s, use):
                    hidden(e, s, 0)
                    if not (isinstance(e, int) and e == 0):
                        take_y(e - 1, 1 - s, use if s else use - 1)
                    hidden(e, s, 1)
                    hidden(e, s, 2)

                over_experts(dve, step)
                take_y(E - 1, 1, E // 2 - 1)


def combine(nc, ins, m, out):
    with ExitStack() as ctx:
        def sem(name):
            return ctx.enter_context(nc.semaphore(name))

        yb = [[ctx.enter_context(nc.sbuf_tensor(f"outputs{k}_{c}", [LQ, CB, D], F32)) for k in range(2)]
              for c in range(NC)]
        loaded = [[sem(f"outputs_loaded{k}_{c}") for k in range(2)] for c in range(NC)]
        first_added, weighted, added, stored = (sem(n) for n in ("first_added", "second_weighted", "both_added",
                                                                 "out_stored"))
        with nc.Block() as block:

            @block.sync
            def _(sp):
                for c in range(NC):
                    for k in range(2):
                        sp.dma_start(yb[c][k][:, :, :],
                                     ins["yt"][k * N + c * CN:k * N + (c + 1) * CN, :].rearrange("(b t) d -> t b d", t=LQ)
                                     ).then_inc(loaded[c][k], 16)
                for c in range(NC):
                    sp.wait_ge(added, c + 1)
                    sp.dma_start(out[c * CB:(c + 1) * CB, :, :].rearrange("b t d -> t b d"),
                                 m.x[:, c * CB:(c + 1) * CB, :]).then_inc(stored, 16)
                sp.wait_ge(stored, 16 * NC)

            @block.vector
            def _(dve):
                for c in range(NC):
                    dve.wait_ge(loaded[c][0], 16)
                    for b in range(c * CB, (c + 1) * CB):
                        last = nc.vector.scalar_tensor_tensor(m.x[:, b, :], yb[c][0][:, b % CB, :],
                                                              m.weight[:, 0, b:b + 1], m.x[:, b, :],
                                                              ALU.mult, ALU.add)
                    last.then_inc(first_added, 1)

            @block.scalar
            def _(act):
                for c in range(NC):
                    act.wait_ge(loaded[c][1], 16)
                    for b in range(c * CB, (c + 1) * CB):
                        last = nc.scalar.activation(yb[c][1][:, b % CB, :], yb[c][1][:, b % CB, :], ACT.Copy,
                                                    scale=m.weight[:, 1, b:b + 1])
                    last.then_inc(weighted, 1)

            @block.gpsimd
            def _(pool):
                for c in range(NC):
                    pool.wait_ge(first_added, c + 1)
                    pool.wait_ge(weighted, c + 1)
                    rows = m.x[:, c * CB:(c + 1) * CB, :]
                    nc.gpsimd.tensor_tensor(rows, rows, yb[c][1][:, :, :], ALU.add).then_inc(added, 1)


def build(nc, ins, out):
    with ExitStack() as ctx:
        def sb(name, shape, dt=F32):
            return ctx.enter_context(nc.sbuf_tensor(name, shape, dt))

        m = Memory()
        m.x = sb("x", [LQ, B, D])
        m.h2 = sb("h2", [LQ, B, D + 1])
        m.proj = sb("o_projection", [LQ, B, D + 1])
        m.wq, m.wk, m.wv, m.wo = (sb(n, [128, KH, D]) for n in ("wq", "wk", "wv", "wo"))
        m.gb_pre = sb("gain_offset_pre", [128, 2, KH])
        m.g_ln, m.b_ln = sb("gain_ln", [LQ, D]), sb("offset_ln", [LQ, D])
        m.wr, m.br = sb("router_w", [128, KH, E]), sb("router_b", [LQ, E])
        m.gates, m.tanh = sb("gates", [128, 2]), sb("tanh_gates", [128, 2])
        m.ident, m.ident_b = sb("ident", [128, 128]), sb("ident_bf", [128, 128], BF16)
        m.headmask, m.headmask_b = sb("headmask", [128, HH]), sb("headmask_bf", [128, HH], BF16)
        m.pairmask_b = sb("pairmask_bf", [128, HH], BF16)
        m.earlier, m.earlier_b = sb("earlier", [LQ, LQ]), sb("earlier_bf", [LQ, LQ], BF16)
        m.token_u, m.token = sb("output_rows", [LQ, 2, B], U32), sb("output_rows_f", [LQ, 2, B])
        m.expert_u, m.expert_f = sb("expert_ids", [128, E], U32), sb("expert_ids_f", [128, E])
        m.ones, m.ones_b = sb("ones", [128, 128]), sb("ones_bf", [128, 128], BF16)
        m.inside = sb("inside_clip", [1, 1], U32)
        m.minus_half, m.eps = sb("minus_half", [128, 8]), sb("eps", [128, 8])
        m.mv = [sb(f"mean_var{s}", [128, KT + 1, 2]) for s in range(2)]
        m.zeros = sb("zeros", [128, RT, D + 1])
        m.scatter_at = sb("scatter_at", [LQ, 2, B], U32)
        m.weight = sb("expert_weight", [LQ, 2, B])
        m.raw_loaded = [ctx.enter_context(nc.semaphore(f"raw_loaded{s}")) for s in range(2)]
        m.raw = [sb(f"ctx_raw{s}", [128, KT, D]) for s in range(2)]

        setup(nc, ins, m)
        attention(nc, ins, m)
        m.expert_w = [mlp_weights(nc, ctx, f"expert{s}") for s in range(2)]
        m.expert_loaded = [ctx.enter_context(nc.semaphore(f"expert_loaded{s}")) for s in range(2)]
        tokens(nc, ins, m)
        experts(nc, ins, m)
        combine(nc, ins, m, out)


def kernel(**inputs):
    import numpy as np
    import concourse.bacc as bacc
    from concourse.bass_utils import run_bass_kernel_spmd

    nc = bacc.Bacc("TRN2", target_bir_lowering=False, num_devices=1)
    given = {
        "x": inputs["x"], "ctx": inputs["ctx_1024"], "g_xattn": inputs["g_xattn"], "g_ffn": inputs["g_ffn"],
        "g_pre": np.asarray(inputs["L0_xattn_g_pre"]).reshape(KH, 128).T,
        "b_pre": np.asarray(inputs["L0_xattn_b_pre"]).reshape(KH, 128).T,
        "g_ln": inputs["L0_xattn_g_ln"], "b_ln": inputs["L0_xattn_b_ln"],
        "wqT": np.asarray(inputs["L0_xattn_Wq"]).T, "wkT": np.asarray(inputs["L0_xattn_Wk"]).T,
        "wvT": np.asarray(inputs["L0_xattn_Wv"]).T, "woT": np.asarray(inputs["L0_xattn_Wo"]).T,
        "router_w": inputs["L0_ffn_router_w"], "router_b": inputs["L0_ffn_router_b"],
        "w_gate": inputs["L0_ffn_w_gate"], "w_up": inputs["L0_ffn_w_up"], "w_down": inputs["L0_ffn_w_down"],
        "sw_gate": inputs["L0_ffn_sw_gate"], "sw_up": inputs["L0_ffn_sw_up"], "sw_down": inputs["L0_ffn_sw_down"],
    }
    arrays, aps = {}, {}
    for name, a in given.items():
        a = np.ascontiguousarray(a)
        arrays[f"in_{name}"] = a
        aps[name] = nc.dram_tensor(f"in_{name}", a.shape, mybir.dt.from_np(a.dtype), kind="ExternalInput").ap()
    aps["xg"] = nc.dram_tensor("expert_rows", (E * CAP, D + 1), F32, kind="Internal").ap()
    aps["yt"] = nc.dram_tensor("expert_outputs", (2 * N, D), F32, kind="Internal").ap()
    out = nc.dram_tensor("out", (B, LQ, D), F32, kind="ExternalOutput").ap()
    build(nc, aps, out)
    return run_bass_kernel_spmd(nc, [arrays], core_ids=[0]).results[0]["out"]
```
